# Optimizing a Trainium2 kernel written in Bass

```python
import numpy as np
import jax
import jax.numpy as jnp

def _softmax(x, axis=-1):
    return jax.nn.softmax(x, axis=axis)

def _gelu(x):
    return jax.nn.gelu(x, approximate=True)

def _silu(x):
    return jax.nn.silu(x)

def _sigmoid(x):
    return jax.nn.sigmoid(x)

def _layernorm(x, axis=-1, eps=1e-05):
    m = jnp.mean(x, axis=axis, keepdims=True)
    v = jnp.var(x, axis=axis, keepdims=True)
    return (x - m) / jnp.sqrt(v + eps)

def _scatter_add(tgt, idx, src, axis=0):
    return tgt.at[idx].add(src)

def _segment_sum(src, seg, n):
    return jax.ops.segment_sum(src, seg, n)
kernel_name = 'mk_gnn_resnorm_d4_gnn_r64_2af222'

def setup_inputs(seed: int=0):
    np.random.seed(seed)
    _w = jnp.asarray

    def _rec_inputs():
        import jax
        import jax.numpy as jnp
        _gk = jax.random.key(seed)
        x = -0.000202 + 1 * jax.random.normal(jax.random.fold_in(_gk, 1), (100000, 128), jnp.float32)
        src = jax.random.randint(jax.random.fold_in(_gk, 2), (25000,), 0, 100000, jnp.int32)
        dst = jax.random.randint(jax.random.fold_in(_gk, 3), (25000,), 0, 100000, jnp.int32)
        _o = jnp.argsort(dst, stable=True)
        src = src[_o]
        dst = dst[_o]
        edge_type_8 = jax.random.randint(jax.random.fold_in(_gk, 13), (25000,), 0, 8, jnp.int32)
        return (x, src, dst, edge_type_8)
    x, src, dst, edge_type_8 = _rec_inputs()

    def _L0_gnn_setup():
        import jax, jax.numpy as jnp
        import numpy as np
        N, E, D = (50000, 625000, 128)
        L, H, C = (3, 4, 32)
        NEG_SLOPE = 0.2

        def _gat_layer(x, src, dst, W_i, a_src_i, a_dst_i, b_i):
            n = x.shape[0]
            h = (x @ W_i).reshape(n, H, C)
            es = jnp.einsum('nhc,hc->nh', h, a_src_i)
            ed = jnp.einsum('nhc,hc->nh', h, a_dst_i)
            e = es[src] + ed[dst]
            e = jnp.where(e > 0, e, NEG_SLOPE * e)
            m = jax.ops.segment_max(e, dst, num_segments=n)
            p = jnp.exp(e - m[dst])
            denom = jax.ops.segment_sum(p, dst, num_segments=n)
            alpha = p / denom[dst]
            msg = alpha[:, :, None] * h[src]
            out = jax.ops.segment_sum(msg, dst, num_segments=n)
            return out.reshape(n, H * C) + b_i
        key = jax.random.key(seed)
        ks = jax.random.split(key, 6)
        x = jax.random.normal(ks[0], (N, D), dtype=jnp.float32)
        edge_index = jax.random.randint(ks[1], (2, E), 0, N, dtype=jnp.int32)
        W = jax.random.normal(ks[2], (L, D, H * C), dtype=jnp.float32) * 0.1
        att_src = jax.random.normal(ks[3], (L, H, C), dtype=jnp.float32) * 0.1
        att_dst = jax.random.normal(ks[4], (L, H, C), dtype=jnp.float32) * 0.1
        bias = jnp.zeros((L, H * C), dtype=jnp.float32)
        return {'x': x, 'edge_index': edge_index, 'W': W, 'att_src': att_src, 'att_dst': att_dst, 'bias': bias}
    _L0_gnn_all = _L0_gnn_setup()
    _L0_gnn_in = {k: v for k, v in _L0_gnn_all.items() if k in ('W', 'att_src', 'att_dst', 'bias')}
    del _L0_gnn_all

    def _L1_gnn_setup():
        import jax, jax.numpy as jnp
        import numpy as np
        N_NODES = 100000
        N_EDGES = 25000
        D_IN = 128
        D_OUT = 128
        key = jax.random.key(seed)
        k1, k2, k3, k4 = jax.random.split(key, 4)
        h = jax.random.normal(k1, (N_NODES, D_IN), dtype=jnp.float32)
        src = jax.random.randint(k2, (N_EDGES,), 0, N_NODES, dtype=jnp.int64 if jax.config.jax_enable_x64 else jnp.int32)
        dst = jax.random.randint(k3, (N_EDGES,), 0, N_NODES, dtype=jnp.int64 if jax.config.jax_enable_x64 else jnp.int32)
        W = jax.random.normal(k4, (D_OUT, 2 * D_IN), dtype=jnp.float32) * (1.0 / np.sqrt(2 * D_IN))
        b = jnp.zeros((D_OUT,), dtype=jnp.float32)
        return {'h': h, 'src': src, 'dst': dst, 'W': W, 'b': b}
    _L1_gnn_all = _L1_gnn_setup()
    _L1_gnn_in = {k: v for k, v in _L1_gnn_all.items() if k in ('W', 'b')}
    del _L1_gnn_all

    def _L2_gnn_setup():
        import jax, jax.numpy as jnp
        import numpy as np
        IN_DIM = 128
        OUT_DIM = 128
        NUM_RELS = 8
        N_NODES = 50000
        N_EDGES = 500000
        key = jax.random.key(seed)
        k_x, k_ei_s, k_ei_d, k_et, k_w, k_sw = jax.random.split(key, 6)
        x = jax.random.normal(k_x, (N_NODES, IN_DIM), dtype=jnp.float32)
        src = jax.random.randint(k_ei_s, (N_EDGES,), 0, N_NODES)
        dst = jax.random.randint(k_ei_d, (N_EDGES,), 0, N_NODES)
        edge_index = jnp.stack([src, dst], axis=0).astype(jnp.int64)
        edge_type = jax.random.randint(k_et, (N_EDGES,), 0, NUM_RELS).astype(jnp.int64)
        bw = float(np.sqrt(6.0 / (IN_DIM + OUT_DIM)))
        weight = jax.random.uniform(k_w, (NUM_RELS, IN_DIM, OUT_DIM), dtype=jnp.float32, minval=-bw, maxval=bw)
        self_loop_weight = jax.random.uniform(k_sw, (IN_DIM, OUT_DIM), dtype=jnp.float32, minval=-bw, maxval=bw)
        bias = jnp.zeros((OUT_DIM,), dtype=jnp.float32)
        return {'x': x, 'weight': weight, 'self_loop_weight': self_loop_weight, 'bias': bias, 'edge_index': edge_index, 'edge_type': edge_type, 'num_entities': N_NODES}
    _L2_gnn_all = _L2_gnn_setup()
    _L2_gnn_in = {k: v for k, v in _L2_gnn_all.items() if k in ('weight', 'self_loop_weight', 'bias')}
    del _L2_gnn_all

    def _L3_gnn_setup():
        import math
        import jax, jax.numpy as jnp
        import numpy as np
        N = 50000
        E = 12500
        HID = 128
        H = 8
        D = HID // H
        key = jax.random.key(seed)
        ks = jax.random.split(key, 12)
        s = 1.0 / math.sqrt(HID)
        inp = {'h': jax.random.normal(ks[0], (N, HID), dtype=jnp.float32), 'src': jax.random.randint(ks[1], (E,), 0, N, dtype=jnp.int32), 'dst': jax.random.randint(ks[2], (E,), 0, N, dtype=jnp.int32), 'Wq': jax.random.normal(ks[3], (HID, HID), dtype=jnp.float32) * s, 'bq': jax.random.normal(ks[4], (HID,), dtype=jnp.float32) * s, 'Wk': jax.random.normal(ks[5], (HID, HID), dtype=jnp.float32) * s, 'bk': jax.random.normal(ks[6], (HID,), dtype=jnp.float32) * s, 'Wv': jax.random.normal(ks[7], (HID, HID), dtype=jnp.float32) * s, 'bv': jax.random.normal(ks[8], (HID,), dtype=jnp.float32) * s, 'Wo': jax.random.normal(ks[9], (HID, HID), dtype=jnp.float32) * s, 'bo': jax.random.normal(ks[10], (HID,), dtype=jnp.float32) * s}
        return inp
    _L3_gnn_all = _L3_gnn_setup()
    _L3_gnn_in = {k: v for k, v in _L3_gnn_all.items() if k in ('Wq', 'bq', 'Wk', 'bk', 'Wv', 'bv', 'Wo', 'bo')}
    del _L3_gnn_all
    return {'x': x, 'src': src, 'dst': dst, 'edge_type_8': edge_type_8, 'L0_gnn_W': _L0_gnn_in['W'], 'L0_gnn_att_src': _L0_gnn_in['att_src'], 'L0_gnn_att_dst': _L0_gnn_in['att_dst'], 'L0_gnn_bias': _L0_gnn_in['bias'], 'L1_gnn_W': _L1_gnn_in['W'], 'L1_gnn_b': _L1_gnn_in['b'], 'L2_gnn_weight': _L2_gnn_in['weight'], 'L2_gnn_self_loop_weight': _L2_gnn_in['self_loop_weight'], 'L2_gnn_bias': _L2_gnn_in['bias'], 'L3_gnn_Wq': _L3_gnn_in['Wq'], 'L3_gnn_bq': _L3_gnn_in['bq'], 'L3_gnn_Wk': _L3_gnn_in['Wk'], 'L3_gnn_bk': _L3_gnn_in['bk'], 'L3_gnn_Wv': _L3_gnn_in['Wv'], 'L3_gnn_bv': _L3_gnn_in['bv'], 'L3_gnn_Wo': _L3_gnn_in['Wo'], 'L3_gnn_bo': _L3_gnn_in['bo']}

def reference(x, src, dst, edge_type_8, L0_gnn_W, L0_gnn_att_src, L0_gnn_att_dst, L0_gnn_bias, L1_gnn_W, L1_gnn_b, L2_gnn_weight, L2_gnn_self_loop_weight, L2_gnn_bias, L3_gnn_Wq, L3_gnn_bq, L3_gnn_Wk, L3_gnn_bk, L3_gnn_Wv, L3_gnn_bv, L3_gnn_Wo, L3_gnn_bo):
    import jax
    import jax.numpy as jnp

    def _L0_gnn_ref(x, edge_index, W, att_src, att_dst, bias):
        import jax, jax.numpy as jnp
        import numpy as np
        N, E, D = (50000, 625000, 128)
        L, H, C = (3, 4, 32)
        NEG_SLOPE = 0.2

        def _gat_layer(x, src, dst, W_i, a_src_i, a_dst_i, b_i):
            n = x.shape[0]
            h = (x @ W_i).reshape(n, H, C)
            es = jnp.einsum('nhc,hc->nh', h, a_src_i)
            ed = jnp.einsum('nhc,hc->nh', h, a_dst_i)
            e = es[src] + ed[dst]
            e = jnp.where(e > 0, e, NEG_SLOPE * e)
            m = jax.ops.segment_max(e, dst, num_segments=n)
            p = jnp.exp(e - m[dst])
            denom = jax.ops.segment_sum(p, dst, num_segments=n)
            alpha = p / denom[dst]
            msg = alpha[:, :, None] * h[src]
            out = jax.ops.segment_sum(msg, dst, num_segments=n)
            return out.reshape(n, H * C) + b_i
        n = x.shape[0]
        loops = jnp.arange(n, dtype=edge_index.dtype)
        src = jnp.concatenate([edge_index[0], loops])
        dst = jnp.concatenate([edge_index[1], loops])
        for i in range(L):
            x = jax.nn.elu(_gat_layer(x, src, dst, W[i], att_src[i], att_dst[i], bias[i]))
        return x

    def _L1_gnn_ref(h, src, dst, W, b):
        import jax, jax.numpy as jnp
        import numpy as np
        N_NODES = 100000
        N_EDGES = 25000
        D_IN = 128
        D_OUT = 128
        n = h.shape[0]
        msg = h[src]
        summed = jax.ops.segment_sum(msg, dst, num_segments=n)
        deg = jax.ops.segment_sum(jnp.ones((src.shape[0],), h.dtype), dst, num_segments=n)
        h_N = summed / jnp.maximum(deg, 1.0)[:, None]
        h_total = jnp.concatenate([h, h_N], axis=1)
        return h_total @ W.T + b

    def _L2_gnn_ref(x, weight, self_loop_weight, bias, edge_index, edge_type, num_entities):
        import jax, jax.numpy as jnp
        import numpy as np
        IN_DIM = 128
        OUT_DIM = 128
        NUM_RELS = 8
        N_NODES = 50000
        N_EDGES = 500000
        hr = jnp.einsum('nd,rdo->rno', x, weight)
        src, dst = (edge_index[0], edge_index[1])
        msg = hr[edge_type, src]
        agg = jax.ops.segment_sum(msg, dst, num_segments=num_entities)
        out = agg + x @ self_loop_weight + bias
        return jax.nn.relu(out)

    def _L3_gnn_ref(h, src, dst, Wq, bq, Wk, bk, Wv, bv, Wo, bo):
        import math
        import jax, jax.numpy as jnp
        import numpy as np
        N = 50000
        E = 12500
        HID = 128
        H = 8
        D = HID // H
        n = h.shape[0]
        q = (h @ Wq.T + bq).reshape(n, H, D)
        k = (h @ Wk.T + bk).reshape(n, H, D)
        v = (h @ Wv.T + bv).reshape(n, H, D)
        eq = q[dst]
        ek = k[src]
        ev = v[src]
        scores = jnp.einsum('ehd,ehd->eh', eq, ek) / jnp.sqrt(jnp.asarray(D, h.dtype))
        scores = jnp.clip(scores, -5.0, 5.0)
        m = jax.ops.segment_max(scores, dst, num_segments=n)
        ex = jnp.exp(scores - m[dst])
        z = jax.ops.segment_sum(ex, dst, num_segments=n)
        attn = ex / z[dst]
        out = jax.ops.segment_sum(attn[..., None] * ev, dst, num_segments=n)
        out = out.reshape(n, H * D)
        return out @ Wo.T + bo
    edge_index = jnp.stack([src, dst])
    x = _layernorm(x + _L0_gnn_ref(x, edge_index, L0_gnn_W, L0_gnn_att_src, L0_gnn_att_dst, L0_gnn_bias), axis=-1)
    x = _layernorm(x + _L1_gnn_ref(x, src, dst, L1_gnn_W, L1_gnn_b), axis=-1)
    x = _layernorm(x + _L2_gnn_ref(x, L2_gnn_weight, L2_gnn_self_loop_weight, L2_gnn_bias, edge_index, edge_type_8, 100000), axis=-1)
    x = _layernorm(x + _L3_gnn_ref(x, src, dst, L3_gnn_Wq, L3_gnn_bq, L3_gnn_Wk, L3_gnn_bk, L3_gnn_Wv, L3_gnn_bv, L3_gnn_Wo, L3_gnn_bo), axis=-1)
    return x

_drawn_inputs = setup_inputs


def setup_inputs(seed=0):
    import zlib

    import numpy as np

    out = dict(_drawn_inputs(seed))
    spreads = {'L0_gnn_bias': (0.0, 0.1), 'L1_gnn_b': (0.0, 0.1), 'L2_gnn_bias': (0.0, 0.1)}
    factors = {'L0_gnn_att_src': 2.898, 'L0_gnn_att_dst': 24.054, 'L3_gnn_bq': 8.0, 'L3_gnn_bk': 64.0}
    for name, (base, spread) in spreads.items():
        noise = np.random.default_rng([zlib.crc32(name.encode()), seed]).standard_normal(out[name].shape)
        drawn = base * np.exp(spread * noise) if base else spread * noise
        out[name] = jnp.asarray(drawn.astype(out[name].dtype))
    for name, factor in factors.items():
        out[name] = (out[name] * factor).astype(out[name].dtype)
    return out
```

```python
from contextlib import ExitStack

import numpy as np

import concourse.bass as bass
from concourse import mybir

F32 = mybir.dt.float32
BF16 = mybir.dt.bfloat16
I32 = mybir.dt.int32
ALU = mybir.AluOpType
ACT = mybir.ActivationFunctionType
AX = mybir.AxisListType

P = 128
D = 128
T = 4
ROWS = P * T
HEADS = 4
HC = D // HEADS
SLOPE = 0.2
RELS = 8
AHEADS = 8
AD = D // AHEADS
LN_EPS = 1e-5
GAT_LAYERS = 3
WIDE = D + AHEADS
FAR = 1e30
DENSE = 4
STRANDS = 2

B_GAT = (0, 1, 2)
B_GAT_SHIFTED = (0, 3, 4)
B_SAGE, B_REL, B_Q, B_K, B_V, B_O = 5, 6, 7, 8, 9, 10
BIASES = 11
BW = D + HEADS


class Signal:

    def __init__(self, sems, counts, unit, per):
        self.sems, self.counts, self.unit, self.per = sems, counts, unit, per

    def __getitem__(self, k):
        return self.sems[k]

    def at(self, k, u, n=0):
        return (u * self.per + (n + 1)) * self.unit + self.counts[k]

    def before(self, k, u):
        return u * (self.per * self.unit) + self.counts[k]


class Signals:

    def __init__(self, nc, ctx):
        self.nc, self.ctx, self.free, self.lent, self.n = nc, ctx, {"step": [], "dma": [], "gather": []}, [], 0
        self.scopes = 0

    def make(self, strands=STRANDS, per=1, kind="step"):
        unit = 1 if kind == "step" else 16
        sems, counts = [], []
        for _ in range(strands):
            if self.free[kind]:
                sem, count = self.free[kind].pop(0)
            else:
                sem, count = self.ctx.enter_context(self.nc.semaphore(f"{kind}_{self.n}")), 0
                self.n += 1
            sems.append(sem)
            counts.append(count)
        signal = Signal(sems, counts, unit, per)
        self.lent.append((kind, signal))
        return signal

    def dma(self, strands=STRANDS, per=1):
        return self.make(strands, per, "dma")

    def gather(self, strands=STRANDS, per=1):
        return self.make(strands, per, "gather")

    @staticmethod
    def idle(*signals):
        for signal in signals:
            signal.per = 0

    def buffers(self, ctx):
        self.scopes += 1
        tag = self.scopes
        return lambda name, shape, dt=F32: ctx.enter_context(self.nc.sbuf_tensor(f"{name}_{tag}", shape, dt))

    def end(self, iterations):
        for kind, s in self.lent:
            for k, sem in enumerate(s.sems):
                self.free[kind].append((sem, s.counts[k] + iterations * s.per * s.unit))
        self.lent = []


def weights_setup(nc, a, w, ps, sig):
    sources = [
        (w.gat[:, :, 0:D], a["L0_gnn_W"].rearrange("l i o -> i l o")),
        (w.raw[:, 0:2, :], a["L1_gnn_W"].rearrange("o (s i) -> o s i", s=2)),
        (w.rel[:, :, :], a["L2_gnn_weight"].rearrange("r i o -> i r o")),
        (w.self_loop[:, :], a["L2_gnn_self_loop_weight"]),
        (w.raw[:, 2, :], a["L3_gnn_Wq"]), (w.raw[:, 3, :], a["L3_gnn_Wk"]),
        (w.raw[:, 4, :], a["L3_gnn_Wv"]), (w.raw[:, 5, :], a["L3_gnn_Wo"]),
        (w.brow[0:1, 0:3, 0:D], a["L0_gnn_bias"].rearrange("(a l) o -> a l o", a=1)),
        (w.brow[0:1, B_GAT_SHIFTED[1]:B_GAT_SHIFTED[2] + 1, 0:D],
         a["L0_gnn_bias"][1:3, :].rearrange("(a l) o -> a l o", a=1)),
        (w.bo_rows[:, :], a["L3_gnn_bo"].partition_broadcast(P)),
    ]
    for row, name in ((B_SAGE, "L1_gnn_b"), (B_REL, "L2_gnn_bias"), (B_Q, "L3_gnn_bq"),
                      (B_K, "L3_gnn_bk"), (B_V, "L3_gnn_bv"), (B_O, "L3_gnn_bo")):
        sources.append((w.brow[0:1, row, 0:D], a[name].rearrange("(a o) -> a o", a=1)))
    for l in range(GAT_LAYERS):
        for s, name in enumerate(("L0_gnn_att_src", "L0_gnn_att_dst")):
            sources.append((w.att[:, l, s:s + 1], a[name][l].rearrange("h (c b) -> (h c) b", b=1)))
    loads = sig.dma(1, per=len(sources))
    zeroed, cleared = sig.make(1), sig.make(1, per=3)
    with nc.Block() as block:
        @block.sync
        def _(sp):
            sp.wait_ge(zeroed[0], zeroed.at(0, 0))
            for dst, src in sources:
                sp.dma_start(dst, src).then_inc(loads[0], 16)
            sp.wait_ge(loads[0], loads.at(0, 0, len(sources) - 1))

        @block.vector
        def _(dve):
            nc.vector.memset(w.brow[:, :, :], 0.0).then_inc(zeroed[0], 1)
            nc.vector.memset(w.bias3[:, :, :], 1.0)
            nc.vector.memset(w.ones_col[:, :], 1.0)
            nc.vector.memset(w.ones4[:, :], 1.0)
            nc.vector.memset(w.minus1[:, :], -1.0)
            nc.vector.memset(w.power[:, :], -0.5)
            nc.vector.memset(w.eps[:, :], LN_EPS)

        @block.gpsimd
        def _(pool):
            nc.gpsimd.memset(w.ident[:, :], 0.0).then_inc(cleared[0], 1)
            nc.gpsimd.memset(w.head_mask[:, :], 1.0).then_inc(cleared[0], 1)
            pool.wait_ge(cleared[0], cleared.at(0, 0, 1))
            nc.gpsimd.affine_select(out=w.ident[:, :], in_=w.ident[:, :], compare_op=ALU.not_equal, fill=1.0,
                                    base=0, pattern=[[-1, P]], channel_multiplier=1)
            nc.gpsimd.affine_select(out=w.head_mask[:, :], in_=w.head_mask[:, :], compare_op=ALU.is_ge, fill=0.0,
                                    base=0, pattern=[[-HC, HEADS]],
                                    channel_multiplier=1).then_inc(cleared[0], 1)
            pool.wait_ge(cleared[0], cleared.at(0, 0, 2))
            nc.gpsimd.affine_select(out=w.head_mask[:, :], in_=w.head_mask[:, :], compare_op=ALU.is_ge, fill=0.0,
                                    base=HC - 1, pattern=[[HC, HEADS]], channel_multiplier=-1)

    sig.end(1)

    transposed, masked, scores, scored, rows, hi, mid, mid32, lo, back = (sig.make(1) for _ in range(10))
    split_out, split_in = sig.dma(1, per=3), sig.dma(1)
    with nc.Block() as block:
        @block.tensor
        def _(pe):
            for l in range(GAT_LAYERS):
                nc.tensor.transpose(ps[:, 0, l * D:(l + 1) * D], w.gat[:, l, 0:D], w.ident[:, :])
            for i in range(6):
                nc.tensor.transpose(ps[:, 1 + i // 4, (i % 4) * D:(i % 4 + 1) * D], w.raw[:, i, :], w.ident[:, :])
            for l in (1, 2):
                last = nc.tensor.matmul(ps[0:1, 3, l * D:(l + 1) * D], w.ones_col[:, :], w.gat[:, l, 0:D],
                                        start=True, stop=True)
            last.then_inc(transposed[0], 1)
            pe.wait_ge(masked[0], masked.at(0, 0))
            for l in range(GAT_LAYERS):
                last = nc.tensor.matmul(ps[:, 4, 8 * l:8 * l + 8], w.gat_t[:, l, :], w.att_heads[:, l, :],
                                        start=True, stop=True)
            last.then_inc(scores[0], 1)

        @block.vector
        def _(dve):
            dve.wait_ge(transposed[0], transposed.at(0, 0))
            nc.vector.tensor_copy(w.gat_t[:, :, :], ps[:, 0, 0:3 * D].rearrange("p (l o) -> p l o", o=D))
            for l in range(GAT_LAYERS):
                for s in range(2):
                    last = nc.vector.tensor_scalar(w.att_heads[:, l, 4 * s:4 * s + 4], w.head_mask[:, :],
                                                   w.att[:, l, s:s + 1], None, ALU.mult)
            last.then_inc(masked[0], 1)
            nc.vector.tensor_tensor(w.sage_own[:, :], ps[:, 1, 0:D], w.ident[:, :], ALU.add)
            nc.vector.tensor_copy(w.sage_mean[:, :], ps[:, 1, D:2 * D])
            nc.vector.tensor_copy(w.q[:, :], ps[:, 1, 2 * D:3 * D])
            nc.vector.tensor_copy(w.kv[:, 0:D], ps[:, 1, 3 * D:4 * D])
            nc.vector.tensor_copy(w.kv[:, D:2 * D], ps[:, 2, 0:D])
            nc.vector.tensor_copy(w.o[:, :], ps[:, 2, D:2 * D])
            for l in (1, 2):
                last = nc.vector.tensor_tensor(w.brow[0:1, B_GAT_SHIFTED[l], 0:D],
                                               w.brow[0:1, B_GAT_SHIFTED[l], 0:D],
                                               ps[0:1, 3, l * D:(l + 1) * D], ALU.subtract)
            last.then_inc(rows[0], 1)
            dve.wait_ge(rows[0], rows.at(0, 0))
            nc.vector.tensor_copy(w.split[0:1, 0], w.brow[:, :, :]).then_inc(hi[0], 1)
            dve.wait_ge(hi[0], hi.at(0, 0))
            nc.vector.tensor_tensor(w.brow[:, :, :], w.brow[:, :, :], w.split[0:1, 0], ALU.subtract).then_inc(mid32[0], 1)
            dve.wait_ge(mid32[0], mid32.at(0, 0))
            nc.vector.tensor_copy(w.split[0:1, 1], w.brow[:, :, :]).then_inc(mid[0], 1)
            dve.wait_ge(mid[0], mid.at(0, 0))
            nc.vector.tensor_tensor(w.brow[:, :, :], w.brow[:, :, :], w.split[0:1, 1], ALU.subtract).then_inc(lo[0], 1)
            dve.wait_ge(lo[0], lo.at(0, 0))
            nc.vector.tensor_copy(w.split[0:1, 2], w.brow[:, :, :]).then_inc(back[0], 1)
            dve.wait_ge(scores[0], scores.at(0, 0))
            for l in range(GAT_LAYERS):
                nc.vector.tensor_copy(w.gat[:, l, D:BW], ps[:, 4, 8 * l:8 * l + 4])
                nc.vector.tensor_copy(w.own_scores[:, l, 0:4], ps[:, 4, 8 * l + 4:8 * l + 8])
                last = nc.vector.tensor_copy(w.own_scores[:, l, 4:8], ps[:, 4, 8 * l:8 * l + 4])
            last.then_inc(scored[0], 1)

        @block.sync
        def _(sp):
            sp.wait_ge(back[0], back.at(0, 0))
            for s in range(3):
                sp.dma_start(w.split_dram[s:s + 1], w.split[0:1, s]).then_inc(split_out[0], 16)
            sp.wait_ge(split_out[0], split_out.at(0, 0, 2))
            sp.dma_start(w.bias3[0:3, :, :], w.split_dram[0:3]).then_inc(split_in[0], 16)
            sp.wait_ge(split_in[0], split_in.at(0, 0))
            sp.wait_ge(scored[0], scored.at(0, 0))
    sig.end(1)


def layer_norm_scale(nc, pool, w, moments, scale, k, u, n, summed, powered, ready):
    pool.wait_ge(summed[k], summed.at(k, u, n))
    nc.gpsimd.tensor_tensor(scale[:, k, :], moments[:, k, :, 1], w.eps[:, :], ALU.add).then_inc(powered[k], 1)
    pool.wait_ge(powered[k], powered.at(k, u, n))
    nc.gpsimd.tensor_tensor(scale[:, k, :], scale[:, k, :], w.power[:, :], ALU.pow).then_inc(ready[k], 1)


def dense_pass(nc, a, w, ps, sig, out):
    x = a["x"]
    n_nodes = x.shape[0]
    groups = -(-n_nodes // ROWS)
    assert groups % DENSE == 0
    rounds = groups // DENSE
    full = n_nodes // ROWS
    x_groups = x[0:full * ROWS, :].rearrange("(g p j) f -> g p (j f)", p=P, j=T)
    out_groups = out[0:full * ROWS, :].rearrange("(g p j) f -> g p (j f)", p=P, j=T)
    last_rows = slice(n_nodes - ROWS, n_nodes)
    x_last = x[last_rows, :].rearrange("(p j) f -> p (j f)", j=T)
    out_last = out[last_rows, :].rearrange("(p j) f -> p (j f)", j=T)
    repeated = (ROWS - (n_nodes - full * ROWS)) // T
    K = range(DENSE)
    ctx = ExitStack()
    with ctx:
        sb = sig.buffers(ctx)
        X, XT, E, R, Y = (sb(f"dense_{n}", [P, DENSE, ROWS]) for n in ("x", "xt", "exp", "r", "y"))
        stats = sb("dense_stats", [P, DENSE, T, 6])
        moments = sb("dense_moments", [P, DENSE, T, 2])
        scale = sb("dense_scale", [P, DENSE, T])
        spare = sb("dense_spare", [P, 1])

        def A(k):
            return ps[:, 2 * k, :]

        def B(k):
            return ps[:, 2 * k + 1, :]

        def tile(j):
            return slice(j * D, (j + 1) * D)

        loaded, stored = sig.dma(DENSE), sig.dma(DENSE)
        products = sig.make(DENSE, per=8)
        copied = sig.make(DENSE, per=3)
        exped = sig.make(DENSE, per=3)
        elued = sig.make(DENSE, per=2)
        relued = sig.make(DENSE)
        summed = sig.make(DENSE, per=2)
        tallied = sig.make(DENSE, per=4)
        aggregated = sig.make(DENSE, per=4)
        powered, scaled = sig.make(DENSE, per=4), sig.make(DENSE, per=4)
        normed = sig.make(DENSE, per=4)

        def load(sp, k, u):
            g = u * DENSE + k
            src = x_last if isinstance(g, int) and g == full else x_groups[g]
            sp.dma_start(X[:, k, :], src).then_inc(loaded[k], 16)

        def store(sp, k, u):
            sp.wait_ge(normed[k], normed.at(k, u, 3))
            g = u * DENSE + k
            if isinstance(g, int) and g == full:
                sp.dma_start(out_last[repeated:P, :], Y[repeated:P, k, :]).then_inc(stored[k], 16)
            else:
                sp.dma_start(out_groups[g], Y[:, k, :]).then_inc(stored[k], 16)

        with nc.Block() as block:
            @block.sync
            def _(sp):
                for k in K:
                    load(sp, k, 0)
                with sp.Fori(0, rounds - 2) as u:
                    for k in K:
                        sp.wait_ge(summed[k], summed.at(k, u))
                        load(sp, k, u + 1)
                    for k in K:
                        store(sp, k, u)
                u = rounds - 2
                for k in K:
                    sp.wait_ge(summed[k], summed.at(k, u))
                    load(sp, k, u + 1)
                for k in K:
                    store(sp, k, u)
                for k in K:
                    store(sp, k, u + 1)
                for k in K:
                    sp.wait_ge(stored[k], stored.at(k, u + 1))

            @block.tensor
            def _(pe):
                def transpose_rows(k, u, n, dst, src):
                    for j in range(T):
                        last = nc.tensor.transpose(dst[:, tile(j)], src[:, k, tile(j)], w.ident[:, :])
                    last.then_inc(products[k], 1)

                def bias_then(k, dst, row):
                    nc.tensor.matmul(dst, w.ones4[0:3, 0:P], w.bias3[0:3, row, 0:D].unsqueeze(1).broadcast_to([3, T, D]),
                                     start=True, stop=False)

                def rows_out(k, dst, weight):
                    for j in range(T):
                        last = nc.tensor.matmul(dst[:, tile(j)], XT[:, k, tile(j)], weight, start=False, stop=j == T - 1)
                    last.then_inc(products[k], 1)

                for u in iterations(pe, rounds):
                    for k in K:
                        pe.wait_ge(loaded[k], loaded.at(k, u))
                        transpose_rows(k, u, 0, A(k), X)
                    for k in K:
                        pe.wait_ge(copied[k], copied.at(k, u, 0))
                        if not first(u):
                            pe.wait_ge(aggregated[k], aggregated.before(k, u))
                        nc.tensor.matmul(B(k), w.bias3[0:4, B_GAT_SHIFTED[0], 0:D], w.ones4[:, :], start=True, stop=False)
                        nc.tensor.matmul(B(k), w.gat[:, 0, 0:D], XT[:, k, :], start=False, stop=True).then_inc(products[k], 1)
                    for k in K:
                        pe.wait_ge(elued[k], elued.at(k, u, 0))
                        nc.tensor.matmul(A(k), w.bias3[0:4, B_GAT_SHIFTED[1], 0:D], w.ones4[:, :], start=True, stop=False)
                        nc.tensor.matmul(A(k), w.gat[:, 1, 0:D], XT[:, k, :], start=False, stop=True).then_inc(products[k], 1)
                    for k in K:
                        pe.wait_ge(elued[k], elued.at(k, u, 1))
                        bias_then(k, B(k), B_GAT_SHIFTED[2])
                        rows_out(k, B(k), w.gat[:, 2, 0:D])
                    for k in K:
                        pe.wait_ge(normed[k], normed.at(k, u, 0))
                        transpose_rows(k, u, 4, A(k), Y)
                    for k in K:
                        pe.wait_ge(copied[k], copied.at(k, u, 1))
                        bias_then(k, B(k), B_SAGE)
                        rows_out(k, B(k), w.sage_own[:, :])
                    for k in K:
                        pe.wait_ge(normed[k], normed.at(k, u, 1))
                        transpose_rows(k, u, 6, A(k), R)
                    for k in K:
                        pe.wait_ge(copied[k], copied.at(k, u, 2))
                        bias_then(k, B(k), B_REL)
                        rows_out(k, B(k), w.self_loop[:, :])

            @block.scalar
            def _(act):
                def copy_out(k, u, n, product):
                    act.wait_ge(products[k], products.at(k, u, product))
                    nc.scalar.activation(XT[:, k, :], A(k), ACT.Copy).then_inc(copied[k], 1)

                with act.Fori(0, rounds) as u:
                    for k in K:
                        copy_out(k, u, 0, 0)
                    for k in K:
                        act.wait_ge(products[k], products.at(k, u, 1))
                        nc.scalar.activation(E[:, k, :], B(k), ACT.Exp, bias=w.minus1[:, :]).then_inc(exped[k], 1)
                    for k in K:
                        act.wait_ge(products[k], products.at(k, u, 2))
                        nc.scalar.activation(E[:, k, :], A(k), ACT.Exp, bias=w.minus1[:, :]).then_inc(exped[k], 1)
                    for k in K:
                        act.wait_ge(products[k], products.at(k, u, 3))
                        nc.scalar.activation(E[:, k, :], B(k), ACT.Exp).then_inc(exped[k], 1)
                    for k in K:
                        copy_out(k, u, 1, 4)
                    for k in K:
                        copy_out(k, u, 2, 6)

            @block.gpsimd
            def _(pool):
                with pool.Fori(0, rounds) as u:
                    for n in range(4):
                        for k in K:
                            layer_norm_scale(nc, pool, w, moments, scale, k, u, n, aggregated, powered, scaled)

            @block.vector
            def _(dve):
                def row_stats(k, src):
                    for j in range(T):
                        last = nc.vector.bn_stats(stats[:, k, j, :], src[:, tile(j)])
                    last.then_inc(tallied[k], 1)

                def moments_of(u, n):
                    dve.wait_ge(tallied[DENSE - 1], tallied.at(DENSE - 1, u, n))
                    nc.vector.memset(spare[:, :], 0.0)
                    for k in K:
                        for j in range(T):
                            last = nc.vector.bn_aggr(moments[:, k, j, :], stats[:, k, j, :])
                        last.then_inc(aggregated[k], 1)

                def normalise(k, u, n, dst, src):
                    dve.wait_ge(scaled[k], scaled.at(k, u, n))
                    for j in range(T):
                        last = nc.vector.tensor_scalar(dst[:, tile(j)], src[:, tile(j)], moments[:, k, j, 0:1],
                                                       scale[:, k, j:j + 1], ALU.subtract, ALU.mult)
                    last.then_inc(normed[k], 1)

                for u in iterations(dve, rounds):
                    for l, src in enumerate((B, A)):
                        for k in K:
                            dve.wait_ge(exped[k], exped.at(k, u, l))
                            nc.vector.scalar_tensor_tensor(XT[:, k, :], E[:, k, :], 1.0, src(k), ALU.min,
                                                           ALU.max).then_inc(elued[k], 1)
                    for k in K:
                        dve.wait_ge(exped[k], exped.at(k, u, 2))
                        nc.vector.scalar_tensor_tensor(R[:, k, :], B(k), 0.0, X[:, k, :], ALU.max,
                                                       ALU.add).then_inc(relued[k], 1)
                    for k in K:
                        dve.wait_ge(relued[k], relued.at(k, u))
                        nc.vector.scalar_tensor_tensor(R[:, k, :], E[:, k, :], 1.0, R[:, k, :], ALU.min,
                                                       ALU.add).then_inc(summed[k], 1)
                    for k in K:
                        dve.wait_ge(summed[k], summed.at(k, u, 0))
                        row_stats(k, R[:, k, :])
                    moments_of(u, 0)
                    for k in K:
                        if not first(u):
                            dve.wait_ge(stored[k], stored.before(k, u))
                        normalise(k, u, 0, Y[:, k, :], R[:, k, :])
                    for k in K:
                        dve.wait_ge(products[k], products.at(k, u, 5))
                        row_stats(k, B(k))
                    moments_of(u, 1)
                    for k in K:
                        normalise(k, u, 1, R[:, k, :], B(k))
                    for k in K:
                        dve.wait_ge(products[k], products.at(k, u, 7))
                        dve.wait_ge(normed[k], normed.at(k, u, 1))
                        nc.vector.scalar_tensor_tensor(Y[:, k, :], B(k), 0.0, R[:, k, :], ALU.max,
                                                       ALU.add).then_inc(summed[k], 1)
                    for k in K:
                        dve.wait_ge(summed[k], summed.at(k, u, 1))
                        row_stats(k, Y[:, k, :])
                    moments_of(u, 2)
                    for k in K:
                        dve.wait_ge(scaled[k], scaled.at(k, u, 2))
                        for j in range(T):
                            last = nc.vector.scalar_tensor_tensor(R[:, k, tile(j)], Y[:, k, tile(j)],
                                                                  scale[:, k, j:j + 1], w.bo_rows[:, :], ALU.mult,
                                                                  ALU.add)
                        last.then_inc(normed[k], 1)
                    for k in K:
                        dve.wait_ge(normed[k], normed.at(k, u, 2))
                        row_stats(k, R[:, k, :])
                    moments_of(u, 3)
                    for k in K:
                        normalise(k, u, 3, Y[:, k, :], R[:, k, :])
        sig.end(rounds)


class Edges:

    def __init__(self, n_nodes, n_edges):
        self.n_nodes, self.n_edges = n_nodes, n_edges
        self.chunks = -(-n_edges // (ROWS * STRANDS)) * STRANDS
        self.rounds = self.chunks // STRANDS
        self.tiles = self.chunks * T
        self.rows = self.tiles * P
        self.blocks = -(-self.tiles // P)
        self.padded = self.blocks * P
        self.score_blocks = -(-self.tiles * HEADS // P)
        self.score_tiles = self.score_blocks * P // HEADS
        self.block_rows = [min(P, self.tiles - b * P) for b in range(self.blocks)]


def dram_ap(ap, offset, pattern):
    return bass.AP(tensor=ap.tensor, offset=offset, ap=pattern)


def iterations(eng, n, tail=0):
    yield 0
    if n - tail > 1:
        with eng.Fori(1, n - tail) as u:
            yield u
    for u in range(max(n - tail, 1), n):
        yield u


def first(u):
    return isinstance(u, int) and u == 0


def edge_setup(nc, a, w, e, ps, sig, sb):
    NB, NTP, NT, NS, NTS = e.blocks, e.padded, e.tiles, e.score_blocks, e.score_tiles
    BIG = float(1 << 21)
    idx = sb("edge_fields", [P, NB, 4, P], I32)
    idx_f = sb("edge_fields_f", [P, NB, 4, P])
    col = sb("edge_columns", [P, 4, NTP])
    masks = sb("end_masks", [P, NB, 2, P])
    tmp = sb("setup_tmp", [P, 2, NTP])
    ends = sb("tile_ends", [P, 2, NTP])
    own_first, own_last = sb("own_first", [P, NS]), sb("own_last", [P, NS])
    dst_scores = sb("dst_by_score", [P, NS, P])
    fill = sb("pos_fill", [P, -(-e.n_nodes // P)], I32)
    slot = sb("slot", [P, NTP])
    slot_i = sb("slot_i", [P, NTP], I32)
    ints = sb("index_ints", [P, 3, NTP], I32)
    pos = sb("positions", [P, NTP], I32)
    pos_f = sb("positions_f", [P, 2, NTP])

    srcs = []
    for f, (name, skip) in enumerate((("src", 0), ("dst", 0), ("dst", 1), ("edge_type_8", 0))):
        n = e.n_edges - skip
        for b in range(NB):
            lo, hi = b * P, min((b + 1) * P, n // P)
            if hi > lo:
                srcs.append((idx[0:hi - lo, b, f, :],
                             a[name][skip + lo * P:skip + hi * P].rearrange("(t e) -> t e", e=P)))
        t, rest = n // P, n % P
        if rest:
            srcs.append((idx[t % P:t % P + 1, t // P, f, 0:rest],
                         a[name][skip + t * P:skip + n].rearrange("(a e) -> a e", a=1)))
    loaded, filled, padded, converted = sig.dma(1, per=len(srcs)), sig.dma(1, per=2 if e.n_nodes % P else 1), sig.make(1, per=2), sig.make(1)
    turned = sig.make(1)
    whole = e.n_nodes // P
    with nc.Block() as block:
        @block.gpsimd
        def _(pool):
            nc.gpsimd.memset(fill[:, :], -1).then_inc(padded[0], 1)
            nc.gpsimd.memset(idx[:, :, 0, :], 0)
            nc.gpsimd.memset(idx[:, :, 1:3, :], e.n_nodes)
            nc.gpsimd.memset(idx[:, :, 3, :], 0).then_inc(padded[0], 1)
            nc.gpsimd.iota(slot_i[:, :], pattern=[[P, NTP]], base=0, channel_multiplier=1)

        @block.sync
        def _(sp):
            sp.wait_ge(padded[0], padded.at(0, 0, 1))
            for dst, src in srcs:
                sp.dma_start(dst, src).then_inc(loaded[0], 16)
            sp.dma_start(w.pos_dram[0:whole * P, :].rearrange("(p n) b -> p (n b)", p=P),
                         fill[:, 0:whole]).then_inc(filled[0], 16)
            rest = e.n_nodes - whole * P
            if rest:
                sp.dma_start(w.pos_dram[whole * P:e.n_nodes, :], fill[0:rest, 0:1]).then_inc(filled[0], 16)
            sp.wait_ge(filled[0], filled.at(0, 0, 1 if rest else 0))

        @block.vector
        def _(dve):
            dve.wait_ge(loaded[0], loaded.at(0, 0, len(srcs) - 1))
            nc.vector.tensor_copy(idx_f[:, :, :, :], idx[:, :, :, :]).then_inc(converted[0], 1)
            dve.wait_ge(turned[0], turned.at(0, 0))
            for f in range(4):
                nc.vector.tensor_copy(col[:, f, :], ps[:, f, 0:NTP])

        @block.tensor
        def _(pe):
            pe.wait_ge(converted[0], converted.at(0, 0))
            for f in range(4):
                for b in range(NB):
                    last = nc.tensor.transpose(ps[:, f, b * P:(b + 1) * P], idx_f[:, b, f, :], w.ident[:, :])
            last.then_inc(turned[0], 1)
    sig.end(1)

    ready, masked, lists = sig.make(1, per=2), sig.make(1), sig.make(1)
    written = sig.dma(1, per=5 * NB + 1)
    read = sig.dma(1, per=1 + 3 * NS)
    listed = sig.dma(1, per=2)
    with nc.Block() as block:
        @block.vector
        def _(dve):
            nc.vector.tensor_tensor(tmp[:, 0, :], col[:, 1, :], col[:, 2, :], ALU.is_equal).then_inc(ready[0], 1)
            dve.wait_ge(ready[0], ready.at(0, 0, 0))
            nc.vector.scalar_tensor_tensor(tmp[:, 1, :], tmp[:, 0, :], BIG, col[:, 1, :], ALU.mult,
                                           ALU.add).then_inc(ready[0], 1)
            nc.vector.tensor_copy(w.dst_col[:, :], col[:, 1, :])
            for r in range(RELS):
                nc.vector.tensor_scalar(w.is_rel[:, r, :], col[:, 3, :], float(r), None, ALU.is_equal)
            nc.vector.tensor_copy(ints[:, 0, :], col[:, 0, :])
            nc.vector.tensor_scalar(ints[:, 1, :], col[:, 1, :], float(e.n_nodes - 1), None, ALU.min)
            dve.wait_ge(ready[0], ready.at(0, 0, 1))
            nc.vector.tensor_copy(ints[:, 2, :], tmp[:, 1, :]).then_inc(lists[0], 1)
            nc.vector.tensor_copy(slot[:, :], slot_i[:, :])
            for b in range(NB):
                for s, at in ((0, 0), (1, P - 1)):
                    last = nc.vector.tensor_scalar(masks[:, b, s, :], idx_f[:, b, 1, :], idx_f[:, b, 1, at:at + 1],
                                                   None, ALU.is_equal)
            last.then_inc(masked[0], 1)

        @block.sync
        def _(sp):
            for b in range(NB):
                sp.dma_start(w.dst_dram[b * P * P:(b + 1) * P * P].rearrange("(t e) -> t e", e=P),
                             idx_f[:, b, 1, :]).then_inc(written[0], 16)
                for s, at in ((0, 0), (1, P - 1)):
                    sp.dma_start(w.ends_dram[s, b * P:(b + 1) * P].rearrange("(t a) -> t a", a=1),
                                 idx_f[:, b, 1, at:at + 1]).then_inc(written[0], 16)
            sp.wait_ge(masked[0], masked.at(0, 0))
            for b in range(NB):
                rows = e.block_rows[b]
                for s in range(2):
                    sp.dma_start(w.masks_dram[s, b * P * P:b * P * P + rows * P].rearrange("(t e) -> t e", e=P),
                                 masks[0:rows, b, s, :]).then_inc(written[0], 16)
            sp.wait_ge(lists[0], lists.at(0, 0))
            sp.dma_start(w.lists_dram[0].rearrange("c p j -> p c j"),
                         ints[:, 0, 0:NT].rearrange("p (c j) -> p c j", j=T)).then_inc(written[0], 16)
            sp.wait_ge(written[0], written.at(0, 0, 5 * NB))
            for f in (1, 2):
                sp.dma_start(w.lists_dram[f].rearrange("c p j -> p c j"),
                             ints[:, f, 0:NT].rearrange("p (c j) -> p c j", j=T)).then_inc(listed[0], 16)
            sp.dma_start(ends[:, :, :], dram_ap(w.ends_dram, 0, [[0, P], [NTP, 2], [1, NTP]])).then_inc(read[0], 16)
            for s, own in enumerate((own_first, own_last)):
                for i in range(NS):
                    sp.dma_start(own[:, i:i + 1], dram_ap(w.ends_dram, s * NTP + i * (P // HEADS),
                                                          [[1, P // HEADS], [0, HEADS], [1, 1]])).then_inc(read[0], 16)
            for s in range(NS):
                sp.dma_start(dst_scores[:, s, :], dram_ap(w.dst_dram, s * P // HEADS * P,
                                                          [[P, P // HEADS], [0, HEADS], [1, P]])).then_inc(read[0], 16)
            sp.wait_ge(read[0], read.at(0, 0, 3 * NS))
            sp.wait_ge(listed[0], listed.at(0, 0, 1))
    sig.end(1)

    compared, cut = sig.make(1), sig.make(1)
    with nc.Block() as block:
        @block.vector
        def _(dve):
            for b in range(NB):
                nc.vector.tensor_scalar(w.carry_eq[:, 0, b, :], ends[:, 0, :], idx_f[:, b, 1, P - 1:P], None,
                                        ALU.is_equal)
                nc.vector.tensor_scalar(w.carry_eq[:, 1, b, :], ends[:, 1, :], idx_f[:, b, 1, 0:1], None, ALU.is_equal)
            for s in range(NS):
                nc.vector.tensor_scalar(w.carry_pen[:, 0, s, :], ends[:, 1, 0:NTS], own_first[:, s:s + 1], None,
                                        ALU.is_equal)
                last = nc.vector.tensor_scalar(w.carry_pen[:, 1, s, :], ends[:, 0, 0:NTS], own_last[:, s:s + 1], None,
                                               ALU.is_equal)
            nc.vector.tensor_tensor(w.step_pen[:, :, 1:P], dst_scores[:, :, 0:P - 1], dst_scores[:, :, 1:P],
                                    ALU.is_equal)
            for s in range(NS):
                nc.vector.tensor_scalar(w.end_pen[:, 0, s, :], dst_scores[:, s, :], dst_scores[:, s, 0:1], None,
                                        ALU.is_equal)
                last = nc.vector.tensor_scalar(w.end_pen[:, 1, s, :], dst_scores[:, s, :], dst_scores[:, s, P - 1:P],
                                               None, ALU.is_equal)
            last.then_inc(compared[0], 1)
            dve.wait_ge(compared[0], compared.at(0, 0))
            for pen in (w.step_pen[:, :, 1:P], w.end_pen[:, :, :, :].rearrange("p a s e -> p (a s e)")):
                nc.vector.tensor_scalar(pen, pen, 1.0, FAR, ALU.subtract, ALU.mult)
            nc.vector.memset(w.step_pen[:, :, 0:1], -FAR)
            nc.vector.memset(w.step_pen[:, :, P:P + 1], -FAR)
            dve.wait_ge(cut[0], cut.at(0, 0))
            pen = w.carry_pen[:, :, :, :].rearrange("p a s t -> p (a s t)")
            nc.vector.tensor_scalar(pen, pen, 1.0, FAR, ALU.subtract, ALU.mult)

        @block.gpsimd
        def _(pool):
            pool.wait_ge(compared[0], compared.at(0, 0))
            for b in range(NB):
                for s, sign in ((0, 1), (1, -1)):
                    m = w.carry_eq[:, s, b, :]
                    nc.gpsimd.affine_select(out=m, in_=m, compare_op=ALU.is_gt, fill=0.0, base=-sign * b * P,
                                            pattern=[[sign, NTP]], channel_multiplier=-sign)
            for s in range(NS):
                m = w.carry_pen[:, 0, s, :]
                nc.gpsimd.affine_select(out=m, in_=m, compare_op=ALU.is_ge, fill=0.0, base=P * s - HEADS,
                                        pattern=[[-HEADS, NTS]], channel_multiplier=1)
                m = w.carry_pen[:, 1, s, :]
                last = nc.gpsimd.affine_select(out=m, in_=m, compare_op=ALU.is_gt, fill=0.0, base=-P * s,
                                               pattern=[[HEADS, NTS]], channel_multiplier=-1)
            last.then_inc(cut[0], 1)
    sig.end(1)

    scattered, found = sig.gather(1, per=NT), sig.gather(1, per=NT)
    with nc.Block() as block:
        @block.gpsimd
        def _(pool):
            for t in range(NT):
                nc.gpsimd.indirect_dma_start(
                    w.pos_dram[:, :], bass.IndirectOffsetOnAxis(ap=ints[:, 2, t:t + 1], axis=0),
                    slot_i[:, t:t + 1], None, bounds_check=e.n_nodes - 1, oob_is_err=False).then_inc(scattered[0], 16)
            pool.wait_ge(scattered[0], scattered.at(0, 0, NT - 1))
            for t in range(NT):
                nc.gpsimd.indirect_dma_start(
                    pos[:, t:t + 1], None, w.pos_dram[:, :],
                    bass.IndirectOffsetOnAxis(ap=ints[:, 0, t:t + 1], axis=0)).then_inc(found[0], 16)
            pool.wait_ge(found[0], found.at(0, 0, NT - 1))
    sig.end(1)

    step = sig.make(1, per=4)
    stored = sig.dma(1)
    with nc.Block() as block:
        @block.vector
        def _(dve):
            p, q, n = pos_f[:, 0, 0:NT], pos_f[:, 1, 0:NT], slot[:, 0:NT]
            nc.vector.tensor_copy(p, pos[:, 0:NT]).then_inc(step[0], 1)
            dve.wait_ge(step[0], step.at(0, 0, 0))
            nc.vector.tensor_scalar(q, p, 0.0, None, ALU.is_ge)
            nc.vector.scalar_tensor_tensor(p, p, float(e.rows), n, ALU.add, ALU.subtract).then_inc(step[0], 1)
            dve.wait_ge(step[0], step.at(0, 0, 1))
            nc.vector.tensor_tensor(p, p, q, ALU.mult).then_inc(step[0], 1)
            dve.wait_ge(step[0], step.at(0, 0, 2))
            nc.vector.tensor_tensor(ints[:, 0, 0:NT], p, n, ALU.add).then_inc(step[0], 1)

        @block.sync
        def _(sp):
            sp.wait_ge(step[0], step.at(0, 0, 3))
            sp.dma_start(w.lists_dram[3].rearrange("c p j -> p c j"),
                         ints[:, 0, 0:NT].rearrange("p (c j) -> p c j", j=T)).then_inc(stored[0], 16)
            sp.wait_ge(stored[0], stored.at(0, 0))
    sig.end(1)


def ln_stats(nc, k, stats, src, tallied):
    for j in range(T):
        last = nc.vector.bn_stats(stats[:, k, j, :], src[:, j, :])
    last.then_inc(tallied[k], 1)


def ln_moments(nc, dve, k, u, b, tallied, aggregated):
    dve.wait_ge(tallied[k], tallied.at(k, u))
    nc.vector.memset(b.spare[:, k:k + 1], 0.0)
    for j in range(T):
        last = nc.vector.bn_aggr(b.moments[:, k, j, :], b.stats[:, k, j, :])
    last.then_inc(aggregated[k], 1)


def ln_apply(nc, dve, k, u, b, dst, src, scaled, normed):
    dve.wait_ge(scaled[k], scaled.at(k, u))
    for j in range(T):
        last = nc.vector.tensor_scalar(dst[:, j, :], src[:, j, :], b.moments[:, k, j, 0:1],
                                       b.scale[:, k, j:j + 1], ALU.subtract, ALU.mult)
    last.then_inc(normed[k], 1)


class Strands:

    def __init__(self, nc, sig, ctx, ps):
        sb = sig.buffers(ctx)
        K = STRANDS
        self.index = sb("chunk_index", [P, K, 2, T], I32)
        self.src = sb("chunk_src", [P, K, T, WIDE])
        self.own = sb("chunk_own", [P, K, T, D])
        self.src_t = sb("chunk_src_t", [P, K, ROWS])
        self.own_t = sb("chunk_own_t", [P, K, ROWS])
        self.e = sb("chunk_e", [P, K, T, D])
        self.new = sb("chunk_new", [P, K, T, D])
        self.v = sb("chunk_v", [P, K, T, WIDE])
        self.same = sb("chunk_same", [P, K, ROWS])
        self.mask = sb("chunk_mask", [2, K, ROWS])
        self.carry = sb("chunk_carry", [2, K, T, WIDE])
        self.stats = sb("chunk_stats", [P, K, T, 6])
        self.moments = sb("chunk_moments", [P, K, T, 2])
        self.scale = sb("chunk_scale", [P, K, T])
        self.small = sb("chunk_small", [P, K, 4, T, 2 * HEADS])
        self.spare = sb("chunk_spare", [P, K])
        self.ps = ps

    def a(self, k):
        return self.ps[:, 4 * k, :]

    def b(self, k):
        return self.ps[:, 4 * k + 1, :]

    def wide(self, k, width):
        return self.ps[:, 4 * k + 2:4 * k + 4, :].rearrange("p b (j f) -> p (b j) f", j=2)[:, :, 0:width]

    def tiles(self, bank):
        return bank.rearrange("p (j f) -> p j f", j=T)


def settle(eng, w):
    eng.sem_inc(w.settled, 1)


def turn(nc, w, dst, src, done):
    for j in range(T):
        last = nc.tensor.transpose(dst[:, j * P:(j + 1) * P], src[:, j, 0:D], w.ident[:, :])
    last.then_inc(done, 1)


def bias_rows(nc, w, dst, row, width=D, tiles=T, stop=False):
    nc.tensor.matmul(dst, w.ones4[0:3, 0:P], w.bias3[0:3, row, 0:width].unsqueeze(1).broadcast_to([3, tiles, width]),
                     start=True, stop=stop)


def gather(nc, rows, table, index, done):
    for j in range(T):
        nc.gpsimd.indirect_dma_start(rows[:, j, 0:D], None, table,
                                     bass.IndirectOffsetOnAxis(ap=index[:, j:j + 1], axis=0)).then_inc(done, 16)


def gat_scores(nc, a, w, e, b, ps, sig, l, old, new):
    K = range(STRANDS)
    n = e.rounds
    gathered = sig.gather(per=T)
    own_in, index_in = sig.gather(per=T) if l == 0 else sig.dma(), sig.dma(per=2 if l == 0 else 1)
    rest_in, stored, kept = sig.dma(), sig.dma(), sig.dma(per=2)
    turned, own_turned, copied, own_copied, projected, scored, exped, lowered, elued = (
        sig.make() for _ in range(9))
    own_kept, h_kept = sig.make(), sig.make()
    summed, tallied, aggregated, powered, scaled, normed = (sig.make() for _ in range(6))
    last_step = normed if l == 2 else elued
    if l != 2:
        sig.idle(rest_in, summed, tallied, aggregated, powered, scaled, normed)
    if l != 0:
        sig.idle(kept)
    old_rows = old.rearrange("(c j p) f -> c p j f", j=T, p=P)
    new_rows = new.rearrange("(c j p) f -> c p j f", j=T, p=P)
    first_rows = w.tables[0].rearrange("(c j p) f -> c p j f", j=T, p=P)

    def load(sp, k, u, prev):
        c = u * STRANDS + k
        if prev is not None:
            sp.wait_ge(gathered[k], gathered.at(k, prev, T - 1))
            settle(sp, w)
            if l == 0:
                sp.wait_ge(own_in[k], own_in.at(k, prev, T - 1))
                settle(sp, w)
            else:
                sp.wait_ge(own_turned[k], own_turned.at(k, prev))
                settle(sp, w)
        if l == 0:
            sp.dma_start(b.index[:, k, 0, :], w.lists_dram[0, c]).then_inc(index_in[k], 16)
            sp.dma_start(b.index[:, k, 1, :], w.lists_dram[1, c]).then_inc(index_in[k], 16)
        else:
            sp.dma_start(b.index[:, k, 0, :], w.lists_dram[3, c]).then_inc(index_in[k], 16)
            sp.dma_start(b.own[:, k], old_rows[e.chunks + c]).then_inc(own_in[k], 16)
        if l == 2:
            if prev is not None:
                sp.wait_ge(summed[k], summed.at(k, prev))
                settle(sp, w)
            sp.dma_start(b.v[:, k, :, 0:D], first_rows[c]).then_inc(rest_in[k], 16)

    def fetch(pool, k, u, prev):
        if prev is not None:
            pool.wait_ge(turned[k], turned.at(k, prev))
            if l == 0:
                pool.wait_ge(own_turned[k], own_turned.at(k, prev))
                pool.wait_ge(kept[k], kept.at(k, prev, 1))
        pool.wait_ge(index_in[k], index_in.at(k, u, 1 if l == 0 else 0))
        pool.wait_ge(w.ready, w.ready_count)
        settle(pool, w)
        if l == 0:
            gather(nc, b.src[:, k], a["x"], b.index[:, k, 0, :], gathered[k])
            gather(nc, b.own[:, k], a["x"], b.index[:, k, 1, :], own_in[k])
        else:
            gather(nc, b.src[:, k], old, b.index[:, k, 0, :], gathered[k])

    with nc.Block() as block:
        @block.sync
        def _(sp):
            for k in K:
                load(sp, k, 0, None)
            for u in iterations(sp, n, tail=1):
                for k in K:
                    if not isinstance(u, int) or u < n - 1:
                        load(sp, k, u + 1, u)
                for k in K:
                    c = u * STRANDS + k
                    if l == 0:
                        sp.wait_ge(gathered[k], gathered.at(k, u, T - 1))
                        sp.dma_start(first_rows[c], b.src[:, k, :, 0:D]).then_inc(kept[k], 16)
                        sp.wait_ge(own_in[k], own_in.at(k, u, T - 1))
                        sp.dma_start(first_rows[e.chunks + c], b.own[:, k]).then_inc(kept[k], 16)
                    sp.wait_ge(last_step[k], last_step.at(k, u))
                    sp.dma_start(new_rows[c], b.new[:, k]).then_inc(stored[k], 16)
            for k in K:
                sp.wait_ge(stored[k], stored.at(k, n - 1))
                if l == 0:
                    sp.wait_ge(kept[k], kept.at(k, n - 1, 1))

        @block.gpsimd
        def _(pool):
            for k in K:
                fetch(pool, k, 0, None)
            for u in iterations(pool, n, tail=1):
                for k in K:
                    if not isinstance(u, int) or u < n - 1:
                        fetch(pool, k, u + 1, u)
                if l == 2:
                    for k in K:
                        layer_norm_scale(nc, pool, w, b.moments, b.scale, k, u, 0, aggregated, powered, scaled)

        @block.tensor
        def _(pe):
            for u in iterations(pe, n):
                for k in K:
                    pe.wait_ge(gathered[k], gathered.at(k, u, T - 1))
                    turn(nc, w, b.a(k), b.src[:, k], turned[k])
                for k in K:
                    pe.wait_ge(own_in[k], own_in.at(k, u, T - 1 if l == 0 else 0))
                    if not first(u):
                        pe.wait_ge(own_kept[k], own_kept.before(k, u))
                    turn(nc, w, b.b(k), b.own[:, k], own_turned[k])
                for k in K:
                    pe.wait_ge(copied[k], copied.at(k, u))
                    if not first(u):
                        pe.wait_ge(last_step[k], last_step.before(k, u))
                        pe.wait_ge(h_kept[k], h_kept.before(k, u))
                    wide = b.wide(k, BW)
                    for half in range(2):
                        bias_rows(nc, w, wide[:, 2 * half:2 * half + 2], B_GAT[l], BW, 2)
                        for j in (2 * half, 2 * half + 1):
                            last = nc.tensor.matmul(wide[:, j], b.src_t[:, k, j * P:(j + 1) * P], w.gat[:, l, :],
                                                    start=False, stop=j % 2 == 1)
                    last.then_inc(projected[k], 1)
                for k in K:
                    pe.wait_ge(own_copied[k], own_copied.at(k, u))
                    for j in range(T):
                        last = nc.tensor.matmul(b.b(k)[:, 8 * j:8 * j + 8], b.own_t[:, k, j * P:(j + 1) * P],
                                                w.own_scores[:, l, :], start=True, stop=True)
                    last.then_inc(scored[k], 1)

        @block.scalar
        def _(act):
            for u in iterations(act, n):
                for k in K:
                    act.wait_ge(turned[k], turned.at(k, u))
                    nc.scalar.activation(b.src_t[:, k, :], b.a(k), ACT.Copy).then_inc(copied[k], 1)
                for k in K:
                    act.wait_ge(own_turned[k], own_turned.at(k, u))
                    nc.scalar.activation(b.own_t[:, k, :], b.b(k), ACT.Copy).then_inc(own_copied[k], 1)
                for k in K:
                    act.wait_ge(projected[k], projected.at(k, u))
                    nc.scalar.activation(b.e[:, k], b.wide(k, D), ACT.Exp).then_inc(exped[k], 1)
                    nc.scalar.activation(w.sums[:, u * STRANDS + k, :, 0:BW], b.wide(k, BW),
                                         ACT.Copy).then_inc(h_kept[k], 1)

        @block.vector
        def _(dve):
            for u in iterations(dve, n):
                for k in K:
                    dve.wait_ge(exped[k], exped.at(k, u))
                    nc.vector.tensor_scalar(b.e[:, k], b.e[:, k], 1.0, 1.0, ALU.min, ALU.subtract).then_inc(lowered[k], 1)
                for k in K:
                    dve.wait_ge(lowered[k], lowered.at(k, u))
                    dve.wait_ge(h_kept[k], h_kept.at(k, u))
                    if not first(u):
                        dve.wait_ge(stored[k], stored.before(k, u))
                    nc.vector.tensor_tensor(b.new[:, k], b.wide(k, D), b.e[:, k], ALU.max).then_inc(elued[k], 1)
                for k in K:
                    dve.wait_ge(scored[k], scored.at(k, u))
                    nc.vector.tensor_scalar(w.own_parts[:, u * STRANDS + k], b.b(k)[:, 0:8 * T].rearrange(
                        "p (j f) -> p j f", j=T), 1.0, None, ALU.mult).then_inc(own_kept[k], 1)
                if l == 2:
                    for k in K:
                        dve.wait_ge(elued[k], elued.at(k, u))
                        dve.wait_ge(rest_in[k], rest_in.at(k, u))
                        nc.vector.tensor_tensor(b.new[:, k], b.new[:, k], b.v[:, k, :, 0:D],
                                                ALU.add).then_inc(summed[k], 1)
                    for k in K:
                        dve.wait_ge(summed[k], summed.at(k, u))
                        ln_stats(nc, k, b.stats, b.new[:, k], tallied)
                    for k in K:
                        ln_moments(nc, dve, k, u, b, tallied, aggregated)
                    for k in K:
                        ln_apply(nc, dve, k, u, b, b.new[:, k], b.new[:, k], scaled, normed)
    sig.end(n)


def gat_softmax(nc, w, e, ps, sig):
    NS, NTS, NT = e.score_blocks, e.score_tiles, e.tiles
    ctx = ExitStack()
    with ctx:
        sb = sig.buffers(ctx)
        by_tile = sb("score_by_tile", [P, NS, P])
        fwd, bwd = sb("max_forward", [P, NS, P]), sb("max_backward", [P, NS, P])
        outer = sb("outer_ends", [P, 2, NTS])
        cand = sb("outer_candidates", [P, 2, NTS])
        best = sb("outer_best", [P, 2, NS])
        parts = w.own_parts[:, :, :, :].rearrange("p c j f -> p (c j) f")
        e_src = w.sums[:, :, :, D:BW].rearrange("p c j f -> p (c j) f")
        edge = w.edge_share[:, 0:NT, :]
        loop = w.loop_share[:, 0:NT, :]
        edge_cols = w.edge_share[:, :, :].rearrange("p t h -> p (t h)")
        loop_cols = w.loop_share[:, :, :].rearrange("p t h -> p (t h)")
        step = sig.make(1, per=12 + 2 * NS)
        turned, back, exped = sig.make(1), sig.make(1), sig.make(1)
        ends_out, ends_in = sig.dma(1, per=2 * NS), sig.dma(1, per=2)
        counts = {}
        with nc.Block() as block:
            @block.vector
            def _(dve):
                done = [0]

                def mark(ins):
                    ins.then_inc(step[0], 1)
                    done[0] += 1

                def wait():
                    dve.wait_ge(step[0], step.at(0, 0, done[0] - 1))

                nc.vector.memset(edge_cols, 0.0)
                mark(nc.vector.memset(loop_cols, 0.0))
                wait()
                nc.vector.tensor_tensor(edge, e_src, parts[:, :, 0:HEADS], ALU.add)
                mark(nc.vector.tensor_tensor(loop, parts[:, :, HEADS:2 * HEADS], parts[:, :, 0:HEADS], ALU.add))
                wait()
                nc.vector.scalar_tensor_tensor(edge, edge, SLOPE, edge, ALU.mult, ALU.max)
                mark(nc.vector.scalar_tensor_tensor(loop, loop, SLOPE, loop, ALU.mult, ALU.max))
                counts["scores"] = done[0] - 1
                dve.wait_ge(turned[0], turned.at(0, 0))
                mark(nc.vector.tensor_copy(by_tile[:, :, :].rearrange("p s e -> p (s e)"),
                                           ps[:, 0:2, :].rearrange("p b f -> p (b f)")[:, 0:NS * P]))
                wait()
                for s in range(NS):
                    nc.vector.tensor_tensor_scan(fwd[:, s, :], w.step_pen[:, s, 0:P], by_tile[:, s, :], -FAR,
                                                 ALU.add, ALU.max)
                    last = nc.vector.tensor_tensor_scan(bwd[:, s, ::-1], w.step_pen[:, s, 1:P + 1][:, ::-1],
                                                        by_tile[:, s, ::-1], -FAR, ALU.add, ALU.max)
                mark(last)
                wait()
                mark(nc.vector.tensor_tensor(fwd[:, :, :], fwd[:, :, :], bwd[:, :, :], ALU.max))
                counts["ends"] = done[0] - 1
                dve.wait_ge(ends_in[0], ends_in.at(0, 0, 1))
                for s in range(NS):
                    for i in range(2):
                        last = nc.vector.tensor_tensor(cand[:, i, :], outer[:, i, :], w.carry_pen[:, i, s, :], ALU.add)
                    mark(last)
                    wait()
                    for i in range(2):
                        last = nc.vector.tensor_reduce(best[:, i, s:s + 1], cand[:, i, :], AX.X, ALU.max)
                    mark(last)
                    wait()
                for i in range(2):
                    for s in range(NS):
                        last = nc.vector.scalar_tensor_tensor(fwd[:, s, :], w.end_pen[:, i, s, :], best[:, i, s:s + 1],
                                                              fwd[:, s, :], ALU.add, ALU.max)
                    mark(last)
                    wait()
                counts["maxima"] = done[0] - 1
                dve.wait_ge(back[0], back.at(0, 0))
                m = bwd[:, :, :].rearrange("p s e -> p (s e)")
                mark(nc.vector.tensor_tensor(m, ps[:, 2:4, :].rearrange("p b f -> p (b f)")[:, 0:NS * P], loop_cols,
                                             ALU.max))
                wait()
                nc.vector.tensor_tensor(edge_cols, edge_cols, m, ALU.subtract)
                mark(nc.vector.tensor_tensor(loop_cols, loop_cols, m, ALU.subtract))
                counts["shifted"] = done[0] - 1
                counts["all"] = done[0]

            step.per = counts["all"]

            @block.tensor
            def _(pe):
                pe.wait_ge(step[0], step.at(0, 0, counts["scores"]))
                for s in range(NS):
                    last = nc.tensor.transpose(ps[:, s // 4, (s % 4) * P:(s % 4 + 1) * P],
                                               edge_cols[:, s * P:(s + 1) * P], w.ident[:, :])
                last.then_inc(turned[0], 1)
                pe.wait_ge(step[0], step.at(0, 0, counts["maxima"]))
                for s in range(NS):
                    last = nc.tensor.transpose(ps[:, 2 + s // 4, (s % 4) * P:(s % 4 + 1) * P], fwd[:, s, :],
                                               w.ident[:, :])
                last.then_inc(back[0], 1)

            @block.sync
            def _(sp):
                sp.wait_ge(step[0], step.at(0, 0, counts["ends"]))
                for i, at in ((0, P - 1), (1, 0)):
                    for s in range(NS):
                        sp.dma_start(dram_ap(w.maxima_dram, i * HEADS * NTS + s * (P // HEADS),
                                             [[1, P // HEADS], [NTS, HEADS], [1, 1]]),
                                     fwd[:, s, at:at + 1],
                                     allow_slow_non_contiguous=True).then_inc(ends_out[0], 16)
                sp.wait_ge(ends_out[0], ends_out.at(0, 0, 2 * NS - 1))
                for i in range(2):
                    sp.dma_start(outer[:, i, :], dram_ap(w.maxima_dram, i * HEADS * NTS,
                                                         [[0, P // HEADS], [NTS, HEADS], [1, NTS]])
                                 ).then_inc(ends_in[0], 16)

            @block.scalar
            def _(act):
                act.wait_ge(step[0], step.at(0, 0, counts["shifted"]))
                nc.scalar.activation(edge_cols, edge_cols, ACT.Exp)
                nc.scalar.activation(loop_cols, loop_cols, ACT.Exp).then_inc(exped[0], 1)
        sig.end(1)


def sum_tile_rows(nc, w, e, sp, k, u, width, kept, ends_out):
    c = u * STRANDS + k
    sp.wait_ge(kept[k], kept.at(k, u))
    sp.dma_start(w.ends_rows_dram[0, c, :, :, 0:width], w.sums[P - 1:P, c, :, 0:width]).then_inc(ends_out[k], 16)
    sp.dma_start(w.ends_rows_dram[1, c, :, :, 0:width], w.sums[0:1, c, :, 0:width]).then_inc(ends_out[k], 16)


def same_segment(nc, w, e, b, dve, k, u, same_in, same):
    c = u * STRANDS + k
    dve.wait_ge(same_in[k], same_in.at(k, u))
    for j in range(T):
        last = nc.vector.tensor_scalar(b.same[:, k, j * P:(j + 1) * P], b.same[:, k, j * P:(j + 1) * P],
                                       w.dst_chunk[:, c, j:j + 1], None, ALU.is_equal)
    last.then_inc(same[k], 1)


def load_same(nc, w, sp, b, k, u, same_in):
    sp.dma_start(b.same[:, k, :], w.dst_rows_dram[u * STRANDS + k].partition_broadcast(P)).then_inc(same_in[k], 16)


def gat_sums(nc, w, e, b, sig):
    K = range(STRANDS)
    n = e.rounds
    width = D + HEADS
    same_in, ends_out = sig.dma(), sig.dma(per=2)
    same, weighted, added, kept = (sig.make() for _ in range(4))
    with nc.Block() as block:
        @block.sync
        def _(sp):
            for k in K:
                load_same(nc, w, sp, b, k, 0, same_in)
            for u in iterations(sp, n, tail=1):
                for k in K:
                    if not isinstance(u, int) or u < n - 1:
                        sp.wait_ge(added[k], added.at(k, u))
                        load_same(nc, w, sp, b, k, u + 1, same_in)
                for k in K:
                    sum_tile_rows(nc, w, e, sp, k, u, width, kept, ends_out)
            for k in K:
                sp.wait_ge(ends_out[k], ends_out.at(k, n - 1, 1))

        @block.vector
        def _(dve):
            for u in iterations(dve, n):
                for k in K:
                    same_segment(nc, w, e, b, dve, k, u, same_in, same)
                for k in K:
                    c = u * STRANDS + k
                    if not first(u):
                        dve.wait_ge(added[k], added.before(k, u))
                    share = w.edge_chunk[:, c]
                    for j in range(T):
                        nc.vector.tensor_tensor(b.v[:, k, j, 0:D].rearrange("p (h f) -> p h f", h=HEADS),
                                                w.sums[:, c, j, 0:D].rearrange("p (h f) -> p h f", h=HEADS),
                                                share[:, j, :].unsqueeze(2).broadcast_to([P, HEADS, HC]), ALU.mult)
                    nc.vector.tensor_scalar(b.v[:, k, :, D:width], share, 1.0, None, ALU.mult).then_inc(weighted[k], 1)

        @block.tensor
        def _(pe):
            for u in iterations(pe, n):
                for k in K:
                    pe.wait_ge(same[k], same.at(k, u))
                    pe.wait_ge(weighted[k], weighted.at(k, u))
                    if not first(u):
                        pe.wait_ge(kept[k], kept.before(k, u))
                    for j in range(T):
                        last = nc.tensor.matmul(b.wide(k, width)[:, j], b.same[:, k, j * P:(j + 1) * P],
                                                b.v[:, k, j, 0:width], start=True, stop=True)
                    last.then_inc(added[k], 1)

        @block.scalar
        def _(act):
            for u in iterations(act, n):
                for k in K:
                    act.wait_ge(added[k], added.at(k, u))
                    act.wait_ge(w.ready, w.ready_count)
                    nc.scalar.activation(w.sums[:, u * STRANDS + k, :, 0:width], b.wide(k, width),
                                         ACT.Copy).then_inc(kept[k], 1)
    sig.end(n)


def carry_sums(nc, w, e, ps, sig, width):
    NB = e.blocks
    ctx = ExitStack()
    with ctx:
        sb = sig.buffers(ctx)
        ends, outer = sb("end_sums", [P, 2, NB, WIDE]), sb("outer_sums", [P, 2, NB, WIDE])
        cleared, multiplied, copied = sig.make(1), sig.make(1), sig.make(1)
        ends_in, carried = sig.dma(1, per=2 * NB), sig.dma(1, per=2 * NB)
        with nc.Block() as block:
            @block.vector
            def _(dve):
                nc.vector.memset(ends[:, :, :, :], 0.0).then_inc(cleared[0], 1)
                dve.wait_ge(multiplied[0], multiplied.at(0, 0))
                for i in range(2):
                    last = nc.vector.tensor_copy(outer[:, i], ps[:, i, 0:NB * WIDE].rearrange("p (m f) -> p m f", m=NB))
                last.then_inc(copied[0], 1)

            @block.sync
            def _(sp):
                sp.wait_ge(cleared[0], cleared.at(0, 0))
                rows = w.ends_rows_dram.rearrange("s c a j f -> s (c a j) f")
                for i in range(2):
                    for m in range(NB):
                        sp.dma_start(ends[0:e.block_rows[m], i, m, 0:width],
                                     rows[i, m * P:m * P + e.block_rows[m], 0:width]).then_inc(ends_in[0], 16)
                sp.wait_ge(copied[0], copied.at(0, 0))
                for i in range(2):
                    for m in range(NB):
                        sp.dma_start(w.carry_dram[i, m * P:m * P + e.block_rows[m], :],
                                     outer[0:e.block_rows[m], i, m, :]).then_inc(carried[0], 16)
                sp.wait_ge(carried[0], carried.at(0, 0, 2 * NB - 1))

            @block.tensor
            def _(pe):
                pe.wait_ge(ends_in[0], ends_in.at(0, 0, 2 * NB - 1))
                for i in range(2):
                    for m in range(NB):
                        for b in range(NB):
                            last = nc.tensor.matmul(ps[:, i, m * WIDE:(m + 1) * WIDE],
                                                    w.carry_eq[:, i, b, m * P:(m + 1) * P], ends[:, i, b, :],
                                                    start=b == 0, stop=b == NB - 1)
                last.then_inc(multiplied[0], 1)
        sig.end(1)


def load_carry(w, sp, b, k, u, width, carry_in):
    c = u * STRANDS + k
    sp.dma_start(b.mask[:, k, :], w.masks_chunk_dram[c]).then_inc(carry_in[k], 16)
    sp.dma_start(b.carry[:, k, :, 0:width], w.carry_chunk_dram[c, :, :, 0:width]).then_inc(carry_in[k], 16)


def add_carry(nc, b, k, width, done):
    for j in range(T):
        last = nc.tensor.matmul(b.wide(k, width)[:, j], b.mask[:, k, j * P:(j + 1) * P], b.carry[:, k, j, 0:width],
                                start=True, stop=True)
    last.then_inc(done, 1)


def gat_finish(nc, w, e, b, sig, l, old, new):
    K = range(STRANDS)
    n = e.rounds
    width = D + HEADS
    own_in, carry_in, rest_in, stored = sig.dma(), sig.dma(per=2), sig.dma(), sig.dma()
    turned, copied, projected, carried, joined, looped, added, divided, exped, lowered, elued = (
        sig.make() for _ in range(11))
    totalled, inverted = sig.make(), sig.make()
    summed, tallied, aggregated, powered, scaled, normed = (sig.make() for _ in range(6))
    last_step = normed if l == 2 else elued
    if l != 2:
        sig.idle(rest_in, summed, tallied, aggregated, powered, scaled, normed)
    old_rows = old.rearrange("(c j p) f -> c p j f", j=T, p=P)
    new_rows = new.rearrange("(c j p) f -> c p j f", j=T, p=P)
    first_rows = w.tables[0].rearrange("(c j p) f -> c p j f", j=T, p=P)

    def load(sp, k, u, prev):
        c = u * STRANDS + k
        if prev is not None:
            sp.wait_ge(turned[k], turned.at(k, prev))
            settle(sp, w)
        sp.dma_start(b.own[:, k], old_rows[e.chunks + c]).then_inc(own_in[k], 16)
        if prev is not None:
            sp.wait_ge(carried[k], carried.at(k, prev))
            settle(sp, w)
        load_carry(w, sp, b, k, u, width, carry_in)
        if l == 2:
            if prev is not None:
                sp.wait_ge(summed[k], summed.at(k, prev))
                settle(sp, w)
            sp.dma_start(b.v[:, k, :, 0:D], first_rows[e.chunks + c]).then_inc(rest_in[k], 16)

    with nc.Block() as block:
        @block.sync
        def _(sp):
            for k in K:
                load(sp, k, 0, None)
            for u in iterations(sp, n, tail=1):
                for k in K:
                    if not isinstance(u, int) or u < n - 1:
                        load(sp, k, u + 1, u)
                for k in K:
                    sp.wait_ge(last_step[k], last_step.at(k, u))
                    sp.dma_start(new_rows[e.chunks + u * STRANDS + k], b.new[:, k]).then_inc(stored[k], 16)
            for k in K:
                sp.wait_ge(stored[k], stored.at(k, n - 1))

        @block.gpsimd
        def _(pool):
            if l == 2:
                for u in iterations(pool, n):
                    for k in K:
                        layer_norm_scale(nc, pool, w, b.moments, b.scale, k, u, 0, aggregated, powered, scaled)

        @block.tensor
        def _(pe):
            for u in iterations(pe, n):
                for k in K:
                    pe.wait_ge(own_in[k], own_in.at(k, u))
                    turn(nc, w, b.a(k), b.own[:, k], turned[k])
                for k in K:
                    pe.wait_ge(carry_in[k], carry_in.at(k, u, 1))
                    if not first(u):
                        pe.wait_ge(joined[k], joined.before(k, u))
                    add_carry(nc, b, k, width, carried[k])
                for k in K:
                    pe.wait_ge(copied[k], copied.at(k, u))
                    if not first(u):
                        pe.wait_ge(looped[k], looped.before(k, u))
                    bias_rows(nc, w, b.b(k), B_GAT[l])
                    for j in range(T):
                        last = nc.tensor.matmul(b.b(k)[:, j * D:(j + 1) * D], b.own_t[:, k, j * P:(j + 1) * P],
                                                w.gat[:, l, 0:D], start=False, stop=j == T - 1)
                    last.then_inc(projected[k], 1)

        @block.scalar
        def _(act):
            for u in iterations(act, n):
                for k in K:
                    act.wait_ge(turned[k], turned.at(k, u))
                    nc.scalar.activation(b.own_t[:, k, :], b.a(k), ACT.Copy).then_inc(copied[k], 1)
                for k in K:
                    act.wait_ge(divided[k], divided.at(k, u))
                    nc.scalar.activation(b.e[:, k], b.src[:, k, :, 0:D], ACT.Exp).then_inc(exped[k], 1)

        @block.vector
        def _(dve):
            def heads(rows):
                return rows.rearrange("p (h f) -> p h f", h=HEADS)

            for u in iterations(dve, n):
                for k in K:
                    dve.wait_ge(carried[k], carried.at(k, u))
                    if not first(u):
                        dve.wait_ge(elued[k], elued.before(k, u))
                    nc.vector.tensor_tensor(b.src[:, k, :, 0:width], b.wide(k, width),
                                            w.sums[:, u * STRANDS + k, :, 0:width], ALU.add).then_inc(joined[k], 1)
                for k in K:
                    dve.wait_ge(projected[k], projected.at(k, u))
                    for j in range(T):
                        last = nc.vector.tensor_tensor(
                            heads(b.e[:, k, j, :]), heads(b.b(k)[:, j * D:(j + 1) * D]),
                            w.loop_chunk[:, u * STRANDS + k, j, :].unsqueeze(2).broadcast_to([P, HEADS, HC]), ALU.mult)
                    last.then_inc(looped[k], 1)
                for k in K:
                    dve.wait_ge(joined[k], joined.at(k, u))
                    nc.vector.tensor_tensor(b.small[:, k, 0, :, 0:HEADS], b.src[:, k, :, D:width],
                                            w.loop_chunk[:, u * STRANDS + k], ALU.add).then_inc(totalled[k], 1)
                for k in K:
                    dve.wait_ge(totalled[k], totalled.at(k, u))
                    nc.vector.reciprocal(b.small[:, k, 1, :, 0:HEADS], b.small[:, k, 0, :, 0:HEADS]).then_inc(inverted[k], 1)
                for k in K:
                    dve.wait_ge(looped[k], looped.at(k, u))
                    nc.vector.tensor_tensor(b.src[:, k, :, 0:D], b.src[:, k, :, 0:D], b.e[:, k],
                                            ALU.add).then_inc(added[k], 1)
                for k in K:
                    dve.wait_ge(added[k], added.at(k, u))
                    dve.wait_ge(inverted[k], inverted.at(k, u))
                    for j in range(T):
                        last = nc.vector.tensor_tensor(
                            heads(b.src[:, k, j, 0:D]), heads(b.src[:, k, j, 0:D]),
                            b.small[:, k, 1, j, 0:HEADS].unsqueeze(2).broadcast_to([P, HEADS, HC]), ALU.mult)
                    last.then_inc(divided[k], 1)
                for k in K:
                    dve.wait_ge(exped[k], exped.at(k, u))
                    nc.vector.tensor_scalar(b.e[:, k], b.e[:, k], 1.0, 1.0, ALU.min, ALU.subtract).then_inc(lowered[k], 1)
                for k in K:
                    dve.wait_ge(lowered[k], lowered.at(k, u))
                    if not first(u):
                        dve.wait_ge(stored[k], stored.before(k, u))
                    nc.vector.tensor_tensor(b.new[:, k], b.src[:, k, :, 0:D], b.e[:, k], ALU.max).then_inc(elued[k], 1)
                if l == 2:
                    for k in K:
                        dve.wait_ge(elued[k], elued.at(k, u))
                        dve.wait_ge(rest_in[k], rest_in.at(k, u))
                        nc.vector.tensor_tensor(b.new[:, k], b.new[:, k], b.v[:, k, :, 0:D],
                                                ALU.add).then_inc(summed[k], 1)
                    for k in K:
                        dve.wait_ge(summed[k], summed.at(k, u))
                        ln_stats(nc, k, b.stats, b.new[:, k], tallied)
                    for k in K:
                        ln_moments(nc, dve, k, u, b, tallied, aggregated)
                    for k in K:
                        ln_apply(nc, dve, k, u, b, b.new[:, k], b.new[:, k], scaled, normed)
    sig.end(n)


def dst_update(nc, a, w, e, b, ps, sig, kind, old, new, out):
    K = range(STRANDS)
    n = e.rounds
    width = {"sage": D + 4, "rel": D, "att": WIDE}[kind]
    own_in, carry_in, stored = sig.dma(), sig.dma(per=2), sig.gather(per=T) if kind == "att" else sig.dma()
    index_in = sig.dma() if kind == "att" else None
    turned, copied, projected, carried, joined, totalled, inverted, divided = (sig.make() for _ in range(8))
    mean_turned, mean_copied, shifted, summed = (sig.make() for _ in range(4))
    tallied, aggregated, powered, scaled, normed = (sig.make() for _ in range(5))
    sig.idle(*{"sage": (shifted, summed), "rel": (totalled, inverted, divided, mean_turned, mean_copied),
               "att": (turned, copied, totalled, shifted)}[kind])
    old_rows = old.rearrange("(c j p) f -> c p j f", j=T, p=P)
    new_rows = None if new is None else new.rearrange("(c j p) f -> c p j f", j=T, p=P)

    def load(sp, k, u, prev):
        c = u * STRANDS + k
        if prev is not None:
            if kind != "att":
                sp.wait_ge(turned[k], turned.at(k, prev))
                settle(sp, w)
            if kind != "sage":
                sp.wait_ge(summed[k], summed.at(k, prev))
                settle(sp, w)
        sp.dma_start(b.own[:, k], old_rows[e.chunks + c]).then_inc(own_in[k], 16)
        if prev is not None:
            sp.wait_ge(carried[k], carried.at(k, prev))
            settle(sp, w)
        load_carry(w, sp, b, k, u, width, carry_in)
        if kind == "att":
            if prev is not None:
                sp.wait_ge(stored[k], stored.at(k, prev, T - 1))
                settle(sp, w)
            sp.dma_start(b.index[:, k, 0, :], w.lists_dram[2, c]).then_inc(index_in[k], 16)

    with nc.Block() as block:
        @block.sync
        def _(sp):
            for k in K:
                load(sp, k, 0, None)
            for u in iterations(sp, n, tail=1):
                for k in K:
                    if not isinstance(u, int) or u < n - 1:
                        load(sp, k, u + 1, u)
                if kind != "att":
                    for k in K:
                        sp.wait_ge(normed[k], normed.at(k, u))
                        sp.dma_start(new_rows[e.chunks + u * STRANDS + k], b.new[:, k]).then_inc(stored[k], 16)
            for k in K:
                sp.wait_ge(stored[k], stored.at(k, n - 1, T - 1 if kind == "att" else 0))

        @block.gpsimd
        def _(pool):
            for u in iterations(pool, n):
                for k in K:
                    layer_norm_scale(nc, pool, w, b.moments, b.scale, k, u, 0, aggregated, powered, scaled)
                if kind == "att":
                    for k in K:
                        pool.wait_ge(normed[k], normed.at(k, u))
                        pool.wait_ge(index_in[k], index_in.at(k, u))
                        pool.wait_ge(w.ready, w.ready_count)
                        settle(pool, w)
                        for j in range(T):
                            nc.gpsimd.indirect_dma_start(
                                out, bass.IndirectOffsetOnAxis(ap=b.index[:, k, 0, j:j + 1], axis=0),
                                b.new[:, k, j, :], None, bounds_check=e.n_nodes - 1,
                                oob_is_err=False).then_inc(stored[k], 16)

        @block.tensor
        def _(pe):
            for u in iterations(pe, n):
                if kind != "att":
                    for k in K:
                        pe.wait_ge(own_in[k], own_in.at(k, u))
                        if kind == "sage" and not first(u):
                            pe.wait_ge(mean_copied[k], mean_copied.before(k, u))
                        turn(nc, w, b.a(k), b.own[:, k], turned[k])
                for k in K:
                    pe.wait_ge(carry_in[k], carry_in.at(k, u, 1))
                    if not first(u):
                        pe.wait_ge(joined[k], joined.before(k, u))
                    add_carry(nc, b, k, width, carried[k])
                if kind == "rel":
                    for k in K:
                        pe.wait_ge(copied[k], copied.at(k, u))
                        if not first(u):
                            pe.wait_ge(shifted[k], shifted.before(k, u))
                        bias_rows(nc, w, b.b(k), B_REL)
                        for j in range(T):
                            last = nc.tensor.matmul(b.b(k)[:, j * D:(j + 1) * D], b.own_t[:, k, j * P:(j + 1) * P],
                                                    w.self_loop[:, :], start=False, stop=j == T - 1)
                        last.then_inc(projected[k], 1)
                else:
                    for k in K:
                        pe.wait_ge(divided[k], divided.at(k, u))
                        if kind == "sage":
                            pe.wait_ge(copied[k], copied.at(k, u))
                        turn(nc, w, b.a(k), b.e[:, k], mean_turned[k])
                    for k in K:
                        pe.wait_ge(mean_copied[k], mean_copied.at(k, u))
                        if not first(u):
                            if kind == "sage":
                                pe.wait_ge(normed[k], normed.before(k, u))
                            else:
                                pe.wait_ge(summed[k], summed.before(k, u))
                        bias_rows(nc, w, b.b(k), B_SAGE if kind == "sage" else B_O)
                        for j in range(T):
                            dst = b.b(k)[:, j * D:(j + 1) * D]
                            if kind == "sage":
                                nc.tensor.matmul(dst, b.own_t[:, k, j * P:(j + 1) * P], w.sage_own[:, :],
                                                 start=False, stop=False)
                            last = nc.tensor.matmul(dst, b.src_t[:, k, j * P:(j + 1) * P],
                                                    w.sage_mean[:, :] if kind == "sage" else w.o[:, :],
                                                    start=False, stop=j == T - 1)
                        last.then_inc(projected[k], 1)

        @block.scalar
        def _(act):
            for u in iterations(act, n):
                if kind != "att":
                    for k in K:
                        act.wait_ge(turned[k], turned.at(k, u))
                        if kind == "sage" and not first(u):
                            act.wait_ge(projected[k], projected.before(k, u))
                        nc.scalar.activation(b.own_t[:, k, :], b.a(k), ACT.Copy).then_inc(copied[k], 1)
                if kind != "rel":
                    for k in K:
                        act.wait_ge(mean_turned[k], mean_turned.at(k, u))
                        nc.scalar.activation(b.src_t[:, k, :], b.a(k), ACT.Copy).then_inc(mean_copied[k], 1)

        @block.vector
        def _(dve):
            for u in iterations(dve, n):
                for k in K:
                    dve.wait_ge(carried[k], carried.at(k, u))
                    nc.vector.tensor_tensor(b.src[:, k, :, 0:width], b.wide(k, width),
                                            w.sums[:, u * STRANDS + k, :, 0:width], ALU.add).then_inc(joined[k], 1)
                if kind == "sage":
                    for k in K:
                        dve.wait_ge(joined[k], joined.at(k, u))
                        nc.vector.tensor_scalar(b.small[:, k, 0, :, 0:1], b.src[:, k, :, D:D + 1], 1.0, None,
                                                ALU.max).then_inc(totalled[k], 1)
                    for k in K:
                        dve.wait_ge(totalled[k], totalled.at(k, u))
                        nc.vector.reciprocal(b.small[:, k, 1, :, 0:1], b.small[:, k, 0, :, 0:1]).then_inc(inverted[k], 1)
                    for k in K:
                        dve.wait_ge(inverted[k], inverted.at(k, u))
                        for j in range(T):
                            last = nc.vector.tensor_scalar(b.e[:, k, j, :], b.src[:, k, j, 0:D],
                                                           b.small[:, k, 1, j, 0:1], None, ALU.mult)
                        last.then_inc(divided[k], 1)
                    for k in K:
                        dve.wait_ge(projected[k], projected.at(k, u))
                        ln_stats(nc, k, b.stats, b.tiles(b.b(k)), tallied)
                if kind == "rel":
                    for k in K:
                        dve.wait_ge(joined[k], joined.at(k, u))
                        dve.wait_ge(projected[k], projected.at(k, u))
                        nc.vector.tensor_tensor(b.src[:, k, :, 0:D], b.tiles(b.b(k)), b.src[:, k, :, 0:D],
                                                ALU.add).then_inc(shifted[k], 1)
                    for k in K:
                        dve.wait_ge(shifted[k], shifted.at(k, u))
                        nc.vector.scalar_tensor_tensor(b.e[:, k], b.src[:, k, :, 0:D], 0.0, b.own[:, k], ALU.max,
                                                       ALU.add).then_inc(summed[k], 1)
                if kind == "att":
                    for k in K:
                        dve.wait_ge(joined[k], joined.at(k, u))
                        nc.vector.reciprocal(b.small[:, k, 1], b.src[:, k, :, D:WIDE]).then_inc(inverted[k], 1)
                    for k in K:
                        dve.wait_ge(inverted[k], inverted.at(k, u))
                        for j in range(T):
                            last = nc.vector.tensor_tensor(
                                b.e[:, k, j, :].rearrange("p (h f) -> p h f", h=AHEADS),
                                b.src[:, k, j, 0:D].rearrange("p (h f) -> p h f", h=AHEADS),
                                b.small[:, k, 1, j, :].unsqueeze(2).broadcast_to([P, AHEADS, AD]), ALU.mult)
                        last.then_inc(divided[k], 1)
                    for k in K:
                        dve.wait_ge(projected[k], projected.at(k, u))
                        dve.wait_ge(own_in[k], own_in.at(k, u))
                        nc.vector.tensor_tensor(b.e[:, k], b.tiles(b.b(k)), b.own[:, k], ALU.add).then_inc(summed[k], 1)
                rows = [b.tiles(b.b(k)) if kind == "sage" else b.e[:, k] for k in K]
                if kind != "sage":
                    for k in K:
                        dve.wait_ge(summed[k], summed.at(k, u))
                        ln_stats(nc, k, b.stats, rows[k], tallied)
                for k in K:
                    ln_moments(nc, dve, k, u, b, tallied, aggregated)
                for k in K:
                    if not first(u):
                        dve.wait_ge(stored[k], stored.before(k, u))
                    ln_apply(nc, dve, k, u, b, b.new[:, k], rows[k], scaled, normed)
    sig.end(n)


def sage_messages(nc, a, w, e, b, ps, sig, old, new):
    K = range(STRANDS)
    n = e.rounds
    width = D + 4
    index_in, gathered, same_in, ends_out, stored = sig.dma(), sig.gather(per=T), sig.dma(), sig.dma(per=2), sig.dma()
    same, added, kept, turned, copied, projected = (sig.make() for _ in range(6))
    tallied, aggregated, powered, scaled, normed = (sig.make() for _ in range(5))
    new_rows = new.rearrange("(c j p) f -> c p j f", j=T, p=P)

    def load(sp, k, u, prev):
        if prev is not None:
            sp.wait_ge(gathered[k], gathered.at(k, prev, T - 1))
            settle(sp, w)
        sp.dma_start(b.index[:, k, 0, :], w.lists_dram[3, u * STRANDS + k]).then_inc(index_in[k], 16)
        if prev is not None:
            sp.wait_ge(added[k], added.at(k, prev))
            settle(sp, w)
        load_same(nc, w, sp, b, k, u, same_in)

    def fetch(pool, k, u, prev):
        if prev is not None:
            pool.wait_ge(turned[k], turned.at(k, prev))
            pool.wait_ge(added[k], added.at(k, prev))
        pool.wait_ge(index_in[k], index_in.at(k, u))
        pool.wait_ge(w.ready, w.ready_count)
        settle(pool, w)
        gather(nc, b.src[:, k], old, b.index[:, k, 0, :], gathered[k])

    with nc.Block() as block:
        @block.vector
        def _(dve):
            nc.vector.memset(b.src[:, :, :, D:WIDE], 0.0)

    with nc.Block() as block:
        @block.vector
        def _(dve):
            nc.vector.memset(b.src[:, :, :, D:D + 1], 1.0)

    with nc.Block() as block:
        @block.sync
        def _(sp):
            for k in K:
                load(sp, k, 0, None)
            for u in iterations(sp, n, tail=1):
                for k in K:
                    if not isinstance(u, int) or u < n - 1:
                        load(sp, k, u + 1, u)
                for k in K:
                    sum_tile_rows(nc, w, e, sp, k, u, width, kept, ends_out)
                for k in K:
                    sp.wait_ge(normed[k], normed.at(k, u))
                    sp.dma_start(new_rows[u * STRANDS + k], b.new[:, k]).then_inc(stored[k], 16)
            for k in K:
                sp.wait_ge(ends_out[k], ends_out.at(k, n - 1, 1))
                sp.wait_ge(stored[k], stored.at(k, n - 1))

        @block.gpsimd
        def _(pool):
            for k in K:
                fetch(pool, k, 0, None)
            for u in iterations(pool, n, tail=1):
                for k in K:
                    if not isinstance(u, int) or u < n - 1:
                        fetch(pool, k, u + 1, u)
                for k in K:
                    layer_norm_scale(nc, pool, w, b.moments, b.scale, k, u, 0, aggregated, powered, scaled)

        @block.tensor
        def _(pe):
            for u in iterations(pe, n):
                for k in K:
                    pe.wait_ge(gathered[k], gathered.at(k, u, T - 1))
                    turn(nc, w, b.a(k), b.src[:, k], turned[k])
                for k in K:
                    pe.wait_ge(same[k], same.at(k, u))
                    if not first(u):
                        pe.wait_ge(kept[k], kept.before(k, u))
                    for j in range(T):
                        last = nc.tensor.matmul(b.wide(k, width)[:, j], b.same[:, k, j * P:(j + 1) * P],
                                                b.src[:, k, j, 0:width], start=True, stop=True)
                    last.then_inc(added[k], 1)
                for k in K:
                    pe.wait_ge(copied[k], copied.at(k, u))
                    if not first(u):
                        pe.wait_ge(normed[k], normed.before(k, u))
                    bias_rows(nc, w, b.b(k), B_SAGE)
                    for j in range(T):
                        last = nc.tensor.matmul(b.b(k)[:, j * D:(j + 1) * D], b.src_t[:, k, j * P:(j + 1) * P],
                                                w.sage_own[:, :], start=False, stop=j == T - 1)
                    last.then_inc(projected[k], 1)

        @block.scalar
        def _(act):
            for u in iterations(act, n):
                for k in K:
                    act.wait_ge(turned[k], turned.at(k, u))
                    nc.scalar.activation(b.src_t[:, k, :], b.a(k), ACT.Copy).then_inc(copied[k], 1)
                for k in K:
                    act.wait_ge(added[k], added.at(k, u))
                    act.wait_ge(w.ready, w.ready_count)
                    nc.scalar.activation(w.sums[:, u * STRANDS + k, :, 0:width], b.wide(k, width),
                                         ACT.Copy).then_inc(kept[k], 1)

        @block.vector
        def _(dve):
            for u in iterations(dve, n):
                for k in K:
                    same_segment(nc, w, e, b, dve, k, u, same_in, same)
                for k in K:
                    dve.wait_ge(projected[k], projected.at(k, u))
                    ln_stats(nc, k, b.stats, b.tiles(b.b(k)), tallied)
                for k in K:
                    ln_moments(nc, dve, k, u, b, tallied, aggregated)
                for k in K:
                    if not first(u):
                        dve.wait_ge(stored[k], stored.before(k, u))
                    ln_apply(nc, dve, k, u, b, b.new[:, k], b.tiles(b.b(k)), scaled, normed)
    sig.end(n)


def rel_messages(nc, a, w, e, b, ps, sig, old, new):
    K = range(STRANDS)
    width = D
    n = e.rounds
    index_in, gathered, same_in, ends_out, stored = sig.dma(), sig.gather(per=T), sig.dma(), sig.dma(per=2), sig.dma()
    same, added, kept, turned, copied, projected, summed = (sig.make() for _ in range(7))
    related, chosen = sig.make(per=T), sig.make(per=T * RELS)
    tallied, aggregated, powered, scaled, normed = (sig.make() for _ in range(5))
    new_rows = new.rearrange("(c j p) f -> c p j f", j=T, p=P)

    def load(sp, k, u, prev):
        if prev is not None:
            sp.wait_ge(gathered[k], gathered.at(k, prev, T - 1))
            settle(sp, w)
        sp.dma_start(b.index[:, k, 0, :], w.lists_dram[3, u * STRANDS + k]).then_inc(index_in[k], 16)
        if prev is not None:
            sp.wait_ge(added[k], added.at(k, prev))
            settle(sp, w)
        load_same(nc, w, sp, b, k, u, same_in)

    def fetch(pool, k, u, prev):
        if prev is not None:
            pool.wait_ge(summed[k], summed.at(k, prev))
        pool.wait_ge(index_in[k], index_in.at(k, u))
        pool.wait_ge(w.ready, w.ready_count)
        settle(pool, w)
        gather(nc, b.src[:, k], old, b.index[:, k, 0, :], gathered[k])

    with nc.Block() as block:
        @block.sync
        def _(sp):
            for k in K:
                load(sp, k, 0, None)
            for u in iterations(sp, n, tail=1):
                for k in K:
                    if not isinstance(u, int) or u < n - 1:
                        load(sp, k, u + 1, u)
                for k in K:
                    sum_tile_rows(nc, w, e, sp, k, u, width, kept, ends_out)
                for k in K:
                    sp.wait_ge(normed[k], normed.at(k, u))
                    sp.dma_start(new_rows[u * STRANDS + k], b.new[:, k]).then_inc(stored[k], 16)
            for k in K:
                sp.wait_ge(ends_out[k], ends_out.at(k, n - 1, 1))
                sp.wait_ge(stored[k], stored.at(k, n - 1))

        @block.gpsimd
        def _(pool):
            for k in K:
                fetch(pool, k, 0, None)
            for u in iterations(pool, n, tail=1):
                for k in K:
                    layer_norm_scale(nc, pool, w, b.moments, b.scale, k, u, 0, aggregated, powered, scaled)
                for k in K:
                    if not isinstance(u, int) or u < n - 1:
                        fetch(pool, k, u + 1, u)

        @block.tensor
        def _(pe):
            for u in iterations(pe, n):
                for k in K:
                    pe.wait_ge(gathered[k], gathered.at(k, u, T - 1))
                    if not first(u):
                        pe.wait_ge(summed[k], summed.before(k, u))
                    turn(nc, w, b.a(k), b.src[:, k], turned[k])
                for j in range(T):
                    for k in K:
                        if j == 0:
                            pe.wait_ge(copied[k], copied.at(k, u))
                            if not first(u):
                                pe.wait_ge(chosen[k], chosen.before(k, u))
                        else:
                            pe.wait_ge(chosen[k], chosen.at(k, u, j * RELS - 1))
                        for half in range(2):
                            last = nc.tensor.matmul(
                                b.ps[:, 4 * k + 2 + half, :], b.src_t[:, k, j * P:(j + 1) * P],
                                w.rel[:, half * RELS // 2:(half + 1) * RELS // 2, :].rearrange("p r o -> p (r o)"),
                                start=True, stop=True)
                        last.then_inc(related[k], 1)
                for k in K:
                    bias_rows(nc, w, b.a(k), B_REL)
                    for j in range(T):
                        last = nc.tensor.matmul(b.a(k)[:, j * D:(j + 1) * D], b.src_t[:, k, j * P:(j + 1) * P],
                                                w.self_loop[:, :], start=False, stop=j == T - 1)
                    last.then_inc(projected[k], 1)
                for k in K:
                    pe.wait_ge(same[k], same.at(k, u))
                    pe.wait_ge(chosen[k], chosen.at(k, u, T * RELS - 1))
                    if not first(u):
                        pe.wait_ge(kept[k], kept.before(k, u))
                    for j in range(T):
                        last = nc.tensor.matmul(b.b(k)[:, j * D:(j + 1) * D], b.same[:, k, j * P:(j + 1) * P],
                                                b.v[:, k, j, 0:D], start=True, stop=True)
                    last.then_inc(added[k], 1)

        @block.scalar
        def _(act):
            for u in iterations(act, n):
                for k in K:
                    act.wait_ge(turned[k], turned.at(k, u))
                    nc.scalar.activation(b.src_t[:, k, :], b.a(k), ACT.Copy).then_inc(copied[k], 1)
                for k in K:
                    act.wait_ge(added[k], added.at(k, u))
                    act.wait_ge(w.ready, w.ready_count)
                    nc.scalar.activation(w.sums[:, u * STRANDS + k, :, 0:D], b.tiles(b.b(k)),
                                         ACT.Copy).then_inc(kept[k], 1)

        @block.vector
        def _(dve):
            for u in iterations(dve, n):
                for k in K:
                    same_segment(nc, w, e, b, dve, k, u, same_in, same)
                for j in range(T):
                    for r in range(RELS):
                        for k in K:
                            c = u * STRANDS + k
                            mine = w.rel_chunk[:, r, c, j:j + 1]
                            product = b.ps[:, 4 * k + 2 + r // 4, (r % 4) * D:(r % 4 + 1) * D]
                            message = b.v[:, k, j, 0:D]
                            if r == 0:
                                dve.wait_ge(related[k], related.at(k, u, j))
                                if j == 0 and not first(u):
                                    dve.wait_ge(added[k], added.before(k, u))
                                nc.vector.tensor_scalar(message, product, mine, None, ALU.mult).then_inc(chosen[k], 1)
                            else:
                                dve.wait_ge(chosen[k], chosen.at(k, u, j * RELS + r - 1))
                                nc.vector.scalar_tensor_tensor(message, product, mine, message, ALU.mult,
                                                               ALU.add).then_inc(chosen[k], 1)
                for k in K:
                    dve.wait_ge(projected[k], projected.at(k, u))
                    nc.vector.scalar_tensor_tensor(b.e[:, k], b.tiles(b.a(k)), 0.0, b.src[:, k, :, 0:D], ALU.max,
                                                   ALU.add).then_inc(summed[k], 1)
                for k in K:
                    dve.wait_ge(summed[k], summed.at(k, u))
                    ln_stats(nc, k, b.stats, b.e[:, k], tallied)
                for k in K:
                    ln_moments(nc, dve, k, u, b, tallied, aggregated)
                for k in K:
                    if not first(u):
                        dve.wait_ge(stored[k], stored.before(k, u))
                    ln_apply(nc, dve, k, u, b, b.new[:, k], b.e[:, k], scaled, normed)
    sig.end(n)


def att_messages(nc, a, w, e, b, ps, sig, old):
    K = range(STRANDS)
    width = WIDE
    n = e.rounds
    index_in, gathered, same_in, ends_out, own_in = sig.dma(), sig.gather(per=T), sig.dma(), sig.dma(per=2), sig.dma()
    same, added, kept, turned, copied, own_turned, own_copied = (sig.make() for _ in range(7))
    keyed, queried, query_kept, matched, reduced, clipped, bounded, exped, weighted = (sig.make() for _ in range(9))
    old_rows = old.rearrange("(c j p) f -> c p j f", j=T, p=P)

    def load(sp, k, u, prev):
        c = u * STRANDS + k
        if prev is not None:
            sp.wait_ge(gathered[k], gathered.at(k, prev, T - 1))
            settle(sp, w)
        sp.dma_start(b.index[:, k, 0, :], w.lists_dram[3, c]).then_inc(index_in[k], 16)
        if prev is not None:
            sp.wait_ge(own_turned[k], own_turned.at(k, prev))
            settle(sp, w)
        sp.dma_start(b.own[:, k], old_rows[e.chunks + c]).then_inc(own_in[k], 16)
        if prev is not None:
            sp.wait_ge(added[k], added.at(k, prev))
            settle(sp, w)
        load_same(nc, w, sp, b, k, u, same_in)

    def fetch(pool, k, u, prev):
        if prev is not None:
            pool.wait_ge(turned[k], turned.at(k, prev))
        pool.wait_ge(index_in[k], index_in.at(k, u))
        pool.wait_ge(w.ready, w.ready_count)
        settle(pool, w)
        gather(nc, b.src[:, k], old, b.index[:, k, 0, :], gathered[k])

    with nc.Block() as block:
        @block.sync
        def _(sp):
            for k in K:
                load(sp, k, 0, None)
            for u in iterations(sp, n, tail=1):
                for k in K:
                    if not isinstance(u, int) or u < n - 1:
                        load(sp, k, u + 1, u)
                for k in K:
                    sum_tile_rows(nc, w, e, sp, k, u, width, kept, ends_out)
            for k in K:
                sp.wait_ge(ends_out[k], ends_out.at(k, n - 1, 1))

        @block.gpsimd
        def _(pool):
            for k in K:
                fetch(pool, k, 0, None)
            for u in iterations(pool, n, tail=1):
                for k in K:
                    if not isinstance(u, int) or u < n - 1:
                        fetch(pool, k, u + 1, u)

        @block.tensor
        def _(pe):
            for u in iterations(pe, n):
                for k in K:
                    pe.wait_ge(gathered[k], gathered.at(k, u, T - 1))
                    turn(nc, w, b.a(k), b.src[:, k], turned[k])
                for k in K:
                    pe.wait_ge(own_in[k], own_in.at(k, u))
                    if not first(u):
                        pe.wait_ge(query_kept[k], query_kept.before(k, u))
                    turn(nc, w, b.b(k), b.own[:, k], own_turned[k])
                for k in K:
                    pe.wait_ge(copied[k], copied.at(k, u))
                    if not first(u):
                        pe.wait_ge(kept[k], kept.before(k, u))
                    wide = b.wide(k, 2 * D)
                    for half in range(2):
                        nc.tensor.matmul(b.ps[:, 4 * k + 2 + half, :].rearrange("p (j s f) -> p j s f", j=2, s=2),
                                         w.ones4[0:3, 0:P],
                                         w.kv_bias[0:3].unsqueeze(1).broadcast_to([3, 2, 2, D]),
                                         start=True, stop=False)
                        for j in (2 * half, 2 * half + 1):
                            last = nc.tensor.matmul(wide[:, j], b.src_t[:, k, j * P:(j + 1) * P], w.kv[:, :],
                                                    start=False, stop=j % 2 == 1)
                    last.then_inc(keyed[k], 1)
                for k in K:
                    pe.wait_ge(own_copied[k], own_copied.at(k, u))
                    bias_rows(nc, w, b.b(k), B_Q)
                    for j in range(T):
                        last = nc.tensor.matmul(b.b(k)[:, j * D:(j + 1) * D], b.own_t[:, k, j * P:(j + 1) * P],
                                                w.q[:, :], start=False, stop=j == T - 1)
                    last.then_inc(queried[k], 1)
                for k in K:
                    pe.wait_ge(same[k], same.at(k, u))
                    pe.wait_ge(weighted[k], weighted.at(k, u))
                    for j in range(T):
                        last = nc.tensor.matmul(b.wide(k, WIDE)[:, j], b.same[:, k, j * P:(j + 1) * P],
                                                b.v[:, k, j, :], start=True, stop=True)
                    last.then_inc(added[k], 1)

        @block.scalar
        def _(act):
            for u in iterations(act, n):
                for k in K:
                    act.wait_ge(turned[k], turned.at(k, u))
                    nc.scalar.activation(b.src_t[:, k, :], b.a(k), ACT.Copy).then_inc(copied[k], 1)
                for k in K:
                    act.wait_ge(own_turned[k], own_turned.at(k, u))
                    nc.scalar.activation(b.own_t[:, k, :], b.b(k), ACT.Copy).then_inc(own_copied[k], 1)
                for k in K:
                    act.wait_ge(queried[k], queried.at(k, u))
                    if not first(u):
                        act.wait_ge(matched[k], matched.before(k, u))
                    nc.scalar.activation(b.e[:, k], b.tiles(b.b(k)), ACT.Copy).then_inc(query_kept[k], 1)
                for k in K:
                    act.wait_ge(bounded[k], bounded.at(k, u))
                    if not first(u):
                        act.wait_ge(weighted[k], weighted.before(k, u))
                        act.wait_ge(added[k], added.before(k, u))
                    nc.scalar.activation(b.v[:, k, :, D:WIDE], b.small[:, k, 2], ACT.Exp).then_inc(exped[k], 1)
                for k in K:
                    act.wait_ge(added[k], added.at(k, u))
                    act.wait_ge(w.ready, w.ready_count)
                    nc.scalar.activation(w.sums[:, u * STRANDS + k, :, :], b.wide(k, WIDE),
                                         ACT.Copy).then_inc(kept[k], 1)

        @block.vector
        def _(dve):
            for u in iterations(dve, n):
                for k in K:
                    same_segment(nc, w, e, b, dve, k, u, same_in, same)
                for k in K:
                    dve.wait_ge(keyed[k], keyed.at(k, u))
                    dve.wait_ge(query_kept[k], query_kept.at(k, u))
                    nc.vector.tensor_tensor(b.new[:, k], b.wide(k, D), b.e[:, k], ALU.mult).then_inc(matched[k], 1)
                for k in K:
                    dve.wait_ge(matched[k], matched.at(k, u))
                    nc.vector.tensor_reduce(b.small[:, k, 0].rearrange("p j h -> p (j h)"),
                                            b.new[:, k].rearrange("p j (h f) -> p (j h) f", h=AHEADS), AX.X,
                                            ALU.add).then_inc(reduced[k], 1)
                for k in K:
                    dve.wait_ge(reduced[k], reduced.at(k, u))
                    nc.vector.tensor_scalar(b.small[:, k, 1], b.small[:, k, 0], AD ** -0.5, 5.0, ALU.mult,
                                            ALU.min).then_inc(clipped[k], 1)
                for k in K:
                    dve.wait_ge(clipped[k], clipped.at(k, u))
                    if not first(u):
                        dve.wait_ge(exped[k], exped.before(k, u))
                    nc.vector.tensor_scalar(b.small[:, k, 2], b.small[:, k, 1], -5.0, None, ALU.max).then_inc(bounded[k], 1)
                for k in K:
                    dve.wait_ge(exped[k], exped.at(k, u))
                    for j in range(T):
                        last = nc.vector.tensor_tensor(
                            b.v[:, k, j, 0:D].rearrange("p (h f) -> p h f", h=AHEADS),
                            b.wide(k, 2 * D)[:, j, D:2 * D].rearrange("p (h f) -> p h f", h=AHEADS),
                            b.v[:, k, j, D:WIDE].unsqueeze(2).broadcast_to([P, AHEADS, AD]), ALU.mult)
                    last.then_inc(weighted[k], 1)
    sig.end(n)


class Weights:
    pass


def ready(nc, w):
    w.ready_count += 1
    with nc.Block() as block:
        @block.sync
        def _(sp):
            sp.sem_inc(w.ready, 1)


def edge_passes(nc, a, w, ps, sig, sb, out):
    e = Edges(a["x"].shape[0], a["src"].shape[0])
    NT, NTP, NC = e.tiles, e.padded, e.chunks

    def dram(name, shape, dt=F32):
        return nc.dram_tensor(f"dram_{name}", shape, dt, kind="Internal").ap()

    w.ready_count = 0
    w.ready = w.ctx.enter_context(nc.semaphore("ready"))
    w.settled = w.ctx.enter_context(nc.semaphore("settled"))
    w.sums = sb("sums", [P, NC, T, WIDE])
    w.dst_col = sb("dst_col", [P, NTP])
    w.is_rel = sb("is_rel", [P, RELS, NTP])
    w.carry_eq = sb("carry_eq", [P, 2, e.blocks, NTP])
    w.carry_pen = sb("carry_pen", [P, 2, e.score_blocks, e.score_tiles], BF16)
    w.step_pen = sb("step_pen", [P, e.score_blocks, P + 1], BF16)
    w.end_pen = sb("end_pen", [P, 2, e.score_blocks, P], BF16)
    w.own_parts = sb("own_parts", [P, NC, T, 2 * HEADS])
    w.edge_share = sb("edge_share", [P, e.score_tiles, HEADS])
    w.loop_share = sb("loop_share", [P, e.score_tiles, HEADS])
    w.dst_chunk = w.dst_col[:, 0:NT].rearrange("p (c j) -> p c j", j=T)
    w.rel_chunk = w.is_rel[:, :, 0:NT].rearrange("p r (c j) -> p r c j", j=T)
    w.edge_chunk = w.edge_share[:, 0:NT, :].rearrange("p (c j) h -> p c j h", j=T)
    w.loop_chunk = w.loop_share[:, 0:NT, :].rearrange("p (c j) h -> p c j h", j=T)
    w.tables = [dram(f"table_{i}", [2 * e.rows, D]) for i in range(3)]
    w.pos_dram = dram("positions", [e.n_nodes, 1], I32)
    w.lists_dram = dram("index_lists", [4, NC, P, T], I32)
    w.dst_dram = dram("dst_by_edge", [NTP * P])
    w.dst_rows_dram = w.dst_dram[0:e.rows].rearrange("(c e) -> c e", e=ROWS)
    w.ends_dram = dram("tile_ends", [2, NTP])
    w.masks_dram = dram("end_masks", [2, e.rows])
    w.masks_chunk_dram = w.masks_dram.rearrange("s (c e) -> c s e", e=ROWS)
    w.maxima_dram = dram("end_maxima", [2 * HEADS * e.score_tiles])
    w.ends_rows_dram = dram("end_sums", [2, NC, 1, T, WIDE])
    w.carry_dram = dram("outer_sums", [2, NT, WIDE])
    w.carry_chunk_dram = w.carry_dram.rearrange("s (c j) f -> c s j f", j=T)

    with ExitStack() as tmp:
        edge_setup(nc, a, w, e, ps, sig, sig.buffers(tmp))
    ready(nc, w)

    t = w.tables
    paths = [(t[0], t[1]), (t[1], t[2]), (t[2], t[1])]
    for l, (old, new) in enumerate(paths):
        with ExitStack() as tmp:
            gat_scores(nc, a, w, e, Strands(nc, sig, tmp, ps), ps, sig, l, old, new)
        ready(nc, w)
        gat_softmax(nc, w, e, ps, sig)
        ready(nc, w)
        with ExitStack() as tmp:
            gat_sums(nc, w, e, Strands(nc, sig, tmp, ps), sig)
        ready(nc, w)
        carry_sums(nc, w, e, ps, sig, D + HEADS)
        ready(nc, w)
        with ExitStack() as tmp:
            gat_finish(nc, w, e, Strands(nc, sig, tmp, ps), sig, l, old, new)
        ready(nc, w)
    for kind, old, new in (("sage", t[1], t[2]), ("rel", t[2], t[1]), ("att", t[1], None)):
        with ExitStack() as tmp:
            b = Strands(nc, sig, tmp, ps)
            if kind == "sage":
                sage_messages(nc, a, w, e, b, ps, sig, old, new)
            elif kind == "rel":
                rel_messages(nc, a, w, e, b, ps, sig, old, new)
            else:
                att_messages(nc, a, w, e, b, ps, sig, old)
        ready(nc, w)
        carry_sums(nc, w, e, ps, sig, {"sage": D + 4, "rel": D, "att": WIDE}[kind])
        ready(nc, w)
        with ExitStack() as tmp:
            dst_update(nc, a, w, e, Strands(nc, sig, tmp, ps), ps, sig, kind, old, new, out)
        ready(nc, w)


def program(nc, a, out):
    ctx = ExitStack()
    with ctx:
        def sb(name, shape, dt=F32):
            return ctx.enter_context(nc.sbuf_tensor(name, shape, dt))

        sig = Signals(nc, ctx)
        w = Weights()
        w.ctx = ctx
        w.ident = sb("identity", [P, P])
        w.ones_col = sb("ones_col", [P, 1])
        w.minus1 = sb("minus1", [P, 1])
        w.power, w.eps = sb("power", [P, T]), sb("eps", [P, T])
        w.ones4 = sb("ones4", [4, ROWS], BF16)
        w.bias3 = sb("bias3", [4, BIASES, BW], BF16)
        w.bo_rows = sb("bo_rows", [P, D])
        w.gat = sb("gat_weights", [P, GAT_LAYERS, BW])
        w.own_scores = sb("own_scores", [P, GAT_LAYERS, 2 * HEADS])
        w.sage_own, w.sage_mean = sb("sage_own", [P, D]), sb("sage_mean", [P, D])
        w.rel = sb("rel_weights", [P, RELS, D])
        w.self_loop = sb("self_loop", [P, D])
        w.q, w.kv, w.o = sb("wq", [P, D]), sb("wkv", [P, 2 * D]), sb("wo", [P, D])
        w.kv_bias = w.bias3[:, B_K:B_K + 2, 0:D]
        w.split_dram = nc.dram_tensor("bias_split", [3, BIASES, BW], BF16, kind="Internal").ap()
        ps = ctx.enter_context(nc.psum_tensor("banks", [P, 8, ROWS], F32))
        with ExitStack() as tmp:
            def tb(name, shape, dt=F32):
                return tmp.enter_context(nc.sbuf_tensor(name, shape, dt))
            w.raw = tb("raw_weights", [P, 6, D])
            w.gat_t = tb("gat_transposed", [P, GAT_LAYERS, D])
            w.att = tb("attention_vectors", [P, GAT_LAYERS, 2])
            w.att_heads = tb("attention_by_head", [P, GAT_LAYERS, 2 * HEADS])
            w.head_mask = tb("head_mask", [P, HEADS])
            w.brow = tb("bias_rows", [1, BIASES, BW])
            w.split = tb("bias_parts", [1, 3, BIASES, BW], BF16)
            weights_setup(nc, a, w, ps, sig)
        dense_pass(nc, a, w, ps, sig, out)
        edge_passes(nc, a, w, ps, sig, sb, out)


def kernel(**inputs):
    import concourse.bacc as _bacc
    from concourse.bass_utils import run_bass_kernel_spmd as _run

    nc = _bacc.Bacc("TRN2", target_bir_lowering=False, num_devices=1)
    arrays, aps = {}, {}
    for name, value in inputs.items():
        v = np.ascontiguousarray(value)
        arrays[f"in_{name}"] = v
        aps[name] = nc.dram_tensor(f"in_{name}", v.shape, mybir.dt.from_np(v.dtype), kind="ExternalInput").ap()
    out = nc.dram_tensor("out_0", inputs["x"].shape, F32, kind="ExternalOutput").ap()
    program(nc, aps, out)
    return _run(nc, [arrays], core_ids=[0]).results[0]["out_0"]
```

```python
from contextlib import ExitStack
from itertools import chain

import numpy as np

import concourse.bass as bass
from concourse import mybir

F32 = mybir.dt.float32
BF16 = mybir.dt.bfloat16
I32 = mybir.dt.int32
ALU = mybir.AluOpType
ACT = mybir.ActivationFunctionType
AX = mybir.AxisListType

P = 128
D = 128
T = 4
ROWS = P * T
HEADS = 4
HC = D // HEADS
SLOPE = 0.2
RELS = 8
CHOICES = RELS - 1
AHEADS = 8
AD = D // AHEADS
LN_EPS = 1e-5
GAT_LAYERS = 3
WIDE = D + AHEADS
FAR = 1e30
DENSE = 3
PASSES = 3 * GAT_LAYERS + 6
STRANDS = 2

B_GAT = (0, 1, 2)
B_GAT_SHIFTED = (0, 3, 4)
B_SAGE, B_REL, B_Q, B_K, B_V, B_O = 5, 6, 7, 8, 9, 10
BIASES = 11
BW = D + HEADS


class Signal:

    def __init__(self, sems, counts, unit, per):
        self.sems, self.counts, self.unit, self.per = sems, counts, unit, per

    def __getitem__(self, k):
        return self.sems[k]

    def at(self, k, u, n=0):
        return (u * self.per + (n + 1)) * self.unit + self.counts[k]

    def before(self, k, u):
        return u * (self.per * self.unit) + self.counts[k]


class Signals:

    def __init__(self, nc, ctx):
        self.nc, self.ctx, self.free, self.lent, self.n = nc, ctx, {"step": [], "dma": [], "gather": []}, [], 0
        self.scopes = 0

    def make(self, strands=STRANDS, per=1, kind="step"):
        unit = 1 if kind == "step" else 16
        sems, counts = [], []
        for _ in range(strands):
            if self.free[kind]:
                sem, count = self.free[kind].pop(0)
            else:
                sem, count = self.ctx.enter_context(self.nc.semaphore(f"{kind}_{self.n}")), 0
                self.n += 1
            sems.append(sem)
            counts.append(count)
        signal = Signal(sems, counts, unit, per)
        self.lent.append((kind, signal))
        return signal

    def dma(self, strands=STRANDS, per=1):
        return self.make(strands, per, "dma")

    def gather(self, strands=STRANDS, per=1):
        return self.make(strands, per, "gather")

    @staticmethod
    def idle(*signals):
        for signal in signals:
            signal.per = 0

    def buffers(self, ctx):
        self.scopes += 1
        tag = self.scopes
        return lambda name, shape, dt=F32: ctx.enter_context(self.nc.sbuf_tensor(f"{name}_{tag}", shape, dt))

    def keep(self):
        kept, self.lent = self.lent, []
        return kept

    def end(self, iterations):
        for kind, s in self.lent:
            for k, sem in enumerate(s.sems):
                self.free[kind].append((sem, s.counts[k] + iterations * s.per * s.unit))
        self.lent = []


def weights_setup(nc, a, w, ps, sig):
    sources = [
        (w.gat[:, :, 0:D], a["L0_gnn_W"].rearrange("l i o -> i l o")),
        (w.raw[:, 0:2, :], a["L1_gnn_W"].rearrange("o (s i) -> o s i", s=2)),
        (w.rel[:, :, :], a["L2_gnn_weight"].rearrange("r i o -> i r o")),
        (w.self_loop[:, :], a["L2_gnn_self_loop_weight"]),
        (w.raw[:, 2, :], a["L3_gnn_Wq"]), (w.raw[:, 3, :], a["L3_gnn_Wk"]),
        (w.raw[:, 4, :], a["L3_gnn_Wv"]), (w.raw[:, 5, :], a["L3_gnn_Wo"]),
        (w.brow[0:1, 0:3, 0:D], a["L0_gnn_bias"].rearrange("(a l) o -> a l o", a=1)),
        (w.brow[0:1, B_GAT_SHIFTED[1]:B_GAT_SHIFTED[2] + 1, 0:D],
         a["L0_gnn_bias"][1:3, :].rearrange("(a l) o -> a l o", a=1)),
        (w.bo_rows[:, :], a["L3_gnn_bo"].partition_broadcast(P)),
    ]
    for row, name in ((B_SAGE, "L1_gnn_b"), (B_REL, "L2_gnn_bias"), (B_Q, "L3_gnn_bq"),
                      (B_K, "L3_gnn_bk"), (B_V, "L3_gnn_bv"), (B_O, "L3_gnn_bo")):
        sources.append((w.brow[0:1, row, 0:D], a[name].rearrange("(a o) -> a o", a=1)))
    for l in range(GAT_LAYERS):
        for s, name in enumerate(("L0_gnn_att_src", "L0_gnn_att_dst")):
            sources.append((w.att[:, l, s:s + 1], a[name][l].rearrange("h (c b) -> (h c) b", b=1)))
    loads = sig.dma(1, per=len(sources))
    zeroed, cleared = sig.make(1), sig.make(1, per=3)
    with nc.Block() as block:
        @block.sync
        def _(sp):
            sp.wait_ge(zeroed[0], zeroed.at(0, 0))
            for dst, src in sources:
                sp.dma_start(dst, src).then_inc(loads[0], 16)
            sp.wait_ge(loads[0], loads.at(0, 0, len(sources) - 1))

        @block.vector
        def _(dve):
            nc.vector.memset(w.brow[:, :, :], 0.0).then_inc(zeroed[0], 1)
            nc.vector.memset(w.bias3[:, :, :], 1.0)
            nc.vector.memset(w.ones_col[:, :], 1.0)
            nc.vector.memset(w.ones4[:, :], 1.0)
            nc.vector.memset(w.minus1[:, :], -1.0)
            nc.vector.memset(w.power[:, :], -0.5)
            nc.vector.memset(w.eps[:, :], LN_EPS)

        @block.gpsimd
        def _(pool):
            nc.gpsimd.memset(w.ident[:, :], 0.0).then_inc(cleared[0], 1)
            nc.gpsimd.memset(w.head_mask[:, :], 1.0).then_inc(cleared[0], 1)
            pool.wait_ge(cleared[0], cleared.at(0, 0, 1))
            nc.gpsimd.affine_select(out=w.ident[:, :], in_=w.ident[:, :], compare_op=ALU.not_equal, fill=1.0,
                                    base=0, pattern=[[-1, P]], channel_multiplier=1)
            nc.gpsimd.affine_select(out=w.head_mask[:, :], in_=w.head_mask[:, :], compare_op=ALU.is_ge, fill=0.0,
                                    base=0, pattern=[[-HC, HEADS]],
                                    channel_multiplier=1).then_inc(cleared[0], 1)
            pool.wait_ge(cleared[0], cleared.at(0, 0, 2))
            nc.gpsimd.affine_select(out=w.head_mask[:, :], in_=w.head_mask[:, :], compare_op=ALU.is_ge, fill=0.0,
                                    base=HC - 1, pattern=[[HC, HEADS]], channel_multiplier=-1)

    sig.end(1)

    transposed, masked, scores, scored, rows, hi, mid, mid32, lo, back = (sig.make(1) for _ in range(10))
    split_out, split_in = sig.dma(1, per=3), sig.dma(1)
    with nc.Block() as block:
        @block.tensor
        def _(pe):
            for l in range(GAT_LAYERS):
                nc.tensor.transpose(ps[:, 0, l * D:(l + 1) * D], w.gat[:, l, 0:D], w.ident[:, :])
            for i in range(6):
                nc.tensor.transpose(ps[:, 1 + i // 4, (i % 4) * D:(i % 4 + 1) * D], w.raw[:, i, :], w.ident[:, :])
            for l in (1, 2):
                last = nc.tensor.matmul(ps[0:1, 3, l * D:(l + 1) * D], w.ones_col[:, :], w.gat[:, l, 0:D],
                                        start=True, stop=True)
            last.then_inc(transposed[0], 1)
            pe.wait_ge(masked[0], masked.at(0, 0))
            for l in range(GAT_LAYERS):
                last = nc.tensor.matmul(ps[:, 4, 8 * l:8 * l + 8], w.gat_t[:, l, :], w.att_heads[:, l, :],
                                        start=True, stop=True)
            last.then_inc(scores[0], 1)

        @block.vector
        def _(dve):
            dve.wait_ge(transposed[0], transposed.at(0, 0))
            nc.vector.tensor_copy(w.gat_t[:, :, :], ps[:, 0, 0:3 * D].rearrange("p (l o) -> p l o", o=D))
            for l in range(GAT_LAYERS):
                for s in range(2):
                    last = nc.vector.tensor_scalar(w.att_heads[:, l, 4 * s:4 * s + 4], w.head_mask[:, :],
                                                   w.att[:, l, s:s + 1], None, ALU.mult)
            last.then_inc(masked[0], 1)
            nc.vector.tensor_tensor(w.sage_own[:, :], ps[:, 1, 0:D], w.ident[:, :], ALU.add)
            nc.vector.tensor_copy(w.sage_mean[:, :], ps[:, 1, D:2 * D])
            nc.vector.tensor_copy(w.q[:, :], ps[:, 1, 2 * D:3 * D])
            nc.vector.tensor_copy(w.kv[:, 0:D], ps[:, 1, 3 * D:4 * D])
            nc.vector.tensor_copy(w.kv[:, D:2 * D], ps[:, 2, 0:D])
            nc.vector.tensor_copy(w.o[:, :], ps[:, 2, D:2 * D])
            for l in (1, 2):
                last = nc.vector.tensor_tensor(w.brow[0:1, B_GAT_SHIFTED[l], 0:D],
                                               w.brow[0:1, B_GAT_SHIFTED[l], 0:D],
                                               ps[0:1, 3, l * D:(l + 1) * D], ALU.subtract)
            last.then_inc(rows[0], 1)
            dve.wait_ge(rows[0], rows.at(0, 0))
            nc.vector.tensor_copy(w.split[0:1, 0], w.brow[:, :, :]).then_inc(hi[0], 1)
            dve.wait_ge(hi[0], hi.at(0, 0))
            nc.vector.tensor_tensor(w.brow[:, :, :], w.brow[:, :, :], w.split[0:1, 0], ALU.subtract).then_inc(mid32[0], 1)
            dve.wait_ge(mid32[0], mid32.at(0, 0))
            nc.vector.tensor_copy(w.split[0:1, 1], w.brow[:, :, :]).then_inc(mid[0], 1)
            dve.wait_ge(mid[0], mid.at(0, 0))
            nc.vector.tensor_tensor(w.brow[:, :, :], w.brow[:, :, :], w.split[0:1, 1], ALU.subtract).then_inc(lo[0], 1)
            dve.wait_ge(lo[0], lo.at(0, 0))
            nc.vector.tensor_copy(w.split[0:1, 2], w.brow[:, :, :]).then_inc(back[0], 1)
            dve.wait_ge(scores[0], scores.at(0, 0))
            for l in range(GAT_LAYERS):
                nc.vector.tensor_copy(w.gat[:, l, D:BW], ps[:, 4, 8 * l:8 * l + 4])
                nc.vector.tensor_copy(w.own_scores[:, l, 0:4], ps[:, 4, 8 * l + 4:8 * l + 8])
                last = nc.vector.tensor_copy(w.own_scores[:, l, 4:8], ps[:, 4, 8 * l:8 * l + 4])
            last.then_inc(scored[0], 1)

        @block.sync
        def _(sp):
            sp.wait_ge(back[0], back.at(0, 0))
            for s in range(3):
                sp.dma_start(w.split_dram[s:s + 1], w.split[0:1, s]).then_inc(split_out[0], 16)
            sp.wait_ge(split_out[0], split_out.at(0, 0, 2))
            sp.dma_start(w.bias3[0:3, :, :], w.split_dram[0:3]).then_inc(split_in[0], 16)
            sp.wait_ge(split_in[0], split_in.at(0, 0))
            sp.wait_ge(scored[0], scored.at(0, 0))
    sig.end(1)


def layer_norm_scale(nc, pool, w, moments, scale, k, u, n, summed, powered, ready):
    pool.wait_ge(summed[k], summed.at(k, u, n))
    nc.gpsimd.tensor_tensor(scale[:, k, :], moments[:, k, :, 1], w.eps[:, :], ALU.add).then_inc(powered[k], 1)
    pool.wait_ge(powered[k], powered.at(k, u, n))
    nc.gpsimd.tensor_tensor(scale[:, k, :], scale[:, k, :], w.power[:, :], ALU.pow).then_inc(ready[k], 1)


def dense_pass(nc, a, w, ps, sig, out, start, beside):
    x, out = a["x"][start:, :], out[start:, :]
    n_nodes = x.shape[0]
    groups = -(-n_nodes // ROWS)
    assert groups % DENSE == 0
    rounds = groups // DENSE
    full = n_nodes // ROWS
    x_groups = x[0:full * ROWS, :].rearrange("(g p j) f -> g p (j f)", p=P, j=T)
    out_groups = out[0:full * ROWS, :].rearrange("(g p j) f -> g p (j f)", p=P, j=T)
    last_rows = slice(n_nodes - ROWS, n_nodes)
    x_last = x[last_rows, :].rearrange("(p j) f -> p (j f)", j=T)
    out_last = out[last_rows, :].rearrange("(p j) f -> p (j f)", j=T)
    repeated = (ROWS - (n_nodes - full * ROWS)) // T
    K = range(DENSE)
    ctx = ExitStack()
    with ctx:
        sb = sig.buffers(ctx)
        room = w.sums[:, :, :, :].rearrange("p c j f -> p (c j f)")
        X, XT, E, R, Y = (room[:, i * DENSE * ROWS:(i + 1) * DENSE * ROWS].rearrange("p (k r) -> p k r", k=DENSE)
                          for i in range(5))
        stats = sb("dense_stats", [P, DENSE, T, 6])
        moments = sb("dense_moments", [P, DENSE, T, 2])
        scale = sb("dense_scale", [P, DENSE, T])
        spare = sb("dense_spare", [P, 1])

        def A(k):
            return ps[:, 2 * k, :]

        def B(k):
            return ps[:, 2 * k + 1, :]

        def tile(j):
            return slice(j * D, (j + 1) * D)

        loaded, stored = sig.dma(DENSE), sig.dma(DENSE)
        products = sig.make(DENSE, per=8)
        copied = sig.make(DENSE, per=3)
        exped = sig.make(DENSE, per=3)
        elued = sig.make(DENSE, per=2)
        relued = sig.make(DENSE)
        summed = sig.make(DENSE, per=2)
        tallied = sig.make(DENSE, per=4)
        aggregated = sig.make(DENSE, per=4)
        powered, scaled = sig.make(DENSE, per=4), sig.make(DENSE, per=4)
        normed = sig.make(DENSE, per=4)

        def load(sp, k, u):
            g = u * DENSE + k
            src = x_last if isinstance(g, int) and g == full else x_groups[g]
            sp.dma_start(X[:, k, :], src).then_inc(loaded[k], 16)

        def store(sp, k, u):
            sp.wait_ge(normed[k], normed.at(k, u, 3))
            g = u * DENSE + k
            if isinstance(g, int) and g == full:
                sp.dma_start(out_last[repeated:P, :], Y[repeated:P, k, :]).then_inc(stored[k], 16)
            else:
                sp.dma_start(out_groups[g], Y[:, k, :]).then_inc(stored[k], 16)

        with nc.Block() as block:
            @block.sync
            def _(sp):
                for k in K:
                    load(sp, k, 0)
                for u in iterations(sp, rounds - 2) if rounds > 2 else ():
                    for k in K:
                        sp.wait_ge(summed[k], summed.at(k, u))
                        load(sp, k, u + 1)
                    for k in K:
                        store(sp, k, u)
                u = rounds - 2
                for k in K:
                    sp.wait_ge(summed[k], summed.at(k, u))
                    load(sp, k, u + 1)
                for k in K:
                    store(sp, k, u)
                for k in K:
                    store(sp, k, u + 1)
                for k in K:
                    sp.wait_ge(stored[k], stored.at(k, u + 1))

            @block.tensor
            def _(pe):
                def transpose_rows(k, u, n, dst, src):
                    for j in range(T):
                        last = nc.tensor.transpose(dst[:, tile(j)], src[:, k, tile(j)], w.ident[:, :])
                    last.then_inc(products[k], 1)

                def bias_then(k, dst, row):
                    nc.tensor.matmul(dst, w.ones4[0:3, 0:P], w.bias3[0:3, row, 0:D].unsqueeze(1).broadcast_to([3, T, D]),
                                     start=True, stop=False)

                def rows_out(k, dst, weight):
                    for j in range(T):
                        last = nc.tensor.matmul(dst[:, tile(j)], XT[:, k, tile(j)], weight, start=False, stop=j == T - 1)
                    last.then_inc(products[k], 1)

                for u in iterations(pe, rounds):
                    for k in K:
                        pe.wait_ge(loaded[k], loaded.at(k, u))
                        transpose_rows(k, u, 0, A(k), X)
                    for k in K:
                        pe.wait_ge(copied[k], copied.at(k, u, 0))
                        if not first(u):
                            pe.wait_ge(aggregated[k], aggregated.before(k, u))
                        nc.tensor.matmul(B(k), w.bias3[0:4, B_GAT_SHIFTED[0], 0:D], w.ones4[:, :], start=True, stop=False)
                        nc.tensor.matmul(B(k), w.gat[:, 0, 0:D], XT[:, k, :], start=False, stop=True).then_inc(products[k], 1)
                    for k in K:
                        pe.wait_ge(elued[k], elued.at(k, u, 0))
                        nc.tensor.matmul(A(k), w.bias3[0:4, B_GAT_SHIFTED[1], 0:D], w.ones4[:, :], start=True, stop=False)
                        nc.tensor.matmul(A(k), w.gat[:, 1, 0:D], XT[:, k, :], start=False, stop=True).then_inc(products[k], 1)
                    for k in K:
                        pe.wait_ge(elued[k], elued.at(k, u, 1))
                        bias_then(k, B(k), B_GAT_SHIFTED[2])
                        rows_out(k, B(k), w.gat[:, 2, 0:D])
                    for k in K:
                        pe.wait_ge(normed[k], normed.at(k, u, 0))
                        transpose_rows(k, u, 4, A(k), Y)
                    for k in K:
                        pe.wait_ge(copied[k], copied.at(k, u, 1))
                        bias_then(k, B(k), B_SAGE)
                        rows_out(k, B(k), w.sage_own[:, :])
                    for k in K:
                        pe.wait_ge(normed[k], normed.at(k, u, 1))
                        transpose_rows(k, u, 6, A(k), R)
                    for k in K:
                        pe.wait_ge(copied[k], copied.at(k, u, 2))
                        bias_then(k, B(k), B_REL)
                        rows_out(k, B(k), w.self_loop[:, :])

            @block.scalar
            def _(act):
                def copy_out(k, u, n, product):
                    act.wait_ge(products[k], products.at(k, u, product))
                    nc.scalar.activation(XT[:, k, :], A(k), ACT.Copy).then_inc(copied[k], 1)

                with act.Fori(0, rounds) as u:
                    for k in K:
                        copy_out(k, u, 0, 0)
                    for k in K:
                        act.wait_ge(products[k], products.at(k, u, 1))
                        nc.scalar.activation(E[:, k, :], B(k), ACT.Exp, bias=w.minus1[:, :]).then_inc(exped[k], 1)
                    for k in K:
                        act.wait_ge(products[k], products.at(k, u, 2))
                        nc.scalar.activation(E[:, k, :], A(k), ACT.Exp, bias=w.minus1[:, :]).then_inc(exped[k], 1)
                    for k in K:
                        act.wait_ge(products[k], products.at(k, u, 3))
                        nc.scalar.activation(E[:, k, :], B(k), ACT.Exp).then_inc(exped[k], 1)
                    for k in K:
                        copy_out(k, u, 1, 4)
                    for k in K:
                        copy_out(k, u, 2, 6)

            @block.gpsimd
            def _(pool):
                line = beside(pool, rounds * 4 * DENSE)
                for u in range(rounds):
                    for n in range(4):
                        for k in K:
                            layer_norm_scale(nc, pool, w, moments, scale, k, u, n, aggregated, powered, scaled)
                            next(line, None)
                for _ in line:
                    pass

            @block.vector
            def _(dve):
                def row_stats(k, src):
                    for j in range(T):
                        last = nc.vector.bn_stats(stats[:, k, j, :], src[:, tile(j)])
                    last.then_inc(tallied[k], 1)

                def moments_of(u, n):
                    dve.wait_ge(tallied[DENSE - 1], tallied.at(DENSE - 1, u, n))
                    nc.vector.memset(spare[:, :], 0.0)
                    for k in K:
                        for j in range(T):
                            last = nc.vector.bn_aggr(moments[:, k, j, :], stats[:, k, j, :])
                        last.then_inc(aggregated[k], 1)

                def normalise(k, u, n, dst, src):
                    dve.wait_ge(scaled[k], scaled.at(k, u, n))
                    for j in range(T):
                        last = nc.vector.tensor_scalar(dst[:, tile(j)], src[:, tile(j)], moments[:, k, j, 0:1],
                                                       scale[:, k, j:j + 1], ALU.subtract, ALU.mult)
                    last.then_inc(normed[k], 1)

                for u in iterations(dve, rounds):
                    for l, src in enumerate((B, A)):
                        for k in K:
                            dve.wait_ge(exped[k], exped.at(k, u, l))
                            nc.vector.scalar_tensor_tensor(XT[:, k, :], E[:, k, :], 1.0, src(k), ALU.min,
                                                           ALU.max).then_inc(elued[k], 1)
                    for k in K:
                        dve.wait_ge(exped[k], exped.at(k, u, 2))
                        nc.vector.scalar_tensor_tensor(R[:, k, :], B(k), 0.0, X[:, k, :], ALU.max,
                                                       ALU.add).then_inc(relued[k], 1)
                    for k in K:
                        dve.wait_ge(relued[k], relued.at(k, u))
                        nc.vector.scalar_tensor_tensor(R[:, k, :], E[:, k, :], 1.0, R[:, k, :], ALU.min,
                                                       ALU.add).then_inc(summed[k], 1)
                    for k in K:
                        dve.wait_ge(summed[k], summed.at(k, u, 0))
                        row_stats(k, R[:, k, :])
                    moments_of(u, 0)
                    for k in K:
                        if not first(u):
                            dve.wait_ge(stored[k], stored.before(k, u))
                        normalise(k, u, 0, Y[:, k, :], R[:, k, :])
                    for k in K:
                        dve.wait_ge(products[k], products.at(k, u, 5))
                        row_stats(k, B(k))
                    moments_of(u, 1)
                    for k in K:
                        normalise(k, u, 1, R[:, k, :], B(k))
                    for k in K:
                        dve.wait_ge(products[k], products.at(k, u, 7))
                        dve.wait_ge(normed[k], normed.at(k, u, 1))
                        nc.vector.scalar_tensor_tensor(Y[:, k, :], B(k), 0.0, R[:, k, :], ALU.max,
                                                       ALU.add).then_inc(summed[k], 1)
                    for k in K:
                        dve.wait_ge(summed[k], summed.at(k, u, 1))
                        row_stats(k, Y[:, k, :])
                    moments_of(u, 2)
                    for k in K:
                        dve.wait_ge(scaled[k], scaled.at(k, u, 2))
                        for j in range(T):
                            last = nc.vector.scalar_tensor_tensor(R[:, k, tile(j)], Y[:, k, tile(j)],
                                                                  scale[:, k, j:j + 1], w.bo_rows[:, :], ALU.mult,
                                                                  ALU.add)
                        last.then_inc(normed[k], 1)
                    for k in K:
                        dve.wait_ge(normed[k], normed.at(k, u, 2))
                        row_stats(k, R[:, k, :])
                    moments_of(u, 3)
                    for k in K:
                        normalise(k, u, 3, Y[:, k, :], R[:, k, :])
        sig.end(rounds)


class Edges:

    def __init__(self, n_nodes, n_edges):
        self.n_nodes, self.n_edges = n_nodes, n_edges
        self.chunks = -(-n_edges // (ROWS * STRANDS)) * STRANDS
        self.rounds = self.chunks // STRANDS
        self.tiles = self.chunks * T
        self.rows = self.tiles * P
        self.blocks = -(-self.tiles // P)
        self.padded = self.blocks * P
        self.score_blocks = -(-self.tiles * HEADS // P)
        self.score_tiles = self.score_blocks * P // HEADS
        self.block_rows = [min(P, self.tiles - b * P) for b in range(self.blocks)]


def dram_ap(ap, offset, pattern):
    return bass.AP(tensor=ap.tensor, offset=offset, ap=pattern)


def iterations(eng, n, tail=0, head=1):
    for u in range(min(head, n)):
        yield u
    if n - tail > head:
        with eng.Fori(head, n - tail) as u:
            yield u
    for u in range(max(n - tail, head), n):
        yield u


def first(u):
    return isinstance(u, int) and u == 0


def edge_setup(nc, a, w, e, ps, sig, sb, dense):
    NB, NTP, NT, NS, NTS = e.blocks, e.padded, e.tiles, e.score_blocks, e.score_tiles
    BIG = float(1 << 21)
    idx = sb("edge_fields", [P, NB, 4, P], I32)
    idx_f = sb("edge_fields_f", [P, NB, 4, P])
    col = sb("edge_columns", [P, 4, NTP])
    masks = sb("end_masks", [P, NB, 2, P])
    tmp = sb("setup_tmp", [P, 2, NTP])
    ends = sb("tile_ends", [P, 2, NTP])
    own_first, own_last = sb("own_first", [P, NS]), sb("own_last", [P, NS])
    dst_scores = sb("dst_by_score", [P, NS, P])
    fill = sb("pos_fill", [P, -(-e.n_nodes // P)], I32)
    slot = sb("slot", [P, NTP])
    slot_i = sb("slot_i", [P, NTP], I32)
    ints = sb("index_ints", [P, 3, NTP], I32)
    pos = sb("positions", [P, NTP], I32)
    pos_f = sb("positions_f", [P, 2, NTP])

    srcs = []
    for f, (name, skip) in enumerate((("src", 0), ("dst", 0), ("dst", 1), ("edge_type_8", 0))):
        n = e.n_edges - skip
        for b in range(NB):
            lo, hi = b * P, min((b + 1) * P, n // P)
            if hi > lo:
                srcs.append((idx[0:hi - lo, b, f, :],
                             a[name][skip + lo * P:skip + hi * P].rearrange("(t e) -> t e", e=P)))
        t, rest = n // P, n % P
        if rest:
            srcs.append((idx[t % P:t % P + 1, t // P, f, 0:rest],
                         a[name][skip + t * P:skip + n].rearrange("(a e) -> a e", a=1)))
    loaded, filled, padded, converted = sig.dma(1, per=len(srcs)), sig.dma(1, per=2 if e.n_nodes % P else 1), sig.make(1, per=2), sig.make(1)
    turned = sig.make(1)
    whole = e.n_nodes // P
    with nc.Block() as block:
        @block.gpsimd
        def _(pool):
            nc.gpsimd.memset(fill[:, :], -1).then_inc(padded[0], 1)
            nc.gpsimd.memset(idx[:, :, 0, :], 0)
            nc.gpsimd.memset(idx[:, :, 1:3, :], e.n_nodes)
            nc.gpsimd.memset(idx[:, :, 3, :], 0).then_inc(padded[0], 1)
            nc.gpsimd.iota(slot_i[:, :], pattern=[[P, NTP]], base=0, channel_multiplier=1)

        @block.sync
        def _(sp):
            sp.wait_ge(padded[0], padded.at(0, 0, 1))
            for dst, src in srcs:
                sp.dma_start(dst, src).then_inc(loaded[0], 16)
            sp.dma_start(w.pos_dram[0:whole * P, :].rearrange("(p n) b -> p (n b)", p=P),
                         fill[:, 0:whole]).then_inc(filled[0], 16)
            rest = e.n_nodes - whole * P
            if rest:
                sp.dma_start(w.pos_dram[whole * P:e.n_nodes, :], fill[0:rest, 0:1]).then_inc(filled[0], 16)
            sp.wait_ge(filled[0], filled.at(0, 0, 1 if rest else 0))

        @block.vector
        def _(dve):
            dve.wait_ge(loaded[0], loaded.at(0, 0, len(srcs) - 1))
            nc.vector.tensor_copy(idx_f[:, :, :, :], idx[:, :, :, :]).then_inc(converted[0], 1)
            dve.wait_ge(turned[0], turned.at(0, 0))
            for f in range(4):
                nc.vector.tensor_copy(col[:, f, :], ps[:, f, 0:NTP])

        @block.tensor
        def _(pe):
            pe.wait_ge(converted[0], converted.at(0, 0))
            for f in range(4):
                for b in range(NB):
                    last = nc.tensor.transpose(ps[:, f, b * P:(b + 1) * P], idx_f[:, b, f, :], w.ident[:, :])
            last.then_inc(turned[0], 1)
    sig.end(1)

    ready, masked, lists = sig.make(1, per=2), sig.make(1), sig.make(1)
    written = sig.dma(1, per=5 * NB + 1)
    read = sig.dma(1, per=1 + 3 * NS)
    listed = sig.dma(1, per=2)
    with nc.Block() as block:
        @block.vector
        def _(dve):
            nc.vector.tensor_tensor(tmp[:, 0, :], col[:, 1, :], col[:, 2, :], ALU.is_equal).then_inc(ready[0], 1)
            dve.wait_ge(ready[0], ready.at(0, 0, 0))
            nc.vector.scalar_tensor_tensor(tmp[:, 1, :], tmp[:, 0, :], BIG, col[:, 1, :], ALU.mult,
                                           ALU.add).then_inc(ready[0], 1)
            nc.vector.tensor_copy(w.dst_col[:, :], col[:, 1, :])
            for r in range(RELS):
                nc.vector.tensor_scalar(w.is_rel[:, r, :], col[:, 3, :], float(r), None, ALU.is_equal)
            nc.vector.tensor_copy(ints[:, 0, :], col[:, 0, :])
            nc.vector.tensor_scalar(ints[:, 1, :], col[:, 1, :], float(e.n_nodes - 1), None, ALU.min)
            dve.wait_ge(ready[0], ready.at(0, 0, 1))
            nc.vector.tensor_copy(ints[:, 2, :], tmp[:, 1, :]).then_inc(lists[0], 1)
            nc.vector.tensor_copy(slot[:, :], slot_i[:, :])
            for b in range(NB):
                for s, at in ((0, 0), (1, P - 1)):
                    last = nc.vector.tensor_scalar(masks[:, b, s, :], idx_f[:, b, 1, :], idx_f[:, b, 1, at:at + 1],
                                                   None, ALU.is_equal)
            last.then_inc(masked[0], 1)

        @block.sync
        def _(sp):
            for b in range(NB):
                sp.dma_start(w.dst_dram[b * P * P:(b + 1) * P * P].rearrange("(t e) -> t e", e=P),
                             idx_f[:, b, 1, :]).then_inc(written[0], 16)
                for s, at in ((0, 0), (1, P - 1)):
                    sp.dma_start(w.ends_dram[s, b * P:(b + 1) * P].rearrange("(t a) -> t a", a=1),
                                 idx_f[:, b, 1, at:at + 1]).then_inc(written[0], 16)
            sp.wait_ge(masked[0], masked.at(0, 0))
            for b in range(NB):
                rows = e.block_rows[b]
                for s in range(2):
                    sp.dma_start(w.masks_dram[s, b * P * P:b * P * P + rows * P].rearrange("(t e) -> t e", e=P),
                                 masks[0:rows, b, s, :]).then_inc(written[0], 16)
            sp.wait_ge(lists[0], lists.at(0, 0))
            sp.dma_start(w.lists_dram[0].rearrange("c p j -> p c j"),
                         ints[:, 0, 0:NT].rearrange("p (c j) -> p c j", j=T)).then_inc(written[0], 16)
            sp.wait_ge(written[0], written.at(0, 0, 5 * NB))
            for f in (1, 2):
                sp.dma_start(w.lists_dram[f].rearrange("c p j -> p c j"),
                             ints[:, f, 0:NT].rearrange("p (c j) -> p c j", j=T)).then_inc(listed[0], 16)
            sp.dma_start(ends[:, :, :], dram_ap(w.ends_dram, 0, [[0, P], [NTP, 2], [1, NTP]])).then_inc(read[0], 16)
            for s, own in enumerate((own_first, own_last)):
                for i in range(NS):
                    sp.dma_start(own[:, i:i + 1], dram_ap(w.ends_dram, s * NTP + i * (P // HEADS),
                                                          [[1, P // HEADS], [0, HEADS], [1, 1]])).then_inc(read[0], 16)
            for s in range(NS):
                sp.dma_start(dst_scores[:, s, :], dram_ap(w.dst_dram, s * P // HEADS * P,
                                                          [[P, P // HEADS], [0, HEADS], [1, P]])).then_inc(read[0], 16)
            sp.wait_ge(read[0], read.at(0, 0, 3 * NS))
            sp.wait_ge(listed[0], listed.at(0, 0, 1))
    sig.end(1)

    compared, cut = sig.make(1), sig.make(1)
    with nc.Block() as block:
        @block.vector
        def _(dve):
            for b in range(NB):
                nc.vector.tensor_scalar(w.carry_eq[:, 0, b, :], ends[:, 0, :], idx_f[:, b, 1, P - 1:P], None,
                                        ALU.is_equal)
                nc.vector.tensor_scalar(w.carry_eq[:, 1, b, :], ends[:, 1, :], idx_f[:, b, 1, 0:1], None, ALU.is_equal)
            for s in range(NS):
                nc.vector.tensor_scalar(w.carry_pen[:, 0, s, :], ends[:, 1, 0:NTS], own_first[:, s:s + 1], None,
                                        ALU.is_equal)
                last = nc.vector.tensor_scalar(w.carry_pen[:, 1, s, :], ends[:, 0, 0:NTS], own_last[:, s:s + 1], None,
                                               ALU.is_equal)
            nc.vector.tensor_tensor(w.step_pen[:, :, 1:P], dst_scores[:, :, 0:P - 1], dst_scores[:, :, 1:P],
                                    ALU.is_equal)
            for s in range(NS):
                nc.vector.tensor_scalar(w.end_pen[:, 0, s, :], dst_scores[:, s, :], dst_scores[:, s, 0:1], None,
                                        ALU.is_equal)
                last = nc.vector.tensor_scalar(w.end_pen[:, 1, s, :], dst_scores[:, s, :], dst_scores[:, s, P - 1:P],
                                               None, ALU.is_equal)
            last.then_inc(compared[0], 1)
            dve.wait_ge(compared[0], compared.at(0, 0))
            for pen in (w.step_pen[:, :, 1:P], w.end_pen[:, :, :, :].rearrange("p a s e -> p (a s e)")):
                nc.vector.tensor_scalar(pen, pen, 1.0, FAR, ALU.subtract, ALU.mult)
            nc.vector.memset(w.step_pen[:, :, 0:1], -FAR)
            nc.vector.memset(w.step_pen[:, :, P:P + 1], -FAR)
            dve.wait_ge(cut[0], cut.at(0, 0))
            pen = w.carry_pen[:, :, :, :].rearrange("p a s t -> p (a s t)")
            nc.vector.tensor_scalar(pen, pen, 1.0, FAR, ALU.subtract, ALU.mult)

        @block.gpsimd
        def _(pool):
            pool.wait_ge(compared[0], compared.at(0, 0))
            for b in range(NB):
                for s, sign in ((0, 1), (1, -1)):
                    m = w.carry_eq[:, s, b, :]
                    nc.gpsimd.affine_select(out=m, in_=m, compare_op=ALU.is_gt, fill=0.0, base=-sign * b * P,
                                            pattern=[[sign, NTP]], channel_multiplier=-sign)
            for s in range(NS):
                m = w.carry_pen[:, 0, s, :]
                nc.gpsimd.affine_select(out=m, in_=m, compare_op=ALU.is_ge, fill=0.0, base=P * s - HEADS,
                                        pattern=[[-HEADS, NTS]], channel_multiplier=1)
                m = w.carry_pen[:, 1, s, :]
                last = nc.gpsimd.affine_select(out=m, in_=m, compare_op=ALU.is_gt, fill=0.0, base=-P * s,
                                               pattern=[[HEADS, NTS]], channel_multiplier=-1)
            last.then_inc(cut[0], 1)
    sig.end(1)

    scattered, found = sig.gather(1, per=NT), sig.gather(1, per=NT)
    held = sig.keep()

    def positions(pool, parts):
        share = -(-2 * NT // parts)
        for t in range(NT):
            nc.gpsimd.indirect_dma_start(
                w.pos_dram[:, :], bass.IndirectOffsetOnAxis(ap=ints[:, 2, t:t + 1], axis=0),
                slot_i[:, t:t + 1], None, bounds_check=e.n_nodes - 1, oob_is_err=False).then_inc(scattered[0], 16)
            if t % share == share - 1:
                yield
        pool.wait_ge(scattered[0], scattered.at(0, 0, NT - 1))
        for t in range(NT):
            nc.gpsimd.indirect_dma_start(
                pos[:, t:t + 1], None, w.pos_dram[:, :],
                bass.IndirectOffsetOnAxis(ap=ints[:, 0, t:t + 1], axis=0)).then_inc(found[0], 16)
            if t % share == share - 1:
                yield
        pool.wait_ge(found[0], found.at(0, 0, NT - 1))

    dense(positions)
    sig.lent = held
    sig.end(1)

    step = sig.make(1, per=4)
    stored = sig.dma(1)
    with nc.Block() as block:
        @block.vector
        def _(dve):
            p, q, n = pos_f[:, 0, 0:NT], pos_f[:, 1, 0:NT], slot[:, 0:NT]
            nc.vector.tensor_copy(p, pos[:, 0:NT]).then_inc(step[0], 1)
            dve.wait_ge(step[0], step.at(0, 0, 0))
            nc.vector.tensor_scalar(q, p, 0.0, None, ALU.is_ge)
            nc.vector.scalar_tensor_tensor(p, p, float(e.rows), n, ALU.add, ALU.subtract).then_inc(step[0], 1)
            dve.wait_ge(step[0], step.at(0, 0, 1))
            nc.vector.tensor_tensor(p, p, q, ALU.mult).then_inc(step[0], 1)
            dve.wait_ge(step[0], step.at(0, 0, 2))
            nc.vector.tensor_tensor(ints[:, 0, 0:NT], p, n, ALU.add).then_inc(step[0], 1)

        @block.sync
        def _(sp):
            sp.wait_ge(step[0], step.at(0, 0, 3))
            sp.dma_start(w.lists_dram[3].rearrange("c p j -> p c j"),
                         ints[:, 0, 0:NT].rearrange("p (c j) -> p c j", j=T)).then_inc(stored[0], 16)
            sp.wait_ge(stored[0], stored.at(0, 0))
    sig.end(1)


LT = 2
LROWS = P * LT


def weave(*lines):
    at = [[next(line, None), line] for line in lines]
    at = [head for head in at if head[0] is not None]
    while at:
        head = min(at, key=lambda h: h[0])
        step = next(head[1], None)
        if step is None:
            at.remove(head)
        else:
            head[0] = step


TABLE = {
    "alone": (2, 3, 3.5, 4, 5, 6, 6.2, 6.5, 7, 8, 3.9, 4.1,
        1, 2, 3.5, 5, 6, 6.5, 8.5, 9, 10,
        2.1, 2.3, 3.5, 4, 5, 6, 7, 8, 9, 6, 9),
    "scores0": (4, 5, 6, 7, 8, 9, 10, 11, 12, 13, 4.5, 7,
        0.2, 2, 4, 6, 7, 8, 8.4, 10, 11,
        0.6, 0.8, 2, 2.5, 3.5, 4.5, 4.9, 6.5, 7.5, 6.4, 8),
    "scores1": (4, 5.6, 6, 7, 8, 9, 10, 11, 12, 13, 5, 8.8,
        1, 2, 4, 6, 7, 8, 9, 10.3, 11,
        2.1, 2.3, 3.7, 4, 4.2, 6, 7, 8, 9, 4.2, 4.3),
    "scores2": (3.4, 4.2, 5.4, 6.4, 7.4, 8.4, 8.5, 9.8, 11.4, 12.4, 5.8, 6.4,
        1.5, 2, 4, 5.5, 7.6, 8.2, 9, 11, 12.5,
        0.4, 0.6, 1.5, 2.2, 3.3, 4.8, 5.3, 6.3, 7.1, 5.2, 8),
    "sums": (2.5, 4.7, 4.8, 7, 7.5, 9, 10, 11, 11.3, 14.1, 5.2, 7,
        1.1, 2, 4, 5.5, 7, 8, 9, 10, 11,
        1.3, 1.5, 2.7, 3.2, 4.2, 5.2, 5.7, 7.1, 8.2, 6.7, 9.5),
    "finish0": (2.3, 3, 3.5, 4, 5, 6, 6.2, 6.5, 7, 8, 3.9, 4.1,
        1, 2, 3.5, 5, 6, 6.5, 8.5, 9, 10,
        2.1, 2.3, 3.5, 4, 5, 6, 7, 8, 9, 5.2, 5.3),
    "finish1": (2, 3, 3.5, 4, 5.4, 6, 6.2, 6.5, 7, 8, 3.9, 4.1,
        1, 2, 3.5, 5, 6, 6.5, 8.5, 9, 10,
        2.1, 2.3, 3.5, 4, 5, 6, 7, 8, 9, 5.2, 5.3),
    "finish2": (2, 3.1, 3.5, 4, 5, 6, 6.2, 6.5, 7, 8, 3.9, 4.1,
        0.2, 3, 3.5, 5, 5.6, 6.5, 8.5, 9, 12.3,
        2.1, 2.3, 3.5, 4, 5, 6, 7, 8, 9, 5.2, 8),
    "sage_messages": (4, 5, 6, 7, 8, 9, 10, 11, 12.7, 13, 4.2, 7,
        1, 2, 4, 6, 7, 8, 9, 10, 11,
        1.7, 1.9, 2.8, 3.6, 4.6, 5.6, 6.6, 6.7, 8.6, 5.2, 8),
    "sage_update": (4, 5, 6, 7, 8, 9, 10, 11, 12, 13, 5, 7,
        1, 2, 4, 6, 7, 8, 9, 10, 11,
        2.1, 2.3, 3.5, 4.6, 5, 6, 7, 7.6, 9, 5.2, 5.3),
    "rel_messages": (4, 6.3, 8, 8.5, 10, 10.5, 11.5, 12.3, 13.5, 14.5, 6.5, 9.3,
        0.2, 2, 2.6, 6, 7, 8, 9, 11.3, 12.4,
        0.2, 2.2, 2.7, 3.3, 4.2, 5.2, 6.2, 8, 9.4, 5.2, 7.3),
    "rel_update": (4, 5, 6, 7, 8, 8.8, 9, 11, 12, 16, 5, 5.3,
        1.2, 2.2, 4.2, 6.2, 7.2, 8.2, 9.2, 9.4, 11.2,
        0.2, 0.7, 1.9, 2.4, 3.4, 3.5, 5.4, 6.4, 9.6, 6.2, 9.6),
    "att_messages": (3.6, 4.6, 5, 6.6, 7.6, 8.6, 9.6, 10.6, 11.6, 12.7, 5.9, 6.6,
        1, 2, 5.2, 6.6, 7, 8, 9, 10.4, 11,
        1.4, 1.6, 2.8, 3.3, 4.3, 5.3, 6.3, 7.3, 8.3, 7.3, 8),
}


class Steps:

    def __init__(self, name):
        (self.front_turn, self.front_copy, self.layer0, self.exp0, self.elu0, self.layer1, self.exp1, self.elu1,
         self.layer2, self.exp2, self.keep, self.load,
         self.residual, self.power0, self.norm0, self.middle_turn, self.middle_copy, self.sage, self.moments1,
         self.power1, self.norm1,
         self.back_turn, self.back_copy, self.rel, self.relu, self.power2, self.bo, self.power3, self.norm3,
         self.store, self.fetch0, self.fetch1) = TABLE[name]


class DenseLine:

    def __init__(self, nc, a, w, ps, sig, sb, out, groups):
        self.nc, self.w, self.groups, self.i, self.at = nc, w, groups, 0, Steps("alone")
        self.x = a["x"][0:groups * LROWS, :].rearrange("(g p j) f -> g p (j f)", p=P, j=LT)
        self.out = out[0:groups * LROWS, :].rearrange("(g p j) f -> g p (j f)", p=P, j=LT)
        self.bank, self.bank2 = ps[:, 6, 0:LROWS], ps[:, 7, 0:LROWS]
        self.X, self.E, self.R, self.Y = (sb(f"front_{n}", [P, LROWS]) for n in ("x", "e", "r", "y"))
        self.XT2, self.R2, self.Y2 = (sb(f"back_{n}", [P, LROWS]) for n in ("xt", "r", "y"))
        self.stats, self.moments, self.scale, self.spare = (
            [sb(f"{half}_{n}", [P, *shape]) for half in ("front", "back")]
            for n, shape in (("stats", (LT, 6)), ("moments", (LT, 2)), ("scale", (LT,)), ("spare", (1,))))

        def one(per=1):
            return sig.make(1, per=per)

        self.loaded, self.stored = sig.dma(1), sig.dma(1)
        self.products, self.copied, self.exped, self.kept = one(4), one(), one(3), one()
        self.elued, self.relued, self.summed = one(2), one(), one()
        self.tallied, self.aggregated, self.powered, self.scaled, self.normed = (one() for _ in range(5))
        self.products2, self.copied2, self.summed2 = one(4), one(2), one()
        self.tallied2, self.aggregated2, self.powered2, self.scaled2, self.normed2 = (one(3) for _ in range(5))
        sig.keep()

    def tile(self, j):
        return slice(j * D, (j + 1) * D)

    def load(self, sp, g):
        sp.dma_start(self.X[:, :], self.x[g]).then_inc(self.loaded[0], 16)

    def store(self, sp, g):
        sp.wait_ge(self.normed2[0], self.normed2.at(0, g, 2))
        settle(sp, self.w)
        sp.dma_start(self.out[g], self.Y2[:, :]).then_inc(self.stored[0], 16)


    def sync_front(self, sp, i):
        if not isinstance(i, int) or i < self.groups - 1:
            yield self.at.load
            sp.wait_ge(self.kept[0], self.kept.at(0, i))
            settle(sp, self.w)
            self.load(sp, i + 1)

    def sync_back(self, sp, g):
        yield self.at.store
        self.store(sp, g)


    def turn(self, dst, src, done):
        for j in range(LT):
            last = self.nc.tensor.transpose(dst[:, self.tile(j)], src[:, self.tile(j)], self.w.ident[:, :])
        last.then_inc(done, 1)

    def rows_out(self, dst, rows_t, row, weight, done):
        w = self.w
        self.nc.tensor.matmul(dst, w.ones4[0:3, 0:P], w.bias3[0:3, row, 0:D].unsqueeze(1).broadcast_to([3, LT, D]),
                              start=True, stop=False)
        for j in range(LT):
            last = self.nc.tensor.matmul(dst[:, self.tile(j)], rows_t[:, self.tile(j)], weight, start=False,
                                         stop=j == LT - 1)
        last.then_inc(done, 1)

    def tensor_front(self, pe, i):
        nc, w, bank = self.nc, self.w, self.bank
        yield self.at.front_turn
        pe.wait_ge(self.loaded[0], self.loaded.at(0, i))
        if not first(i):
            pe.wait_ge(self.summed[0], self.summed.before(0, i))
        self.turn(bank, self.X, self.products[0])
        yield self.at.layer0
        pe.wait_ge(self.copied[0], self.copied.at(0, i))
        nc.tensor.matmul(bank, w.bias3[0:4, B_GAT_SHIFTED[0], 0:D], w.ones4[:, 0:LROWS], start=True, stop=False)
        nc.tensor.matmul(bank, w.gat[:, 0, 0:D], self.E[:, :], start=False, stop=True).then_inc(self.products[0], 1)
        yield self.at.layer1
        pe.wait_ge(self.elued[0], self.elued.at(0, i, 0))
        nc.tensor.matmul(bank, w.bias3[0:4, B_GAT_SHIFTED[1], 0:D], w.ones4[:, 0:LROWS], start=True, stop=False)
        nc.tensor.matmul(bank, w.gat[:, 1, 0:D], self.E[:, :], start=False, stop=True).then_inc(self.products[0], 1)
        yield self.at.layer2
        pe.wait_ge(self.elued[0], self.elued.at(0, i, 1))
        self.rows_out(bank, self.E, B_GAT_SHIFTED[2], w.gat[:, 2, 0:D], self.products[0])

    def tensor_middle(self, pe, g):
        yield self.at.middle_turn
        pe.wait_ge(self.normed[0], self.normed.at(0, g))
        if not first(g):
            pe.wait_ge(self.summed2[0], self.summed2.before(0, g))
        self.turn(self.bank2, self.Y, self.products2[0])
        yield self.at.sage
        pe.wait_ge(self.copied2[0], self.copied2.at(0, g, 0))
        self.rows_out(self.bank2, self.XT2, B_SAGE, self.w.sage_own[:, :], self.products2[0])

    def tensor_back(self, pe, g):
        yield self.at.back_turn
        pe.wait_ge(self.normed2[0], self.normed2.at(0, g, 0))
        self.turn(self.bank2, self.R2, self.products2[0])
        yield self.at.rel
        pe.wait_ge(self.copied2[0], self.copied2.at(0, g, 1))
        self.rows_out(self.bank2, self.XT2, B_REL, self.w.self_loop[:, :], self.products2[0])


    def scalar_front(self, act, i):
        nc, w, bank, E = self.nc, self.w, self.bank, self.E
        yield self.at.front_copy
        act.wait_ge(self.products[0], self.products.at(0, i, 0))
        nc.scalar.activation(E[:, :], bank, ACT.Copy).then_inc(self.copied[0], 1)
        yield self.at.keep
        if not first(i):
            act.wait_ge(self.normed[0], self.normed.before(0, i))
        nc.scalar.activation(self.R[:, :], self.X[:, :], ACT.Copy).then_inc(self.kept[0], 1)
        for n, step in enumerate((self.at.exp0, self.at.exp1, self.at.exp2)):
            yield step
            act.wait_ge(self.products[0], self.products.at(0, i, n + 1))
            if n < 2:
                nc.scalar.activation(E[:, :], bank, ACT.Exp, bias=w.minus1[:, :]).then_inc(self.exped[0], 1)
            else:
                nc.scalar.activation(E[:, :], bank, ACT.Exp).then_inc(self.exped[0], 1)

    def copy_back(self, act, g, product):
        act.wait_ge(self.products2[0], self.products2.at(0, g, product))
        self.nc.scalar.activation(self.XT2[:, :], self.bank2, ACT.Copy).then_inc(self.copied2[0], 1)

    def scalar_middle(self, act, g):
        yield self.at.middle_copy
        self.copy_back(act, g, 0)

    def scalar_back(self, act, g):
        yield self.at.back_copy
        self.copy_back(act, g, 2)


    def power(self, pool, half, g, n, summed, powered, ready):
        nc, w, scale = self.nc, self.w, self.scale[half]
        pool.wait_ge(summed[0], summed.at(0, g, n))
        nc.gpsimd.tensor_tensor(scale[:, :], self.moments[half][:, :, 1], w.eps[:, 0:LT], ALU.add).then_inc(powered[0], 1)
        pool.wait_ge(powered[0], powered.at(0, g, n))
        nc.gpsimd.tensor_tensor(scale[:, :], scale[:, :], w.power[:, 0:LT], ALU.pow).then_inc(ready[0], 1)

    def gpsimd_middle(self, pool, g):
        yield self.at.power0
        self.power(pool, 0, g, 0, self.aggregated, self.powered, self.scaled)
        yield self.at.power1
        self.power(pool, 1, g, 0, self.aggregated2, self.powered2, self.scaled2)

    def gpsimd_back(self, pool, g):
        for n, step in ((1, self.at.power2), (2, self.at.power3)):
            yield step
            self.power(pool, 1, g, n, self.aggregated2, self.powered2, self.scaled2)


    def row_moments(self, dve, half, src, g, n, tallied, aggregated):
        nc, stats = self.nc, self.stats[half]
        for j in range(LT):
            last = nc.vector.bn_stats(stats[:, j, :], src[:, self.tile(j)])
        last.then_inc(tallied[0], 1)
        dve.wait_ge(tallied[0], tallied.at(0, g, n))
        nc.vector.memset(self.spare[half][:, :], 0.0)
        for j in range(LT):
            last = nc.vector.bn_aggr(self.moments[half][:, j, :], stats[:, j, :])
        last.then_inc(aggregated[0], 1)

    def normalise(self, half, dst, src, normed):
        for j in range(LT):
            last = self.nc.vector.tensor_scalar(dst[:, self.tile(j)], src[:, self.tile(j)],
                                                self.moments[half][:, j, 0:1], self.scale[half][:, j:j + 1],
                                                ALU.subtract, ALU.mult)
        last.then_inc(normed[0], 1)

    def vector_front(self, dve, i):
        nc, E = self.nc, self.E
        for l, step in enumerate((self.at.elu0, self.at.elu1)):
            yield step
            dve.wait_ge(self.exped[0], self.exped.at(0, i, l))
            nc.vector.scalar_tensor_tensor(E[:, :], E[:, :], 1.0, self.bank, ALU.min, ALU.max).then_inc(self.elued[0], 1)

    def vector_middle(self, dve, g):
        nc, E, R = self.nc, self.E, self.R
        yield self.at.residual
        dve.wait_ge(self.exped[0], self.exped.at(0, g, 2))
        dve.wait_ge(self.kept[0], self.kept.at(0, g))
        nc.vector.scalar_tensor_tensor(R[:, :], self.bank, 0.0, R[:, :], ALU.max, ALU.add).then_inc(self.relued[0], 1)
        dve.wait_ge(self.relued[0], self.relued.at(0, g))
        nc.vector.scalar_tensor_tensor(R[:, :], E[:, :], 1.0, R[:, :], ALU.min, ALU.add).then_inc(self.summed[0], 1)
        dve.wait_ge(self.summed[0], self.summed.at(0, g))
        self.row_moments(dve, 0, R, g, 0, self.tallied, self.aggregated)
        yield self.at.norm0
        dve.wait_ge(self.scaled[0], self.scaled.at(0, g))
        if not first(g):
            dve.wait_ge(self.products2[0], self.products2.at(0, g - 1, 0))
        self.normalise(0, self.Y, R, self.normed)
        yield self.at.moments1
        dve.wait_ge(self.products2[0], self.products2.at(0, g, 1))
        if not first(g):
            dve.wait_ge(self.normed2[0], self.normed2.before(0, g))
        self.row_moments(dve, 1, self.bank2, g, 0, self.tallied2, self.aggregated2)
        yield self.at.norm1
        dve.wait_ge(self.scaled2[0], self.scaled2.at(0, g, 0))
        self.normalise(1, self.R2, self.bank2, self.normed2)

    def vector_back(self, dve, g):
        nc, bank, R, Y = self.nc, self.bank2, self.R2, self.Y2
        yield self.at.relu
        dve.wait_ge(self.products2[0], self.products2.at(0, g, 3))
        dve.wait_ge(self.normed2[0], self.normed2.at(0, g, 0))
        if not first(g):
            dve.wait_ge(self.stored[0], self.stored.before(0, g))
        nc.vector.scalar_tensor_tensor(Y[:, :], bank, 0.0, R[:, :], ALU.max, ALU.add).then_inc(self.summed2[0], 1)
        dve.wait_ge(self.summed2[0], self.summed2.at(0, g))
        self.row_moments(dve, 1, Y, g, 1, self.tallied2, self.aggregated2)
        yield self.at.bo
        dve.wait_ge(self.scaled2[0], self.scaled2.at(0, g, 1))
        for j in range(LT):
            last = nc.vector.scalar_tensor_tensor(R[:, self.tile(j)], Y[:, self.tile(j)], self.scale[1][:, j:j + 1],
                                                  self.w.bo_rows[:, :], ALU.mult, ALU.add)
        last.then_inc(self.normed2[0], 1)
        dve.wait_ge(self.normed2[0], self.normed2.at(0, g, 1))
        self.row_moments(dve, 1, R, g, 2, self.tallied2, self.aggregated2)
        yield self.at.norm3
        dve.wait_ge(self.scaled2[0], self.scaled2.at(0, g, 2))
        self.normalise(1, Y, R, self.normed2)


    def lines(self, eng, kind, i):
        front, middle, back = {
            "sync": (self.sync_front, None, self.sync_back),
            "tensor": (self.tensor_front, self.tensor_middle, self.tensor_back),
            "scalar": (self.scalar_front, self.scalar_middle, self.scalar_back),
            "gpsimd": (None, self.gpsimd_middle, self.gpsimd_back),
            "vector": (self.vector_front, self.vector_middle, self.vector_back)}[kind]
        lines = []
        for part, lag in ((front, 0), (middle, 1), (back, 2)):
            if part is not None and (not isinstance(i, int) or lag <= i < self.groups + lag):
                lines.append(part(eng, i - lag if lag else i))
        return lines

    def beside(self, eng, kind, n, steps=None, tail=0, norms=None):
        for u in iterations(eng, n, tail, head=3 if self.i == 0 else 2 if norms else 1):
            own = [] if steps is None else [steps(u)]
            if norms and not first(u):
                own.append(norms(u - 1))
            weave(*own, *(self.lines(eng, kind, u + self.i) if self.i + n <= self.groups else ()))
        if norms:
            weave(norms(n - 1))

    def start(self, nc):
        with nc.Block() as block:
            @block.sync
            def _(sp):
                self.load(sp, 0)

    def finish(self, nc):
        with nc.Block() as block:
            @block.tensor
            def _(pe):
                for i in (self.groups, self.groups + 1):
                    weave(*self.lines(pe, "tensor", i))

            @block.scalar
            def _(act):
                for i in (self.groups, self.groups + 1):
                    weave(*self.lines(act, "scalar", i))

            @block.gpsimd
            def _(pool):
                for i in (self.groups, self.groups + 1):
                    weave(*self.lines(pool, "gpsimd", i))

            @block.vector
            def _(dve):
                for i in (self.groups, self.groups + 1):
                    weave(*self.lines(dve, "vector", i))

            @block.sync
            def _(sp):
                for i in (self.groups, self.groups + 1):
                    weave(*self.lines(sp, "sync", i))
                sp.wait_ge(self.stored[0], self.stored.at(0, self.groups - 1))


def ln_stats(nc, k, stats, src, tallied):
    for j in range(T):
        last = nc.vector.bn_stats(stats[:, k, j, :], src[:, j, :])
    last.then_inc(tallied[k], 1)


def ln_moments(nc, dve, k, u, b, tallied, aggregated):
    dve.wait_ge(tallied[k], tallied.at(k, u))
    nc.vector.memset(b.spare[:, k:k + 1], 0.0)
    for j in range(T):
        last = nc.vector.bn_aggr(b.moments[:, k, j, :], b.stats[:, k, j, :])
    last.then_inc(aggregated[k], 1)


def ln_apply(nc, dve, k, u, b, dst, src, scaled, normed):
    dve.wait_ge(scaled[k], scaled.at(k, u))
    for j in range(T):
        last = nc.vector.tensor_scalar(dst[:, j, :], src[:, j, :], b.moments[:, k, j, 0:1],
                                       b.scale[:, k, j:j + 1], ALU.subtract, ALU.mult)
    last.then_inc(normed[k], 1)


class Strands:

    def __init__(self, nc, sig, ctx, ps):
        sb = sig.buffers(ctx)
        K = STRANDS
        self.index = sb("chunk_index", [P, K, 2, T], I32)
        self.src = sb("chunk_src", [P, K, T, WIDE])
        self.own = sb("chunk_own", [P, K, T, D])
        self.src_t = sb("chunk_src_t", [P, K, ROWS])
        self.own_t = sb("chunk_own_t", [P, K, ROWS])
        self.e = sb("chunk_e", [P, K, T, D])
        self.new = sb("chunk_new", [P, K, T, D])
        self.v = sb("chunk_v", [P, K, T, WIDE])
        self.same = sb("chunk_same", [P, K, ROWS])
        self.mask = sb("chunk_mask", [2, K, ROWS])
        self.carry = sb("chunk_carry", [2, K, T, WIDE])
        self.stats = sb("chunk_stats", [P, K, T, 6])
        self.moments = sb("chunk_moments", [P, K, T, 2])
        self.scale = sb("chunk_scale", [P, K, T])
        self.small = sb("chunk_small", [P, K, 3, T, 2 * HEADS])
        self.spare = sb("chunk_spare", [P, K])
        self.ps = ps

    def one(self, k):
        return self.ps[:, 3 * k, :]

    def wide(self, k, width):
        return self.ps[:, 3 * k + 1:3 * k + 3, :].rearrange("p b (j f) -> p (b j) f", j=2)[:, :, 0:width]

    def tiles(self, bank):
        return bank.rearrange("p (j f) -> p j f", j=T)


def settle(eng, w):
    eng.sem_inc(w.settled, 1)


def turn(nc, w, dst, src, done):
    for j in range(T):
        last = nc.tensor.transpose(dst[:, j * P:(j + 1) * P], src[:, j, 0:D], w.ident[:, :])
    last.then_inc(done, 1)


def bias_rows(nc, w, dst, row, width=D, tiles=T, stop=False):
    nc.tensor.matmul(dst, w.ones4[0:3, 0:P], w.bias3[0:3, row, 0:width].unsqueeze(1).broadcast_to([3, tiles, width]),
                     start=True, stop=stop)


def gather(nc, rows, table, index, done):
    for j in range(T):
        nc.gpsimd.indirect_dma_start(rows[:, j, 0:D], None, table,
                                     bass.IndirectOffsetOnAxis(ap=index[:, j:j + 1], axis=0)).then_inc(done, 16)


def gat_scores(nc, a, w, e, b, ps, sig, l, old, new):
    K = range(STRANDS)
    n = e.rounds
    gathered = sig.gather(per=T)
    own_in, index_in = sig.gather(per=T) if l == 0 else sig.dma(), sig.dma(per=2 if l == 0 else 1)
    rest_in, stored, kept = sig.dma(), sig.dma(), sig.dma(per=2)
    turned, own_turned, copied, own_copied, projected, scored, exped, lowered, elued = (
        sig.make() for _ in range(9))
    own_kept, h_kept = sig.make(), sig.make()
    summed, tallied, aggregated, powered, scaled, normed = (sig.make() for _ in range(6))
    last_step = normed if l == 2 else elued
    if l != 2:
        sig.idle(rest_in, summed, tallied, aggregated, powered, scaled, normed)
    if l != 0:
        sig.idle(kept)
    old_rows = old.rearrange("(c j p) f -> c p j f", j=T, p=P)
    new_rows = new.rearrange("(c j p) f -> c p j f", j=T, p=P)
    first_rows = w.tables[0].rearrange("(c j p) f -> c p j f", j=T, p=P)

    def load_index(sp, k, u, prev):
        c = u * STRANDS + k
        if prev is not None:
            sp.wait_ge(gathered[k], gathered.at(k, prev, T - 1))
            settle(sp, w)
            if l == 0:
                sp.wait_ge(own_in[k], own_in.at(k, prev, T - 1))
                settle(sp, w)
        if l == 0:
            sp.dma_start(b.index[:, k, 0, :], w.lists_dram[0, c]).then_inc(index_in[k], 16)
            sp.dma_start(b.index[:, k, 1, :], w.lists_dram[1, c]).then_inc(index_in[k], 16)
        else:
            sp.dma_start(b.index[:, k, 0, :], w.lists_dram[3, c]).then_inc(index_in[k], 16)

    def load_own(sp, k, u, prev):
        if prev is not None:
            sp.wait_ge(own_turned[k], own_turned.at(k, prev))
            settle(sp, w)
        sp.dma_start(b.own[:, k], old_rows[e.chunks + u * STRANDS + k]).then_inc(own_in[k], 16)

    def load_rest(sp, k, u, prev):
        if prev is not None:
            sp.wait_ge(summed[k], summed.at(k, prev))
            settle(sp, w)
        sp.dma_start(b.v[:, k, :, 0:D], first_rows[u * STRANDS + k]).then_inc(rest_in[k], 16)

    def fetch(pool, k, u, prev):
        if prev is not None:
            pool.wait_ge(turned[k], turned.at(k, prev))
            if l == 0:
                pool.wait_ge(own_turned[k], own_turned.at(k, prev))
                pool.wait_ge(kept[k], kept.at(k, prev, 1))
        pool.wait_ge(index_in[k], index_in.at(k, u, 1 if l == 0 else 0))
        pool.wait_ge(w.ready, w.ready_count)
        settle(pool, w)
        if l == 0:
            gather(nc, b.src[:, k], a["x"], b.index[:, k, 0, :], gathered[k])
            gather(nc, b.own[:, k], a["x"], b.index[:, k, 1, :], own_in[k])
        else:
            gather(nc, b.src[:, k], old, b.index[:, k, 0, :], gathered[k])

    with nc.Block() as block:
        @block.sync
        def _(sp):
            for k in K:
                load_index(sp, k, 0, None)
                if l != 0:
                    load_own(sp, k, 0, None)
                if l == 2:
                    load_rest(sp, k, 0, None)
            def steps(u):
                more = not isinstance(u, int) or u < n - 1
                yield 0.8
                for k in K:
                    if more:
                        load_index(sp, k, u + 1, u)
                if l == 0:
                    yield 2
                    for k in K:
                        c = u * STRANDS + k
                        sp.wait_ge(gathered[k], gathered.at(k, u, T - 1))
                        sp.dma_start(first_rows[c], b.src[:, k, :, 0:D]).then_inc(kept[k], 16)
                        sp.wait_ge(own_in[k], own_in.at(k, u, T - 1))
                        sp.dma_start(first_rows[e.chunks + c], b.own[:, k]).then_inc(kept[k], 16)
                else:
                    yield 4
                    for k in K:
                        if more:
                            load_own(sp, k, u + 1, u)
                if l == 2:
                    yield 9
                    for k in K:
                        if not isinstance(u, int) or u < n - 1:
                            load_rest(sp, k, u + 1, u)
                if l != 2:
                    yield 12
                    store(sp, u)

            def store(sp, u):
                for k in K:
                    sp.wait_ge(last_step[k], last_step.at(k, u))
                    sp.dma_start(new_rows[u * STRANDS + k], b.new[:, k]).then_inc(stored[k], 16)

            def norms(u):
                yield 4.3
                store(sp, u)

            w.line.beside(sp, "sync", n, steps, 1, norms if l == 2 else None)
            for k in K:
                sp.wait_ge(stored[k], stored.at(k, n - 1))
                if l == 0:
                    sp.wait_ge(kept[k], kept.at(k, n - 1, 1))

        @block.gpsimd
        def _(pool):
            for k in K:
                fetch(pool, k, 0, None)
            def steps(u):
                yield w.line.at.fetch0
                if not isinstance(u, int) or u < n - 1:
                    fetch(pool, 0, u + 1, u)
                yield w.line.at.fetch1
                if not isinstance(u, int) or u < n - 1:
                    fetch(pool, 1, u + 1, u)

            def norms(u):
                yield 0.9
                for k in K:
                    layer_norm_scale(nc, pool, w, b.moments, b.scale, k, u, 0, aggregated, powered, scaled)

            w.line.beside(pool, "gpsimd", n, steps, 1, norms if l == 2 else None)

        @block.tensor
        def _(pe):
            def steps(u):
                yield 1
                for k in K:
                    pe.wait_ge(gathered[k], gathered.at(k, u, T - 1))
                    if not first(u):
                        pe.wait_ge(own_kept[k], own_kept.before(k, u))
                    turn(nc, w, b.one(k), b.src[:, k], turned[k])
                yield 3
                for k in K:
                    pe.wait_ge(copied[k], copied.at(k, u))
                    if not first(u):
                        pe.wait_ge(elued[k], elued.before(k, u))
                        pe.wait_ge(h_kept[k], h_kept.before(k, u))
                    wide = b.wide(k, BW)
                    for half in range(2):
                        bias_rows(nc, w, wide[:, 2 * half:2 * half + 2], B_GAT[l], BW, 2)
                        for j in (2 * half, 2 * half + 1):
                            last = nc.tensor.matmul(wide[:, j], b.src_t[:, k, j * P:(j + 1) * P], w.gat[:, l, :],
                                                    start=False, stop=j % 2 == 1)
                    last.then_inc(projected[k], 1)
                yield 3
                for k in K:
                    pe.wait_ge(copied[k], copied.at(k, u))
                    pe.wait_ge(own_in[k], own_in.at(k, u, T - 1 if l == 0 else 0))
                    turn(nc, w, b.one(k), b.own[:, k], own_turned[k])
                yield 5
                for k in K:
                    pe.wait_ge(own_copied[k], own_copied.at(k, u))
                    for j in range(T):
                        last = nc.tensor.matmul(b.one(k)[:, 8 * j:8 * j + 8], b.own_t[:, k, j * P:(j + 1) * P],
                                                w.own_scores[:, l, :], start=True, stop=True)
                    last.then_inc(scored[k], 1)
            w.line.beside(pe, "tensor", n, steps)

        @block.scalar
        def _(act):
            def steps(u):
                yield 2
                for k in K:
                    act.wait_ge(turned[k], turned.at(k, u))
                    nc.scalar.activation(b.src_t[:, k, :], b.one(k), ACT.Copy).then_inc(copied[k], 1)
                yield 4
                for k in K:
                    act.wait_ge(own_turned[k], own_turned.at(k, u))
                    nc.scalar.activation(b.own_t[:, k, :], b.one(k), ACT.Copy).then_inc(own_copied[k], 1)
                yield 4
                for k in K:
                    act.wait_ge(projected[k], projected.at(k, u))
                    nc.scalar.activation(b.e[:, k], b.wide(k, D), ACT.Exp).then_inc(exped[k], 1)
                    nc.scalar.activation(w.sums[:, u * STRANDS + k, :, 0:BW], b.wide(k, BW),
                                         ACT.Copy).then_inc(h_kept[k], 1)
            w.line.beside(act, "scalar", n, steps)

        @block.vector
        def _(dve):
            def steps(u):
                yield 5
                for k in K:
                    dve.wait_ge(exped[k], exped.at(k, u))
                    nc.vector.tensor_scalar(b.e[:, k], b.e[:, k], 1.0, 1.0, ALU.min, ALU.subtract).then_inc(lowered[k], 1)
                yield 6
                for k in K:
                    dve.wait_ge(lowered[k], lowered.at(k, u))
                    dve.wait_ge(h_kept[k], h_kept.at(k, u))
                    if not first(u):
                        dve.wait_ge(stored[k], stored.before(k, u))
                    nc.vector.tensor_tensor(b.new[:, k], b.wide(k, D), b.e[:, k], ALU.max).then_inc(elued[k], 1)
                yield 7
                for k in K:
                    dve.wait_ge(scored[k], scored.at(k, u))
                    nc.vector.tensor_scalar(w.own_parts[:, u * STRANDS + k], b.one(k)[:, 0:8 * T].rearrange(
                        "p (j f) -> p j f", j=T), 1.0, None, ALU.mult).then_inc(own_kept[k], 1)
                if l == 2:
                    yield 8
                    for k in K:
                        dve.wait_ge(elued[k], elued.at(k, u))
                        dve.wait_ge(rest_in[k], rest_in.at(k, u))
                        nc.vector.tensor_tensor(b.new[:, k], b.new[:, k], b.v[:, k, :, 0:D],
                                                ALU.add).then_inc(summed[k], 1)

            def norms(u):
                yield 0.5
                for k in K:
                    dve.wait_ge(summed[k], summed.at(k, u))
                    ln_stats(nc, k, b.stats, b.new[:, k], tallied)
                for k in K:
                    ln_moments(nc, dve, k, u, b, tallied, aggregated)
                yield 3.7
                for k in K:
                    ln_apply(nc, dve, k, u, b, b.new[:, k], b.new[:, k], scaled, normed)

            w.line.beside(dve, "vector", n, steps, 0, norms if l == 2 else None)
    sig.end(n)


def gat_softmax(nc, w, e, ps, sig):
    NS, NTS, NT = e.score_blocks, e.score_tiles, e.tiles
    ctx = ExitStack()
    with ctx:
        sb = sig.buffers(ctx)
        by_tile = sb("score_by_tile", [P, NS, P])
        fwd, bwd = sb("max_forward", [P, NS, P]), sb("max_backward", [P, NS, P])
        outer = sb("outer_ends", [P, 2, NTS])
        cand = sb("outer_candidates", [P, 2, NTS])
        best = sb("outer_best", [P, 2, NS])
        parts = w.own_parts[:, :, :, :].rearrange("p c j f -> p (c j) f")
        e_src = w.sums[:, :, :, D:BW].rearrange("p c j f -> p (c j) f")
        edge = w.edge_share[:, 0:NT, :]
        loop = w.loop_share[:, 0:NT, :]
        edge_cols = w.edge_share[:, :, :].rearrange("p t h -> p (t h)")
        loop_cols = w.loop_share[:, :, :].rearrange("p t h -> p (t h)")
        step = sig.make(1, per=12 + 2 * NS)
        turned, back, exped = sig.make(1), sig.make(1), sig.make(1)
        ends_out, ends_in = sig.dma(1, per=2 * NS), sig.dma(1, per=2)
        counts = {}
        with nc.Block() as block:
            @block.vector
            def _(dve):
                done = [0]

                def mark(ins):
                    ins.then_inc(step[0], 1)
                    done[0] += 1

                def wait():
                    dve.wait_ge(step[0], step.at(0, 0, done[0] - 1))

                nc.vector.memset(edge_cols, 0.0)
                mark(nc.vector.memset(loop_cols, 0.0))
                wait()
                nc.vector.tensor_tensor(edge, e_src, parts[:, :, 0:HEADS], ALU.add)
                mark(nc.vector.tensor_tensor(loop, parts[:, :, HEADS:2 * HEADS], parts[:, :, 0:HEADS], ALU.add))
                wait()
                nc.vector.scalar_tensor_tensor(edge, edge, SLOPE, edge, ALU.mult, ALU.max)
                mark(nc.vector.scalar_tensor_tensor(loop, loop, SLOPE, loop, ALU.mult, ALU.max))
                counts["scores"] = done[0] - 1
                dve.wait_ge(turned[0], turned.at(0, 0))
                mark(nc.vector.tensor_copy(by_tile[:, :, :].rearrange("p s e -> p (s e)"),
                                           ps[:, 0:2, :].rearrange("p b f -> p (b f)")[:, 0:NS * P]))
                wait()
                for s in range(NS):
                    nc.vector.tensor_tensor_scan(fwd[:, s, :], w.step_pen[:, s, 0:P], by_tile[:, s, :], -FAR,
                                                 ALU.add, ALU.max)
                    last = nc.vector.tensor_tensor_scan(bwd[:, s, ::-1], w.step_pen[:, s, 1:P + 1][:, ::-1],
                                                        by_tile[:, s, ::-1], -FAR, ALU.add, ALU.max)
                mark(last)
                wait()
                mark(nc.vector.tensor_tensor(fwd[:, :, :], fwd[:, :, :], bwd[:, :, :], ALU.max))
                counts["ends"] = done[0] - 1
                dve.wait_ge(ends_in[0], ends_in.at(0, 0, 1))
                for s in range(NS):
                    for i in range(2):
                        last = nc.vector.tensor_tensor(cand[:, i, :], outer[:, i, :], w.carry_pen[:, i, s, :], ALU.add)
                    mark(last)
                    wait()
                    for i in range(2):
                        last = nc.vector.tensor_reduce(best[:, i, s:s + 1], cand[:, i, :], AX.X, ALU.max)
                    mark(last)
                    wait()
                for i in range(2):
                    for s in range(NS):
                        last = nc.vector.scalar_tensor_tensor(fwd[:, s, :], w.end_pen[:, i, s, :], best[:, i, s:s + 1],
                                                              fwd[:, s, :], ALU.add, ALU.max)
                    mark(last)
                    wait()
                counts["maxima"] = done[0] - 1
                dve.wait_ge(back[0], back.at(0, 0))
                m = bwd[:, :, :].rearrange("p s e -> p (s e)")
                mark(nc.vector.tensor_tensor(m, ps[:, 2:4, :].rearrange("p b f -> p (b f)")[:, 0:NS * P], loop_cols,
                                             ALU.max))
                wait()
                nc.vector.tensor_tensor(edge_cols, edge_cols, m, ALU.subtract)
                mark(nc.vector.tensor_tensor(loop_cols, loop_cols, m, ALU.subtract))
                counts["shifted"] = done[0] - 1
                counts["all"] = done[0]

            step.per = counts["all"]

            @block.tensor
            def _(pe):
                pe.wait_ge(step[0], step.at(0, 0, counts["scores"]))
                for s in range(NS):
                    last = nc.tensor.transpose(ps[:, s // 4, (s % 4) * P:(s % 4 + 1) * P],
                                               edge_cols[:, s * P:(s + 1) * P], w.ident[:, :])
                last.then_inc(turned[0], 1)
                pe.wait_ge(step[0], step.at(0, 0, counts["maxima"]))
                for s in range(NS):
                    last = nc.tensor.transpose(ps[:, 2 + s // 4, (s % 4) * P:(s % 4 + 1) * P], fwd[:, s, :],
                                               w.ident[:, :])
                last.then_inc(back[0], 1)

            @block.sync
            def _(sp):
                sp.wait_ge(step[0], step.at(0, 0, counts["ends"]))
                for i, at in ((0, P - 1), (1, 0)):
                    for s in range(NS):
                        sp.dma_start(dram_ap(w.maxima_dram, i * HEADS * NTS + s * (P // HEADS),
                                             [[1, P // HEADS], [NTS, HEADS], [1, 1]]),
                                     fwd[:, s, at:at + 1],
                                     allow_slow_non_contiguous=True).then_inc(ends_out[0], 16)
                sp.wait_ge(ends_out[0], ends_out.at(0, 0, 2 * NS - 1))
                for i in range(2):
                    sp.dma_start(outer[:, i, :], dram_ap(w.maxima_dram, i * HEADS * NTS,
                                                         [[0, P // HEADS], [NTS, HEADS], [1, NTS]])
                                 ).then_inc(ends_in[0], 16)

            @block.scalar
            def _(act):
                act.wait_ge(step[0], step.at(0, 0, counts["shifted"]))
                nc.scalar.activation(edge_cols, edge_cols, ACT.Exp)
                nc.scalar.activation(loop_cols, loop_cols, ACT.Exp).then_inc(exped[0], 1)
        sig.end(1)


def sum_tile_rows(nc, w, e, sp, k, u, width, kept, ends_out):
    c = u * STRANDS + k
    sp.wait_ge(kept[k], kept.at(k, u))
    sp.dma_start(w.ends_rows_dram[0, c, :, :, 0:width], w.sums[P - 1:P, c, :, 0:width]).then_inc(ends_out[k], 16)
    sp.dma_start(w.ends_rows_dram[1, c, :, :, 0:width], w.sums[0:1, c, :, 0:width]).then_inc(ends_out[k], 16)


def same_segment(nc, w, e, b, dve, k, u, same_in, same):
    c = u * STRANDS + k
    dve.wait_ge(same_in[k], same_in.at(k, u))
    for j in range(T):
        last = nc.vector.tensor_scalar(b.same[:, k, j * P:(j + 1) * P], b.same[:, k, j * P:(j + 1) * P],
                                       w.dst_chunk[:, c, j:j + 1], None, ALU.is_equal)
    last.then_inc(same[k], 1)


def load_same(nc, w, sp, b, k, u, same_in):
    sp.dma_start(b.same[:, k, :], w.dst_rows_dram[u * STRANDS + k].partition_broadcast(P)).then_inc(same_in[k], 16)


def gat_sums(nc, w, e, b, sig):
    K = range(STRANDS)
    n = e.rounds
    width = D + HEADS
    same_in, ends_out = sig.dma(), sig.dma(per=2)
    same, weighted, added, kept = (sig.make() for _ in range(4))
    with nc.Block() as block:
        @block.sync
        def _(sp):
            for k in K:
                load_same(nc, w, sp, b, k, 0, same_in)
            def steps(u):
                yield 5
                for k in K:
                    if not isinstance(u, int) or u < n - 1:
                        sp.wait_ge(added[k], added.at(k, u))
                        load_same(nc, w, sp, b, k, u + 1, same_in)
                yield 6
                for k in K:
                    sum_tile_rows(nc, w, e, sp, k, u, width, kept, ends_out)
            w.line.beside(sp, "sync", n, steps, tail=1)
            for k in K:
                sp.wait_ge(ends_out[k], ends_out.at(k, n - 1, 1))

        @block.gpsimd
        def _(pool):
            w.line.beside(pool, "gpsimd", n)

        @block.vector
        def _(dve):
            def steps(u):
                yield 1
                for k in K:
                    same_segment(nc, w, e, b, dve, k, u, same_in, same)
                yield 3
                for k in K:
                    c = u * STRANDS + k
                    if not first(u):
                        dve.wait_ge(added[k], added.before(k, u))
                    share = w.edge_chunk[:, c]
                    for j in range(T):
                        nc.vector.tensor_tensor(b.v[:, k, j, 0:D].rearrange("p (h f) -> p h f", h=HEADS),
                                                w.sums[:, c, j, 0:D].rearrange("p (h f) -> p h f", h=HEADS),
                                                share[:, j, :].unsqueeze(2).broadcast_to([P, HEADS, HC]), ALU.mult)
                    nc.vector.tensor_scalar(b.v[:, k, :, D:width], share, 1.0, None, ALU.mult).then_inc(weighted[k], 1)
            w.line.beside(dve, "vector", n, steps)

        @block.tensor
        def _(pe):
            def steps(u):
                yield 4
                for k in K:
                    pe.wait_ge(same[k], same.at(k, u))
                    pe.wait_ge(weighted[k], weighted.at(k, u))
                    if not first(u):
                        pe.wait_ge(kept[k], kept.before(k, u))
                    for j in range(T):
                        last = nc.tensor.matmul(b.wide(k, width)[:, j], b.same[:, k, j * P:(j + 1) * P],
                                                b.v[:, k, j, 0:width], start=True, stop=True)
                    last.then_inc(added[k], 1)
            w.line.beside(pe, "tensor", n, steps)

        @block.scalar
        def _(act):
            def steps(u):
                yield 5
                for k in K:
                    act.wait_ge(added[k], added.at(k, u))
                    act.wait_ge(w.ready, w.ready_count)
                    nc.scalar.activation(w.sums[:, u * STRANDS + k, :, 0:width], b.wide(k, width),
                                         ACT.Copy).then_inc(kept[k], 1)
            w.line.beside(act, "scalar", n, steps)
    sig.end(n)


def carry_sums(nc, w, e, ps, sig, width):
    NB = e.blocks
    ctx = ExitStack()
    with ctx:
        sb = sig.buffers(ctx)
        ends, outer = sb("end_sums", [P, 2, NB, WIDE]), sb("outer_sums", [P, 2, NB, WIDE])
        cleared, multiplied, copied = sig.make(1), sig.make(1), sig.make(1)
        ends_in, carried = sig.dma(1, per=2 * NB), sig.dma(1, per=2 * NB)
        with nc.Block() as block:
            @block.vector
            def _(dve):
                nc.vector.memset(ends[:, :, :, :], 0.0).then_inc(cleared[0], 1)
                dve.wait_ge(multiplied[0], multiplied.at(0, 0))
                for i in range(2):
                    last = nc.vector.tensor_copy(outer[:, i], ps[:, i, 0:NB * WIDE].rearrange("p (m f) -> p m f", m=NB))
                last.then_inc(copied[0], 1)

            @block.sync
            def _(sp):
                sp.wait_ge(cleared[0], cleared.at(0, 0))
                rows = w.ends_rows_dram.rearrange("s c a j f -> s (c a j) f")
                for i in range(2):
                    for m in range(NB):
                        sp.dma_start(ends[0:e.block_rows[m], i, m, 0:width],
                                     rows[i, m * P:m * P + e.block_rows[m], 0:width]).then_inc(ends_in[0], 16)
                sp.wait_ge(copied[0], copied.at(0, 0))
                for i in range(2):
                    for m in range(NB):
                        sp.dma_start(w.carry_dram[i, m * P:m * P + e.block_rows[m], :],
                                     outer[0:e.block_rows[m], i, m, :]).then_inc(carried[0], 16)
                sp.wait_ge(carried[0], carried.at(0, 0, 2 * NB - 1))

            @block.tensor
            def _(pe):
                pe.wait_ge(ends_in[0], ends_in.at(0, 0, 2 * NB - 1))
                for i in range(2):
                    for m in range(NB):
                        for b in range(NB):
                            last = nc.tensor.matmul(ps[:, i, m * WIDE:(m + 1) * WIDE],
                                                    w.carry_eq[:, i, b, m * P:(m + 1) * P], ends[:, i, b, :],
                                                    start=b == 0, stop=b == NB - 1)
                last.then_inc(multiplied[0], 1)
        sig.end(1)


def load_carry(w, sp, b, k, u, width, carry_in):
    c = u * STRANDS + k
    sp.dma_start(b.mask[:, k, :], w.masks_chunk_dram[c]).then_inc(carry_in[k], 16)
    sp.dma_start(b.carry[:, k, :, 0:width], w.carry_chunk_dram[c, :, :, 0:width]).then_inc(carry_in[k], 16)


def add_carry(nc, b, k, width, done):
    for j in range(T):
        last = nc.tensor.matmul(b.wide(k, width)[:, j], b.mask[:, k, j * P:(j + 1) * P], b.carry[:, k, j, 0:width],
                                start=True, stop=True)
    last.then_inc(done, 1)


def gat_finish(nc, w, e, b, sig, l, old, new):
    K = range(STRANDS)
    n = e.rounds
    width = D + HEADS
    own_in, carry_in, rest_in, stored = sig.dma(), sig.dma(per=2), sig.dma(), sig.dma()
    turned, copied, projected, carried, joined, looped, added, divided, exped, lowered, elued = (
        sig.make() for _ in range(11))
    totalled, inverted = sig.make(), sig.make()
    summed, tallied, aggregated, powered, scaled, normed = (sig.make() for _ in range(6))
    last_step = normed if l == 2 else elued
    if l != 2:
        sig.idle(rest_in, summed, tallied, aggregated, powered, scaled, normed)
    old_rows = old.rearrange("(c j p) f -> c p j f", j=T, p=P)
    new_rows = new.rearrange("(c j p) f -> c p j f", j=T, p=P)
    first_rows = w.tables[0].rearrange("(c j p) f -> c p j f", j=T, p=P)

    def load(sp, k, u, prev):
        c = u * STRANDS + k
        if prev is not None:
            sp.wait_ge(turned[k], turned.at(k, prev))
            settle(sp, w)
        sp.dma_start(b.own[:, k], old_rows[e.chunks + c]).then_inc(own_in[k], 16)
        if prev is not None:
            sp.wait_ge(carried[k], carried.at(k, prev))
            settle(sp, w)
        load_carry(w, sp, b, k, u, width, carry_in)

    def load_rest(sp, k, u, prev):
        if prev is not None:
            sp.wait_ge(summed[k], summed.at(k, prev))
            settle(sp, w)
        sp.dma_start(b.v[:, k, :, 0:D], first_rows[e.chunks + u * STRANDS + k]).then_inc(rest_in[k], 16)

    with nc.Block() as block:
        @block.sync
        def _(sp):
            for k in K:
                load(sp, k, 0, None)
                if l == 2:
                    load_rest(sp, k, 0, None)
            def steps(u):
                yield 3
                for k in K:
                    if not isinstance(u, int) or u < n - 1:
                        load(sp, k, u + 1, u)
                if l == 2:
                    yield 12
                    for k in K:
                        if not isinstance(u, int) or u < n - 1:
                            load_rest(sp, k, u + 1, u)
                if l != 2:
                    yield 15
                    store(sp, u)

            def store(sp, u):
                for k in K:
                    sp.wait_ge(last_step[k], last_step.at(k, u))
                    sp.dma_start(new_rows[e.chunks + u * STRANDS + k], b.new[:, k]).then_inc(stored[k], 16)

            def norms(u):
                yield 6.5
                store(sp, u)

            w.line.beside(sp, "sync", n, steps, 1, norms if l == 2 else None)
            for k in K:
                sp.wait_ge(stored[k], stored.at(k, n - 1))

        @block.gpsimd
        def _(pool):
            def norms(u):
                yield 0.9
                for k in K:
                    layer_norm_scale(nc, pool, w, b.moments, b.scale, k, u, 0, aggregated, powered, scaled)

            w.line.beside(pool, "gpsimd", n, None, 0, norms if l == 2 else None)

        @block.tensor
        def _(pe):
            def steps(u):
                yield 1
                for k in K:
                    pe.wait_ge(own_in[k], own_in.at(k, u))
                    if not first(u):
                        pe.wait_ge(looped[k], looped.before(k, u))
                    turn(nc, w, b.one(k), b.own[:, k], turned[k])
                yield 2
                for k in K:
                    pe.wait_ge(carry_in[k], carry_in.at(k, u, 1))
                    if not first(u):
                        pe.wait_ge(joined[k], joined.before(k, u))
                    add_carry(nc, b, k, width, carried[k])
                yield 3
                for k in K:
                    pe.wait_ge(copied[k], copied.at(k, u))
                    bias_rows(nc, w, b.one(k), B_GAT[l])
                    for j in range(T):
                        last = nc.tensor.matmul(b.one(k)[:, j * D:(j + 1) * D], b.own_t[:, k, j * P:(j + 1) * P],
                                                w.gat[:, l, 0:D], start=False, stop=j == T - 1)
                    last.then_inc(projected[k], 1)
            w.line.beside(pe, "tensor", n, steps)

        @block.scalar
        def _(act):
            def steps(u):
                yield 2
                for k in K:
                    act.wait_ge(turned[k], turned.at(k, u))
                    nc.scalar.activation(b.own_t[:, k, :], b.one(k), ACT.Copy).then_inc(copied[k], 1)
                yield 8
                for k in K:
                    act.wait_ge(divided[k], divided.at(k, u))
                    nc.scalar.activation(b.e[:, k], b.src[:, k, :, 0:D], ACT.Exp).then_inc(exped[k], 1)
            w.line.beside(act, "scalar", n, steps)

        @block.vector
        def _(dve):
            def heads(rows):
                return rows.rearrange("p (h f) -> p h f", h=HEADS)

            def steps(u):
                yield 3
                for k in K:
                    dve.wait_ge(carried[k], carried.at(k, u))
                    if not first(u):
                        dve.wait_ge(elued[k], elued.before(k, u))
                    nc.vector.tensor_tensor(b.src[:, k, :, 0:width], b.wide(k, width),
                                            w.sums[:, u * STRANDS + k, :, 0:width], ALU.add).then_inc(joined[k], 1)
                yield 4
                for k in K:
                    dve.wait_ge(projected[k], projected.at(k, u))
                    for j in range(T):
                        last = nc.vector.tensor_tensor(
                            heads(b.e[:, k, j, :]), heads(b.one(k)[:, j * D:(j + 1) * D]),
                            w.loop_chunk[:, u * STRANDS + k, j, :].unsqueeze(2).broadcast_to([P, HEADS, HC]), ALU.mult)
                    last.then_inc(looped[k], 1)
                yield 4
                for k in K:
                    dve.wait_ge(joined[k], joined.at(k, u))
                    nc.vector.tensor_tensor(b.small[:, k, 0, :, 0:HEADS], b.src[:, k, :, D:width],
                                            w.loop_chunk[:, u * STRANDS + k], ALU.add).then_inc(totalled[k], 1)
                yield 5
                for k in K:
                    dve.wait_ge(totalled[k], totalled.at(k, u))
                    nc.vector.reciprocal(b.small[:, k, 1, :, 0:HEADS], b.small[:, k, 0, :, 0:HEADS]).then_inc(inverted[k], 1)
                yield 6
                for k in K:
                    dve.wait_ge(looped[k], looped.at(k, u))
                    nc.vector.tensor_tensor(b.src[:, k, :, 0:D], b.src[:, k, :, 0:D], b.e[:, k],
                                            ALU.add).then_inc(added[k], 1)
                yield 7
                for k in K:
                    dve.wait_ge(added[k], added.at(k, u))
                    dve.wait_ge(inverted[k], inverted.at(k, u))
                    for j in range(T):
                        last = nc.vector.tensor_tensor(
                            heads(b.src[:, k, j, 0:D]), heads(b.src[:, k, j, 0:D]),
                            b.small[:, k, 1, j, 0:HEADS].unsqueeze(2).broadcast_to([P, HEADS, HC]), ALU.mult)
                    last.then_inc(divided[k], 1)
                yield 9
                for k in K:
                    dve.wait_ge(exped[k], exped.at(k, u))
                    nc.vector.tensor_scalar(b.e[:, k], b.e[:, k], 1.0, 1.0, ALU.min, ALU.subtract).then_inc(lowered[k], 1)
                yield 10
                for k in K:
                    dve.wait_ge(lowered[k], lowered.at(k, u))
                    if not first(u):
                        dve.wait_ge(stored[k], stored.before(k, u))
                    nc.vector.tensor_tensor(b.new[:, k], b.src[:, k, :, 0:D], b.e[:, k], ALU.max).then_inc(elued[k], 1)
                if l == 2:
                    yield 11
                    for k in K:
                        dve.wait_ge(elued[k], elued.at(k, u))
                        dve.wait_ge(rest_in[k], rest_in.at(k, u))
                        nc.vector.tensor_tensor(b.new[:, k], b.new[:, k], b.v[:, k, :, 0:D],
                                                ALU.add).then_inc(summed[k], 1)

            def norms(u):
                yield 0.5
                for k in K:
                    dve.wait_ge(summed[k], summed.at(k, u))
                    ln_stats(nc, k, b.stats, b.new[:, k], tallied)
                for k in K:
                    ln_moments(nc, dve, k, u, b, tallied, aggregated)
                yield 5.5
                for k in K:
                    ln_apply(nc, dve, k, u, b, b.new[:, k], b.new[:, k], scaled, normed)

            w.line.beside(dve, "vector", n, steps, 0, norms if l == 2 else None)
    sig.end(n)


def dst_update(nc, a, w, e, b, ps, sig, kind, old, new, out):
    K = range(STRANDS)
    n = e.rounds
    width = {"sage": D + 4, "rel": D, "att": WIDE}[kind]
    own_in, carry_in, stored = sig.dma(), sig.dma(per=2), sig.gather(per=T) if kind == "att" else sig.dma()
    index_in = sig.dma() if kind == "att" else None
    turned, copied, projected, carried, joined, totalled, inverted, divided = (sig.make() for _ in range(8))
    mean_turned, mean_copied, shifted, summed = (sig.make() for _ in range(4))
    tallied, aggregated, powered, scaled, normed = (sig.make() for _ in range(5))
    sig.idle(*{"sage": (shifted, summed), "rel": (totalled, inverted, divided, mean_turned, mean_copied),
               "att": (turned, copied, totalled, shifted)}[kind])
    old_rows = old.rearrange("(c j p) f -> c p j f", j=T, p=P)
    new_rows = None if new is None else new.rearrange("(c j p) f -> c p j f", j=T, p=P)

    late = kind != "sage"
    summed_rows = b.v[:, :, :, 0:D] if late else b.e

    def load(sp, k, u, prev):
        if prev is not None:
            if kind != "att":
                sp.wait_ge(turned[k], turned.at(k, prev))
                settle(sp, w)
            if kind != "sage":
                sp.wait_ge(summed[k], summed.at(k, prev))
                settle(sp, w)
        sp.dma_start(b.own[:, k], old_rows[e.chunks + u * STRANDS + k]).then_inc(own_in[k], 16)

    def load_sums(sp, k, u, prev):
        if prev is not None:
            sp.wait_ge(carried[k], carried.at(k, prev))
            settle(sp, w)
        load_carry(w, sp, b, k, u, width, carry_in)

    def load_index(sp, k, u, prev):
        if prev is not None:
            sp.wait_ge(stored[k], stored.at(k, prev, T - 1))
            settle(sp, w)
        sp.dma_start(b.index[:, k, 0, :], w.lists_dram[2, u * STRANDS + k]).then_inc(index_in[k], 16)

    def run(eng, name, steps, norms, tail=0):
        if late:
            w.line.beside(eng, name, n, steps, tail, norms)
        else:
            w.line.beside(eng, name, n, lambda u: chain(steps(u), norms(u)), tail)

    def nothing(u):
        return iter(())

    with nc.Block() as block:
        @block.sync
        def _(sp):
            for k in K:
                load(sp, k, 0, None)
                load_sums(sp, k, 0, None)
                if kind == "att":
                    load_index(sp, k, 0, None)

            def steps(u):
                yield 3
                for k in K:
                    if not isinstance(u, int) or u < n - 1:
                        load_sums(sp, k, u + 1, u)
                yield {"sage": 3, "rel": 8, "att": 10}[kind]
                for k in K:
                    if not isinstance(u, int) or u < n - 1:
                        load(sp, k, u + 1, u)

            def norms(u):
                yield 6.5 if late else 14
                for k in K:
                    if kind != "att":
                        sp.wait_ge(normed[k], normed.at(k, u))
                        sp.dma_start(new_rows[e.chunks + u * STRANDS + k], b.new[:, k]).then_inc(stored[k], 16)
                    elif not isinstance(u, int) or u < n - 1:
                        load_index(sp, k, u + 1, u)

            run(sp, "sync", steps, norms, tail=1)
            for k in K:
                sp.wait_ge(stored[k], stored.at(k, n - 1, T - 1 if kind == "att" else 0))

        @block.gpsimd
        def _(pool):
            def norms(u):
                yield 1 if late else 12
                for k in K:
                    layer_norm_scale(nc, pool, w, b.moments, b.scale, k, u, 0, aggregated, powered, scaled)
                if kind == "att":
                    yield 6
                    for k in K:
                        pool.wait_ge(normed[k], normed.at(k, u))
                        pool.wait_ge(index_in[k], index_in.at(k, u))
                        pool.wait_ge(w.ready, w.ready_count)
                        settle(pool, w)
                        for j in range(T):
                            nc.gpsimd.indirect_dma_start(
                                out, bass.IndirectOffsetOnAxis(ap=b.index[:, k, 0, j:j + 1], axis=0),
                                b.new[:, k, j, :], None, bounds_check=e.n_nodes - 1,
                                oob_is_err=False).then_inc(stored[k], 16)
            run(pool, "gpsimd", nothing, norms)

        @block.tensor
        def _(pe):
            def steps(u):
                if kind != "att":
                    yield 1
                    for k in K:
                        pe.wait_ge(own_in[k], own_in.at(k, u))
                        if not first(u):
                            free = normed if kind == "sage" else shifted
                            pe.wait_ge(free[k], free.before(k, u))
                        turn(nc, w, b.one(k), b.own[:, k], turned[k])
                yield 2
                for k in K:
                    pe.wait_ge(carry_in[k], carry_in.at(k, u, 1))
                    if not first(u):
                        pe.wait_ge(joined[k], joined.before(k, u))
                    add_carry(nc, b, k, width, carried[k])
                if kind == "rel":
                    yield 3
                    for k in K:
                        pe.wait_ge(copied[k], copied.at(k, u))
                        bias_rows(nc, w, b.one(k), B_REL)
                        for j in range(T):
                            last = nc.tensor.matmul(b.one(k)[:, j * D:(j + 1) * D], b.own_t[:, k, j * P:(j + 1) * P],
                                                    w.self_loop[:, :], start=False, stop=j == T - 1)
                        last.then_inc(projected[k], 1)
                else:
                    yield 7
                    for k in K:
                        pe.wait_ge(divided[k], divided.at(k, u))
                        if kind == "sage":
                            pe.wait_ge(copied[k], copied.at(k, u))
                        elif not first(u):
                            pe.wait_ge(summed[k], summed.before(k, u))
                        turn(nc, w, b.one(k), b.e[:, k], mean_turned[k])
                    yield 9
                    for k in K:
                        pe.wait_ge(mean_copied[k], mean_copied.at(k, u))
                        bias_rows(nc, w, b.one(k), B_SAGE if kind == "sage" else B_O)
                        for j in range(T):
                            dst = b.one(k)[:, j * D:(j + 1) * D]
                            if kind == "sage":
                                nc.tensor.matmul(dst, b.own_t[:, k, j * P:(j + 1) * P], w.sage_own[:, :],
                                                 start=False, stop=False)
                            last = nc.tensor.matmul(dst, b.src_t[:, k, j * P:(j + 1) * P],
                                                    w.sage_mean[:, :] if kind == "sage" else w.o[:, :],
                                                    start=False, stop=j == T - 1)
                        last.then_inc(projected[k], 1)
            run(pe, "tensor", steps, nothing)

        @block.scalar
        def _(act):
            def steps(u):
                if kind != "att":
                    yield 2
                    for k in K:
                        act.wait_ge(turned[k], turned.at(k, u))
                        if kind == "sage" and not first(u):
                            act.wait_ge(projected[k], projected.before(k, u))
                        nc.scalar.activation(b.own_t[:, k, :], b.one(k), ACT.Copy).then_inc(copied[k], 1)
                if kind != "rel":
                    yield 8
                    for k in K:
                        act.wait_ge(mean_turned[k], mean_turned.at(k, u))
                        nc.scalar.activation(b.src_t[:, k, :], b.one(k), ACT.Copy).then_inc(mean_copied[k], 1)
            run(act, "scalar", steps, nothing)

        @block.vector
        def _(dve):
            def steps(u):
                yield 3
                for k in K:
                    dve.wait_ge(carried[k], carried.at(k, u))
                    nc.vector.tensor_tensor(b.src[:, k, :, 0:width], b.wide(k, width),
                                            w.sums[:, u * STRANDS + k, :, 0:width], ALU.add).then_inc(joined[k], 1)
                if kind == "sage":
                    yield 4
                    for k in K:
                        dve.wait_ge(joined[k], joined.at(k, u))
                        nc.vector.tensor_scalar(b.small[:, k, 0, :, 0:1], b.src[:, k, :, D:D + 1], 1.0, None,
                                                ALU.max).then_inc(totalled[k], 1)
                    yield 4
                    for k in K:
                        dve.wait_ge(totalled[k], totalled.at(k, u))
                        nc.vector.reciprocal(b.small[:, k, 1, :, 0:1], b.small[:, k, 0, :, 0:1]).then_inc(inverted[k], 1)
                    yield 5
                    for k in K:
                        dve.wait_ge(inverted[k], inverted.at(k, u))
                        for j in range(T):
                            last = nc.vector.tensor_scalar(b.e[:, k, j, :], b.src[:, k, j, 0:D],
                                                           b.small[:, k, 1, j, 0:1], None, ALU.mult)
                        last.then_inc(divided[k], 1)
                    yield 10
                    for k in K:
                        dve.wait_ge(projected[k], projected.at(k, u))
                        ln_stats(nc, k, b.stats, b.tiles(b.one(k)), tallied)
                if kind == "rel":
                    yield 6
                    for k in K:
                        dve.wait_ge(joined[k], joined.at(k, u))
                        dve.wait_ge(projected[k], projected.at(k, u))
                        nc.vector.tensor_tensor(b.src[:, k, :, 0:D], b.tiles(b.one(k)), b.src[:, k, :, 0:D],
                                                ALU.add).then_inc(shifted[k], 1)
                    yield 7
                    for k in K:
                        dve.wait_ge(shifted[k], shifted.at(k, u))
                        if not first(u):
                            dve.wait_ge(normed[k], normed.before(k, u))
                        nc.vector.scalar_tensor_tensor(summed_rows[:, k], b.src[:, k, :, 0:D], 0.0, b.own[:, k], ALU.max,
                                                       ALU.add).then_inc(summed[k], 1)
                if kind == "att":
                    yield 4
                    for k in K:
                        dve.wait_ge(joined[k], joined.at(k, u))
                        nc.vector.reciprocal(b.small[:, k, 1], b.src[:, k, :, D:WIDE]).then_inc(inverted[k], 1)
                    yield 5
                    for k in K:
                        dve.wait_ge(inverted[k], inverted.at(k, u))
                        for j in range(T):
                            last = nc.vector.tensor_tensor(
                                b.e[:, k, j, :].rearrange("p (h f) -> p h f", h=AHEADS),
                                b.src[:, k, j, 0:D].rearrange("p (h f) -> p h f", h=AHEADS),
                                b.small[:, k, 1, j, :].unsqueeze(2).broadcast_to([P, AHEADS, AD]), ALU.mult)
                        last.then_inc(divided[k], 1)
                    yield 9
                    for k in K:
                        dve.wait_ge(projected[k], projected.at(k, u))
                        dve.wait_ge(own_in[k], own_in.at(k, u))
                        if not first(u):
                            dve.wait_ge(normed[k], normed.before(k, u))
                        nc.vector.tensor_tensor(summed_rows[:, k], b.tiles(b.one(k)), b.own[:, k],
                                                ALU.add).then_inc(summed[k], 1)

            def norms(u):
                rows = [b.tiles(b.one(k)) if kind == "sage" else summed_rows[:, k] for k in K]
                if kind != "sage":
                    yield 0.5 if late else 10
                    for k in K:
                        dve.wait_ge(summed[k], summed.at(k, u))
                        ln_stats(nc, k, b.stats, rows[k], tallied)
                yield 0.6 if late else 11
                for k in K:
                    ln_moments(nc, dve, k, u, b, tallied, aggregated)
                yield 5.5 if late else 13
                for k in K:
                    if not first(u):
                        dve.wait_ge(stored[k], stored.before(k, u))
                    ln_apply(nc, dve, k, u, b, b.new[:, k], rows[k], scaled, normed)

            run(dve, "vector", steps, norms)
    sig.end(n)


def sage_messages(nc, a, w, e, b, ps, sig, old, new):
    K = range(STRANDS)
    n = e.rounds
    width = D + 4
    index_in, gathered, same_in, ends_out, stored = sig.dma(), sig.gather(per=T), sig.dma(), sig.dma(per=2), sig.dma()
    same, added, kept, turned, copied, projected = (sig.make() for _ in range(6))
    tallied, aggregated, powered, scaled, normed = (sig.make() for _ in range(5))
    new_rows = new.rearrange("(c j p) f -> c p j f", j=T, p=P)

    def load(sp, k, u, prev):
        if prev is not None:
            sp.wait_ge(gathered[k], gathered.at(k, prev, T - 1))
            settle(sp, w)
        sp.dma_start(b.index[:, k, 0, :], w.lists_dram[3, u * STRANDS + k]).then_inc(index_in[k], 16)

    def load_segments(sp, k, u, prev):
        if prev is not None:
            sp.wait_ge(added[k], added.at(k, prev))
            settle(sp, w)
        load_same(nc, w, sp, b, k, u, same_in)

    def fetch(pool, k, u, prev):
        if prev is not None:
            pool.wait_ge(turned[k], turned.at(k, prev))
            pool.wait_ge(added[k], added.at(k, prev))
        pool.wait_ge(index_in[k], index_in.at(k, u))
        pool.wait_ge(w.ready, w.ready_count)
        settle(pool, w)
        gather(nc, b.src[:, k], old, b.index[:, k, 0, :], gathered[k])

    with nc.Block() as block:
        @block.vector
        def _(dve):
            nc.vector.memset(b.src[:, :, :, D:WIDE], 0.0)

    with nc.Block() as block:
        @block.vector
        def _(dve):
            nc.vector.memset(b.src[:, :, :, D:D + 1], 1.0)

    with nc.Block() as block:
        @block.sync
        def _(sp):
            for k in K:
                load(sp, k, 0, None)
                load_segments(sp, k, 0, None)
            def steps(u):
                yield 0.8
                for k in K:
                    if not isinstance(u, int) or u < n - 1:
                        load(sp, k, u + 1, u)
                yield 3
                for k in K:
                    if not isinstance(u, int) or u < n - 1:
                        load_segments(sp, k, u + 1, u)
                yield 4
                for k in K:
                    sum_tile_rows(nc, w, e, sp, k, u, width, kept, ends_out)
                yield 7
                for k in K:
                    sp.wait_ge(normed[k], normed.at(k, u))
                    sp.dma_start(new_rows[u * STRANDS + k], b.new[:, k]).then_inc(stored[k], 16)
            w.line.beside(sp, "sync", n, steps, tail=1)
            for k in K:
                sp.wait_ge(ends_out[k], ends_out.at(k, n - 1, 1))
                sp.wait_ge(stored[k], stored.at(k, n - 1))

        @block.gpsimd
        def _(pool):
            for k in K:
                fetch(pool, k, 0, None)
            def steps(u):
                yield 5
                for k in K:
                    layer_norm_scale(nc, pool, w, b.moments, b.scale, k, u, 0, aggregated, powered, scaled)
                yield w.line.at.fetch0
                if not isinstance(u, int) or u < n - 1:
                    fetch(pool, 0, u + 1, u)
                yield w.line.at.fetch1
                if not isinstance(u, int) or u < n - 1:
                    fetch(pool, 1, u + 1, u)
            w.line.beside(pool, "gpsimd", n, steps, tail=1)

        @block.tensor
        def _(pe):
            def steps(u):
                yield 1
                for k in K:
                    pe.wait_ge(gathered[k], gathered.at(k, u, T - 1))
                    if not first(u):
                        pe.wait_ge(normed[k], normed.before(k, u))
                    turn(nc, w, b.one(k), b.src[:, k], turned[k])
                yield 2
                for k in K:
                    pe.wait_ge(same[k], same.at(k, u))
                    if not first(u):
                        pe.wait_ge(kept[k], kept.before(k, u))
                    for j in range(T):
                        last = nc.tensor.matmul(b.wide(k, width)[:, j], b.same[:, k, j * P:(j + 1) * P],
                                                b.src[:, k, j, 0:width], start=True, stop=True)
                    last.then_inc(added[k], 1)
                yield 3
                for k in K:
                    pe.wait_ge(copied[k], copied.at(k, u))
                    bias_rows(nc, w, b.one(k), B_SAGE)
                    for j in range(T):
                        last = nc.tensor.matmul(b.one(k)[:, j * D:(j + 1) * D], b.src_t[:, k, j * P:(j + 1) * P],
                                                w.sage_own[:, :], start=False, stop=j == T - 1)
                    last.then_inc(projected[k], 1)
            w.line.beside(pe, "tensor", n, steps)

        @block.scalar
        def _(act):
            def steps(u):
                yield 2
                for k in K:
                    act.wait_ge(turned[k], turned.at(k, u))
                    nc.scalar.activation(b.src_t[:, k, :], b.one(k), ACT.Copy).then_inc(copied[k], 1)
                yield 3
                for k in K:
                    act.wait_ge(added[k], added.at(k, u))
                    act.wait_ge(w.ready, w.ready_count)
                    nc.scalar.activation(w.sums[:, u * STRANDS + k, :, 0:width], b.wide(k, width),
                                         ACT.Copy).then_inc(kept[k], 1)
            w.line.beside(act, "scalar", n, steps)

        @block.vector
        def _(dve):
            def steps(u):
                yield 1
                for k in K:
                    same_segment(nc, w, e, b, dve, k, u, same_in, same)
                yield 4
                for k in K:
                    dve.wait_ge(projected[k], projected.at(k, u))
                    ln_stats(nc, k, b.stats, b.tiles(b.one(k)), tallied)
                yield 4
                for k in K:
                    ln_moments(nc, dve, k, u, b, tallied, aggregated)
                yield 6
                for k in K:
                    if not first(u):
                        dve.wait_ge(stored[k], stored.before(k, u))
                    ln_apply(nc, dve, k, u, b, b.new[:, k], b.tiles(b.one(k)), scaled, normed)
            w.line.beside(dve, "vector", n, steps)
    sig.end(n)


def rel_messages(nc, a, w, e, b, ps, sig, old, new):
    K = range(STRANDS)
    width = D
    n = e.rounds
    index_in, gathered, same_in, ends_out, stored = sig.dma(), sig.gather(per=T), sig.dma(), sig.dma(per=2), sig.dma()
    same, added, kept, turned, copied, projected, summed = (sig.make() for _ in range(7))
    related, chosen = sig.make(per=T), sig.make(per=T * CHOICES)
    tallied, aggregated, powered, scaled, normed = (sig.make() for _ in range(5))
    begun = sig.make(per=T)
    new_rows = new.rearrange("(c j p) f -> c p j f", j=T, p=P)

    def load(sp, k, u, prev):
        if prev is not None:
            sp.wait_ge(gathered[k], gathered.at(k, prev, T - 1))
            settle(sp, w)
        sp.dma_start(b.index[:, k, 0, :], w.lists_dram[3, u * STRANDS + k]).then_inc(index_in[k], 16)

    def load_segments(sp, k, u, prev):
        if prev is not None:
            sp.wait_ge(added[k], added.at(k, prev))
            settle(sp, w)
        load_same(nc, w, sp, b, k, u, same_in)

    def fetch(pool, k, u, prev):
        if prev is not None:
            pool.wait_ge(summed[k], summed.at(k, prev))
        pool.wait_ge(index_in[k], index_in.at(k, u))
        pool.wait_ge(w.ready, w.ready_count)
        settle(pool, w)
        gather(nc, b.src[:, k], old, b.index[:, k, 0, :], gathered[k])

    def halves(k, j):
        return b.v[:, k, j, 0:D], b.own[:, k, j, :]

    def mine(u, k, j, half, q):
        return w.rel_chunk[:, half * RELS // 2 + q, u * STRANDS + k, j:j + 1]

    def product(k, half, q):
        return b.ps[:, 3 * k + 1 + half, q * D:(q + 1) * D]

    with nc.Block() as block:
        @block.sync
        def _(sp):
            for k in K:
                load(sp, k, 0, None)
                load_segments(sp, k, 0, None)
            def steps(u):
                yield 2
                for k in K:
                    if not isinstance(u, int) or u < n - 1:
                        load(sp, k, u + 1, u)
                yield 13
                for k in K:
                    sp.wait_ge(normed[k], normed.at(k, u))
                    sp.dma_start(new_rows[u * STRANDS + k], b.new[:, k]).then_inc(stored[k], 16)
                yield 13
                for k in K:
                    if not isinstance(u, int) or u < n - 1:
                        load_segments(sp, k, u + 1, u)
                yield 14
                for k in K:
                    sum_tile_rows(nc, w, e, sp, k, u, width, kept, ends_out)
            w.line.beside(sp, "sync", n, steps, tail=1)
            for k in K:
                sp.wait_ge(ends_out[k], ends_out.at(k, n - 1, 1))
                sp.wait_ge(stored[k], stored.at(k, n - 1))

        @block.gpsimd
        def _(pool):
            for k in K:
                fetch(pool, k, 0, None)
            def steps(u):
                yield 5
                for k in K:
                    layer_norm_scale(nc, pool, w, b.moments, b.scale, k, u, 0, aggregated, powered, scaled)
                yield w.line.at.fetch0
                if not isinstance(u, int) or u < n - 1:
                    fetch(pool, 0, u + 1, u)
                yield w.line.at.fetch1
                if not isinstance(u, int) or u < n - 1:
                    fetch(pool, 1, u + 1, u)
            w.line.beside(pool, "gpsimd", n, steps, tail=1)

        @block.tensor
        def _(pe):
            def steps(u):
                yield 1
                for k in K:
                    pe.wait_ge(gathered[k], gathered.at(k, u, T - 1))
                    if not first(u):
                        pe.wait_ge(kept[k], kept.before(k, u))
                    turn(nc, w, b.one(k), b.src[:, k], turned[k])
                yield 3
                for k in K:
                    pe.wait_ge(copied[k], copied.at(k, u))
                    bias_rows(nc, w, b.one(k), B_REL)
                    for j in range(T):
                        last = nc.tensor.matmul(b.one(k)[:, j * D:(j + 1) * D], b.src_t[:, k, j * P:(j + 1) * P],
                                                w.self_loop[:, :], start=False, stop=j == T - 1)
                    last.then_inc(projected[k], 1)
                for j in range(T):
                    yield 4 + 2 * j
                    for k in K:
                        if j == 0:
                            pe.wait_ge(copied[k], copied.at(k, u))
                            if not first(u):
                                pe.wait_ge(chosen[k], chosen.before(k, u))
                        else:
                            pe.wait_ge(chosen[k], chosen.at(k, u, j * CHOICES - 1))
                        for half in range(2):
                            last = nc.tensor.matmul(
                                b.ps[:, 3 * k + 1 + half, :], b.src_t[:, k, j * P:(j + 1) * P],
                                w.rel[:, half * RELS // 2:(half + 1) * RELS // 2, :].rearrange("p r o -> p (r o)"),
                                start=True, stop=True)
                        last.then_inc(related[k], 1)
                yield 12
                for k in K:
                    pe.wait_ge(same[k], same.at(k, u))
                    pe.wait_ge(chosen[k], chosen.at(k, u, T * CHOICES - 1))
                    pe.wait_ge(summed[k], summed.at(k, u))
                    for j in range(T):
                        last = nc.tensor.matmul(b.one(k)[:, j * D:(j + 1) * D], b.same[:, k, j * P:(j + 1) * P],
                                                b.v[:, k, j, 0:D], start=True, stop=True)
                    last.then_inc(added[k], 1)
            w.line.beside(pe, "tensor", n, steps)

        @block.scalar
        def _(act):
            def steps(u):
                yield 2
                for k in K:
                    act.wait_ge(turned[k], turned.at(k, u))
                    nc.scalar.activation(b.src_t[:, k, :], b.one(k), ACT.Copy).then_inc(copied[k], 1)
                for j in range(T):
                    yield 4.5 + 2 * j
                    for k in K:
                        act.wait_ge(related[k], related.at(k, u, j))
                        if j == 0 and not first(u):
                            act.wait_ge(added[k], added.before(k, u))
                        act.wait_ge(w.ready, w.ready_count)
                        for half in range(2):
                            last = nc.scalar.activation(halves(k, j)[half], product(k, half, 0), ACT.Copy,
                                                        scale=mine(u, k, j, half, 0))
                        last.then_inc(begun[k], 1)
                yield 13
                for k in K:
                    act.wait_ge(added[k], added.at(k, u))
                    act.wait_ge(w.ready, w.ready_count)
                    nc.scalar.activation(w.sums[:, u * STRANDS + k, :, 0:D], b.tiles(b.one(k)),
                                         ACT.Copy).then_inc(kept[k], 1)
            w.line.beside(act, "scalar", n, steps)

        @block.vector
        def _(dve):
            def steps(u):
                yield 1
                for k in K:
                    same_segment(nc, w, e, b, dve, k, u, same_in, same)
                yield 4
                for k in K:
                    dve.wait_ge(projected[k], projected.at(k, u))
                    nc.vector.scalar_tensor_tensor(b.e[:, k], b.tiles(b.one(k)), 0.0, b.src[:, k, :, 0:D], ALU.max,
                                                   ALU.add).then_inc(summed[k], 1)
                yield 4
                for k in K:
                    dve.wait_ge(summed[k], summed.at(k, u))
                    ln_stats(nc, k, b.stats, b.e[:, k], tallied)
                yield 4
                for k in K:
                    ln_moments(nc, dve, k, u, b, tallied, aggregated)
                for j in range(T):
                    yield 5 + 2 * j
                    for k in K:
                        dve.wait_ge(begun[k], begun.at(k, u, j))
                        for i in range(CHOICES - 1):
                            half, q = i % 2, 1 + i // 2
                            if i >= 2:
                                dve.wait_ge(chosen[k], chosen.at(k, u, j * CHOICES + i - 2))
                            part = halves(k, j)[half]
                            nc.vector.scalar_tensor_tensor(part, product(k, half, q), mine(u, k, j, half, q), part,
                                                           ALU.mult, ALU.add).then_inc(chosen[k], 1)
                        dve.wait_ge(chosen[k], chosen.at(k, u, j * CHOICES + CHOICES - 2))
                        one, other = halves(k, j)
                        nc.vector.tensor_tensor(one, one, other, ALU.add).then_inc(chosen[k], 1)
                yield 12
                for k in K:
                    if not first(u):
                        dve.wait_ge(stored[k], stored.before(k, u))
                    ln_apply(nc, dve, k, u, b, b.new[:, k], b.e[:, k], scaled, normed)
            w.line.beside(dve, "vector", n, steps)
    sig.end(n)


def att_messages(nc, a, w, e, b, ps, sig, old):
    K = range(STRANDS)
    width = WIDE
    n = e.rounds
    index_in, gathered, same_in, ends_out, own_in = sig.dma(), sig.gather(per=T), sig.dma(), sig.dma(per=2), sig.dma()
    same, added, kept, turned, copied, own_turned, own_copied = (sig.make() for _ in range(7))
    keyed, queried, query_kept, matched, reduced, clipped, bounded, exped, weighted = (sig.make() for _ in range(9))
    old_rows = old.rearrange("(c j p) f -> c p j f", j=T, p=P)

    def load(sp, k, u, prev):
        c = u * STRANDS + k
        if prev is not None:
            sp.wait_ge(gathered[k], gathered.at(k, prev, T - 1))
            settle(sp, w)
        sp.dma_start(b.index[:, k, 0, :], w.lists_dram[3, c]).then_inc(index_in[k], 16)

    def load_own(sp, k, u, prev):
        c = u * STRANDS + k
        if prev is not None:
            sp.wait_ge(own_turned[k], own_turned.at(k, prev))
            settle(sp, w)
        sp.dma_start(b.own[:, k], old_rows[e.chunks + c]).then_inc(own_in[k], 16)

    def load_segments(sp, k, u, prev):
        if prev is not None:
            sp.wait_ge(added[k], added.at(k, prev))
            settle(sp, w)
        load_same(nc, w, sp, b, k, u, same_in)

    def fetch(pool, k, u, prev):
        if prev is not None:
            pool.wait_ge(turned[k], turned.at(k, prev))
        pool.wait_ge(index_in[k], index_in.at(k, u))
        pool.wait_ge(w.ready, w.ready_count)
        settle(pool, w)
        gather(nc, b.src[:, k], old, b.index[:, k, 0, :], gathered[k])

    with nc.Block() as block:
        @block.sync
        def _(sp):
            for k in K:
                load(sp, k, 0, None)
                load_own(sp, k, 0, None)
                load_segments(sp, k, 0, None)
            def steps(u):
                yield 0.8
                for k in K:
                    if not isinstance(u, int) or u < n - 1:
                        load(sp, k, u + 1, u)
                yield 4
                for k in K:
                    if not isinstance(u, int) or u < n - 1:
                        load_own(sp, k, u + 1, u)
                yield 13
                for k in K:
                    if not isinstance(u, int) or u < n - 1:
                        load_segments(sp, k, u + 1, u)
                yield 14
                for k in K:
                    sum_tile_rows(nc, w, e, sp, k, u, width, kept, ends_out)
            w.line.beside(sp, "sync", n, steps, tail=1)
            for k in K:
                sp.wait_ge(ends_out[k], ends_out.at(k, n - 1, 1))

        @block.gpsimd
        def _(pool):
            for k in K:
                fetch(pool, k, 0, None)
            def steps(u):
                yield w.line.at.fetch0
                if not isinstance(u, int) or u < n - 1:
                    fetch(pool, 0, u + 1, u)
                yield w.line.at.fetch1
                if not isinstance(u, int) or u < n - 1:
                    fetch(pool, 1, u + 1, u)
            w.line.beside(pool, "gpsimd", n, steps, tail=1)

        @block.tensor
        def _(pe):
            def steps(u):
                yield 1
                for k in K:
                    pe.wait_ge(gathered[k], gathered.at(k, u, T - 1))
                    if not first(u):
                        pe.wait_ge(query_kept[k], query_kept.before(k, u))
                    turn(nc, w, b.one(k), b.src[:, k], turned[k])
                yield 3
                for k in K:
                    pe.wait_ge(copied[k], copied.at(k, u))
                    if not first(u):
                        pe.wait_ge(kept[k], kept.before(k, u))
                    wide = b.wide(k, 2 * D)
                    for half in range(2):
                        nc.tensor.matmul(b.ps[:, 3 * k + 1 + half, :].rearrange("p (j s f) -> p j s f", j=2, s=2),
                                         w.ones4[0:3, 0:P],
                                         w.kv_bias[0:3].unsqueeze(1).broadcast_to([3, 2, 2, D]),
                                         start=True, stop=False)
                        for j in (2 * half, 2 * half + 1):
                            last = nc.tensor.matmul(wide[:, j], b.src_t[:, k, j * P:(j + 1) * P], w.kv[:, :],
                                                    start=False, stop=j % 2 == 1)
                    last.then_inc(keyed[k], 1)
                yield 3
                for k in K:
                    pe.wait_ge(copied[k], copied.at(k, u))
                    pe.wait_ge(own_in[k], own_in.at(k, u))
                    turn(nc, w, b.one(k), b.own[:, k], own_turned[k])
                yield 5
                for k in K:
                    pe.wait_ge(own_copied[k], own_copied.at(k, u))
                    bias_rows(nc, w, b.one(k), B_Q)
                    for j in range(T):
                        last = nc.tensor.matmul(b.one(k)[:, j * D:(j + 1) * D], b.own_t[:, k, j * P:(j + 1) * P],
                                                w.q[:, :], start=False, stop=j == T - 1)
                    last.then_inc(queried[k], 1)
                yield 12
                for k in K:
                    pe.wait_ge(same[k], same.at(k, u))
                    pe.wait_ge(weighted[k], weighted.at(k, u))
                    for j in range(T):
                        last = nc.tensor.matmul(b.wide(k, WIDE)[:, j], b.same[:, k, j * P:(j + 1) * P],
                                                b.v[:, k, j, :], start=True, stop=True)
                    last.then_inc(added[k], 1)
            w.line.beside(pe, "tensor", n, steps)

        @block.scalar
        def _(act):
            def steps(u):
                yield 2
                for k in K:
                    act.wait_ge(turned[k], turned.at(k, u))
                    nc.scalar.activation(b.src_t[:, k, :], b.one(k), ACT.Copy).then_inc(copied[k], 1)
                yield 4
                for k in K:
                    act.wait_ge(own_turned[k], own_turned.at(k, u))
                    nc.scalar.activation(b.own_t[:, k, :], b.one(k), ACT.Copy).then_inc(own_copied[k], 1)
                yield 6
                for k in K:
                    act.wait_ge(queried[k], queried.at(k, u))
                    if not first(u):
                        act.wait_ge(matched[k], matched.before(k, u))
                    nc.scalar.activation(b.e[:, k], b.tiles(b.one(k)), ACT.Copy).then_inc(query_kept[k], 1)
                yield 10
                for k in K:
                    act.wait_ge(bounded[k], bounded.at(k, u))
                    if not first(u):
                        act.wait_ge(weighted[k], weighted.before(k, u))
                        act.wait_ge(added[k], added.before(k, u))
                    nc.scalar.activation(b.v[:, k, :, D:WIDE], b.small[:, k, 2], ACT.Exp).then_inc(exped[k], 1)
                yield 13
                for k in K:
                    act.wait_ge(added[k], added.at(k, u))
                    act.wait_ge(w.ready, w.ready_count)
                    nc.scalar.activation(w.sums[:, u * STRANDS + k, :, :], b.wide(k, WIDE),
                                         ACT.Copy).then_inc(kept[k], 1)
            w.line.beside(act, "scalar", n, steps)

        @block.vector
        def _(dve):
            def steps(u):
                yield 1
                for k in K:
                    same_segment(nc, w, e, b, dve, k, u, same_in, same)
                yield 7
                for k in K:
                    dve.wait_ge(keyed[k], keyed.at(k, u))
                    dve.wait_ge(query_kept[k], query_kept.at(k, u))
                    nc.vector.tensor_tensor(b.new[:, k], b.wide(k, D), b.e[:, k], ALU.mult).then_inc(matched[k], 1)
                yield 8
                for k in K:
                    dve.wait_ge(matched[k], matched.at(k, u))
                    nc.vector.tensor_reduce(b.small[:, k, 0].rearrange("p j h -> p (j h)"),
                                            b.new[:, k].rearrange("p j (h f) -> p (j h) f", h=AHEADS), AX.X,
                                            ALU.add).then_inc(reduced[k], 1)
                yield 9
                for k in K:
                    dve.wait_ge(reduced[k], reduced.at(k, u))
                    nc.vector.tensor_scalar(b.small[:, k, 1], b.small[:, k, 0], AD ** -0.5, 5.0, ALU.mult,
                                            ALU.min).then_inc(clipped[k], 1)
                yield 9
                for k in K:
                    dve.wait_ge(clipped[k], clipped.at(k, u))
                    if not first(u):
                        dve.wait_ge(exped[k], exped.before(k, u))
                    nc.vector.tensor_scalar(b.small[:, k, 2], b.small[:, k, 1], -5.0, None, ALU.max).then_inc(bounded[k], 1)
                yield 11
                for k in K:
                    dve.wait_ge(exped[k], exped.at(k, u))
                    for j in range(T):
                        last = nc.vector.tensor_tensor(
                            b.v[:, k, j, 0:D].rearrange("p (h f) -> p h f", h=AHEADS),
                            b.wide(k, 2 * D)[:, j, D:2 * D].rearrange("p (h f) -> p h f", h=AHEADS),
                            b.v[:, k, j, D:WIDE].unsqueeze(2).broadcast_to([P, AHEADS, AD]), ALU.mult)
                    last.then_inc(weighted[k], 1)
            w.line.beside(dve, "vector", n, steps)
    sig.end(n)


class Weights:
    pass


def ready(nc, w, iterations=0):
    w.line.i += iterations
    w.ready_count += 1
    with nc.Block() as block:
        @block.sync
        def _(sp):
            sp.sem_inc(w.ready, 1)


def edge_passes(nc, a, w, e, ps, sig, sb, out):
    NT, NTP, NC = e.tiles, e.padded, e.chunks

    def dram(name, shape, dt=F32):
        return nc.dram_tensor(f"dram_{name}", shape, dt, kind="Internal").ap()

    w.ready_count = 0
    w.ready = w.ctx.enter_context(nc.semaphore("ready"))
    w.settled = w.ctx.enter_context(nc.semaphore("settled"))
    w.sums = sb("sums", [P, NC, T, WIDE])
    w.dst_col = sb("dst_col", [P, NTP])
    w.is_rel = sb("is_rel", [P, RELS, NTP])
    w.carry_eq = sb("carry_eq", [P, 2, e.blocks, NTP])
    w.carry_pen = sb("carry_pen", [P, 2, e.score_blocks, e.score_tiles], BF16)
    w.step_pen = sb("step_pen", [P, e.score_blocks, P + 1], BF16)
    w.end_pen = sb("end_pen", [P, 2, e.score_blocks, P], BF16)
    w.own_parts = sb("own_parts", [P, NC, T, 2 * HEADS])
    w.edge_share = sb("edge_share", [P, e.score_tiles, HEADS])
    w.loop_share = sb("loop_share", [P, e.score_tiles, HEADS])
    w.dst_chunk = w.dst_col[:, 0:NT].rearrange("p (c j) -> p c j", j=T)
    w.rel_chunk = w.is_rel[:, :, 0:NT].rearrange("p r (c j) -> p r c j", j=T)
    w.edge_chunk = w.edge_share[:, 0:NT, :].rearrange("p (c j) h -> p c j h", j=T)
    w.loop_chunk = w.loop_share[:, 0:NT, :].rearrange("p (c j) h -> p c j h", j=T)
    w.tables = [dram(f"table_{i}", [2 * e.rows, D]) for i in range(3)]
    w.pos_dram = dram("positions", [e.n_nodes, 1], I32)
    w.lists_dram = dram("index_lists", [4, NC, P, T], I32)
    w.dst_dram = dram("dst_by_edge", [NTP * P])
    w.dst_rows_dram = w.dst_dram[0:e.rows].rearrange("(c e) -> c e", e=ROWS)
    w.ends_dram = dram("tile_ends", [2, NTP])
    w.masks_dram = dram("end_masks", [2, e.rows])
    w.masks_chunk_dram = w.masks_dram.rearrange("s (c e) -> c s e", e=ROWS)
    w.maxima_dram = dram("end_maxima", [2 * HEADS * e.score_tiles])
    w.ends_rows_dram = dram("end_sums", [2, NC, 1, T, WIDE])
    w.carry_dram = dram("outer_sums", [2, NT, WIDE])
    w.carry_chunk_dram = w.carry_dram.rearrange("s (c j) f -> c s j f", j=T)

    with ExitStack() as tmp:
        edge_setup(nc, a, w, e, ps, sig, sig.buffers(tmp),
                   lambda beside: dense_pass(nc, a, w, ps, sig, out, w.line.groups * LROWS, beside))
    ready(nc, w)

    t = w.tables
    paths = [(t[0], t[1]), (t[1], t[2]), (t[2], t[1])]
    for l, (old, new) in enumerate(paths):
        w.line.at = Steps(f"scores{l}")
        with ExitStack() as tmp:
            gat_scores(nc, a, w, e, Strands(nc, sig, tmp, ps), ps, sig, l, old, new)
        ready(nc, w, e.rounds)
        gat_softmax(nc, w, e, ps, sig)
        ready(nc, w)
        w.line.at = Steps("sums")
        with ExitStack() as tmp:
            gat_sums(nc, w, e, Strands(nc, sig, tmp, ps), sig)
        ready(nc, w, e.rounds)
        carry_sums(nc, w, e, ps, sig, D + HEADS)
        ready(nc, w)
        w.line.at = Steps(f"finish{l}")
        with ExitStack() as tmp:
            gat_finish(nc, w, e, Strands(nc, sig, tmp, ps), sig, l, old, new)
        ready(nc, w, e.rounds)
    for kind, old, new in (("sage", t[1], t[2]), ("rel", t[2], t[1]), ("att", t[1], None)):
        w.line.at = Steps(f"{kind}_messages")
        with ExitStack() as tmp:
            b = Strands(nc, sig, tmp, ps)
            if kind == "sage":
                sage_messages(nc, a, w, e, b, ps, sig, old, new)
            elif kind == "rel":
                rel_messages(nc, a, w, e, b, ps, sig, old, new)
            else:
                att_messages(nc, a, w, e, b, ps, sig, old)
        ready(nc, w, e.rounds)
        carry_sums(nc, w, e, ps, sig, {"sage": D + 4, "rel": D, "att": WIDE}[kind])
        ready(nc, w)
        w.line.at = Steps("alone" if kind == "att" else f"{kind}_update")
        if kind == "att":
            w.line.finish(nc)
        with ExitStack() as tmp:
            dst_update(nc, a, w, e, Strands(nc, sig, tmp, ps), ps, sig, kind, old, new, out)
        ready(nc, w, e.rounds)


def program(nc, a, out):
    ctx = ExitStack()
    with ctx:
        def sb(name, shape, dt=F32):
            return ctx.enter_context(nc.sbuf_tensor(name, shape, dt))

        sig = Signals(nc, ctx)
        w = Weights()
        w.ctx = ctx
        w.ident = sb("identity", [P, P])
        w.ones_col = sb("ones_col", [P, 1])
        w.minus1 = sb("minus1", [P, 1])
        w.power, w.eps = sb("power", [P, T]), sb("eps", [P, T])
        w.ones4 = sb("ones4", [4, ROWS], BF16)
        w.bias3 = sb("bias3", [4, BIASES, BW], BF16)
        w.bo_rows = sb("bo_rows", [P, D])
        w.gat = sb("gat_weights", [P, GAT_LAYERS, BW])
        w.own_scores = sb("own_scores", [P, GAT_LAYERS, 2 * HEADS])
        w.sage_own, w.sage_mean = sb("sage_own", [P, D]), sb("sage_mean", [P, D])
        w.rel = sb("rel_weights", [P, RELS, D])
        w.self_loop = sb("self_loop", [P, D])
        w.q, w.kv, w.o = sb("wq", [P, D]), sb("wkv", [P, 2 * D]), sb("wo", [P, D])
        w.kv_bias = w.bias3[:, B_K:B_K + 2, 0:D]
        w.split_dram = nc.dram_tensor("bias_split", [3, BIASES, BW], BF16, kind="Internal").ap()
        ps = ctx.enter_context(nc.psum_tensor("banks", [P, 8, ROWS], F32))
        with ExitStack() as tmp:
            def tb(name, shape, dt=F32):
                return tmp.enter_context(nc.sbuf_tensor(name, shape, dt))
            w.raw = tb("raw_weights", [P, 6, D])
            w.gat_t = tb("gat_transposed", [P, GAT_LAYERS, D])
            w.att = tb("attention_vectors", [P, GAT_LAYERS, 2])
            w.att_heads = tb("attention_by_head", [P, GAT_LAYERS, 2 * HEADS])
            w.head_mask = tb("head_mask", [P, HEADS])
            w.brow = tb("bias_rows", [1, BIASES, BW])
            w.split = tb("bias_parts", [1, 3, BIASES, BW], BF16)
            weights_setup(nc, a, w, ps, sig)
        e = Edges(a["x"].shape[0], a["src"].shape[0])
        beside = (PASSES - 1) * e.rounds
        w.line = DenseLine(nc, a, w, ps, sig, sig.buffers(ctx), out, beside)
        w.line.start(nc)
        edge_passes(nc, a, w, e, ps, sig, sb, out)


def kernel(**inputs):
    import concourse.bacc as _bacc
    from concourse.bass_utils import run_bass_kernel_spmd as _run

    nc = _bacc.Bacc("TRN2", target_bir_lowering=False, num_devices=1)
    arrays, aps = {}, {}
    for name, value in inputs.items():
        v = np.ascontiguousarray(value)
        arrays[f"in_{name}"] = v
        aps[name] = nc.dram_tensor(f"in_{name}", v.shape, mybir.dt.from_np(v.dtype), kind="ExternalInput").ap()
    out = nc.dram_tensor("out_0", inputs["x"].shape, F32, kind="ExternalOutput").ap()
    program(nc, aps, out)
    return _run(nc, [arrays], core_ids=[0]).results[0]["out_0"]
```
